# Optimizing a Trainium2 kernel written in Bass

```python
import numpy as np
import jax
import jax.numpy as jnp

def _softmax(x, axis=-1):
    return jax.nn.softmax(x, axis=axis)

def _gelu(x):
    return jax.nn.gelu(x, approximate=True)

def _silu(x):
    return jax.nn.silu(x)

def _sigmoid(x):
    return jax.nn.sigmoid(x)

def _layernorm(x, axis=-1, eps=1e-05):
    m = jnp.mean(x, axis=axis, keepdims=True)
    v = jnp.var(x, axis=axis, keepdims=True)
    return (x - m) / jnp.sqrt(v + eps)

def _scatter_add(tgt, idx, src, axis=0):
    return tgt.at[idx].add(src)

def _segment_sum(src, seg, n):
    return jax.ops.segment_sum(src, seg, n)
kernel_name = 'mk_seq_preln_d1_jaxref_r8_3cba2c'

def setup_inputs(seed: int=0):
    np.random.seed(seed)
    _w = jnp.asarray

    def _L0_attn_setup():
        import jax, jax.numpy as jnp
        import numpy as np
        D_MODEL, D_STATE, D_CONV, EXPAND = (128, 16, 4, 2)
        D_INNER = EXPAND * D_MODEL
        BATCH, SEQ = (4, 256)
        key = jax.random.key(seed)
        ks = jax.random.split(key, 10)
        s_in = 1.0 / np.sqrt(D_MODEL)
        s_x = 1.0 / np.sqrt(D_INNER)
        return {'x': jax.random.normal(ks[0], (BATCH, SEQ, D_MODEL), jnp.float32), 'W_in': jax.random.normal(ks[1], (2 * D_INNER, D_MODEL), jnp.float32) * s_in, 'conv_w': jax.random.normal(ks[2], (D_INNER, 1, D_CONV), jnp.float32) * 0.5, 'conv_b': jax.random.normal(ks[3], (D_INNER,), jnp.float32) * 0.1, 'W_x': jax.random.normal(ks[4], (2 * D_STATE, D_INNER), jnp.float32) * s_x, 'W_dt': jax.random.normal(ks[5], (D_STATE, D_INNER), jnp.float32) * s_x, 'b_dt': jax.random.normal(ks[6], (D_STATE,), jnp.float32) * 0.1, 'A_log': jax.random.normal(ks[7], (D_STATE,), jnp.float32), 'D': jnp.ones((D_INNER,), jnp.float32), 'W_out': jax.random.normal(ks[8], (D_MODEL, D_INNER), jnp.float32) * s_x}
    _L0_attn_in = _L0_attn_setup()

    def _L0_ffn_setup():
        import jax, jax.numpy as jnp
        import numpy as np
        D_MODEL = 128
        D_FF = 512
        NUM_M = 2
        E_ROUTER = 8 * NUM_M - 1
        D_FF_R = D_FF // NUM_M
        TOP_K = NUM_M * 2 - 1
        B, T = (2, 256)

        def _expert_stack(x, W1, b1, W2, b2):
            h = jax.nn.gelu(jnp.einsum('btd,edf->ebtf', x, W1) + b1[:, None, None, :], approximate=False)
            return jnp.einsum('ebtf,efd->ebtd', h, W2) + b2[:, None, None, :]
        key = jax.random.key(seed)
        ks = jax.random.split(key, 12)
        s = lambda fan_in: 1.0 / np.sqrt(fan_in)
        x = jax.random.normal(ks[0], (B, T, D_MODEL), dtype=jnp.float32)
        sW1 = jax.random.uniform(ks[1], (1, D_MODEL, D_FF), jnp.float32, -s(D_MODEL), s(D_MODEL))
        sb1 = jax.random.uniform(ks[2], (1, D_FF), jnp.float32, -s(D_MODEL), s(D_MODEL))
        sW2 = jax.random.uniform(ks[3], (1, D_FF, D_MODEL), jnp.float32, -s(D_FF), s(D_FF))
        sb2 = jax.random.uniform(ks[4], (1, D_MODEL), jnp.float32, -s(D_FF), s(D_FF))
        rW1 = jax.random.uniform(ks[5], (E_ROUTER, D_MODEL, D_FF_R), jnp.float32, -s(D_MODEL), s(D_MODEL))
        rb1 = jax.random.uniform(ks[6], (E_ROUTER, D_FF_R), jnp.float32, -s(D_MODEL), s(D_MODEL))
        rW2 = jax.random.uniform(ks[7], (E_ROUTER, D_FF_R, D_MODEL), jnp.float32, -s(D_FF_R), s(D_FF_R))
        rb2 = jax.random.uniform(ks[8], (E_ROUTER, D_MODEL), jnp.float32, -s(D_FF_R), s(D_FF_R))
        gW = jax.random.uniform(ks[9], (D_MODEL, E_ROUTER), jnp.float32, -s(D_MODEL), s(D_MODEL))
        gb = jax.random.uniform(ks[10], (E_ROUTER,), jnp.float32, -s(D_MODEL), s(D_MODEL))
        return {'x': x, 'sW1': sW1, 'sb1': sb1, 'sW2': sW2, 'sb2': sb2, 'rW1': rW1, 'rb1': rb1, 'rW2': rW2, 'rb2': rb2, 'gW': gW, 'gb': gb}
    _L0_ffn_in = _L0_ffn_setup()
    _d = {'L0_attn_x': _L0_attn_in['x'], 'L0_attn_W_in': _L0_attn_in['W_in'], 'L0_attn_conv_w': _L0_attn_in['conv_w'], 'L0_attn_conv_b': _L0_attn_in['conv_b'], 'L0_attn_W_x': _L0_attn_in['W_x'], 'L0_attn_W_dt': _L0_attn_in['W_dt'], 'L0_attn_b_dt': _L0_attn_in['b_dt'], 'L0_attn_A_log': _L0_attn_in['A_log'], 'L0_attn_D': _L0_attn_in['D'], 'L0_attn_W_out': _L0_attn_in['W_out'], 'L0_ffn_sW1': _L0_ffn_in['sW1'], 'L0_ffn_sb1': _L0_ffn_in['sb1'], 'L0_ffn_sW2': _L0_ffn_in['sW2'], 'L0_ffn_sb2': _L0_ffn_in['sb2'], 'L0_ffn_rW1': _L0_ffn_in['rW1'], 'L0_ffn_rb1': _L0_ffn_in['rb1'], 'L0_ffn_rW2': _L0_ffn_in['rW2'], 'L0_ffn_rb2': _L0_ffn_in['rb2'], 'L0_ffn_gW': _L0_ffn_in['gW'], 'L0_ffn_gb': _L0_ffn_in['gb']}
    _x0 = _d['L0_attn_x']
    _d['L0_attn_x'] = jax.random.normal(jax.random.fold_in(jax.random.key(seed), 1), (8, 1024, 128), dtype=_x0.dtype)
    del _x0
    return _d

def reference(L0_attn_x, L0_attn_W_in, L0_attn_conv_w, L0_attn_conv_b, L0_attn_W_x, L0_attn_W_dt, L0_attn_b_dt, L0_attn_A_log, L0_attn_D, L0_attn_W_out, L0_ffn_sW1, L0_ffn_sb1, L0_ffn_sW2, L0_ffn_sb2, L0_ffn_rW1, L0_ffn_rb1, L0_ffn_rW2, L0_ffn_rb2, L0_ffn_gW, L0_ffn_gb):

    def _L0_attn_ref(x, W_in, conv_w, conv_b, W_x, W_dt, b_dt, A_log, D, W_out):
        import jax, jax.numpy as jnp
        import numpy as np
        D_MODEL, D_STATE, D_CONV, EXPAND = (128, 16, 4, 2)
        D_INNER = EXPAND * D_MODEL
        BATCH, SEQ = (4, 256)
        B, L, _ = x.shape
        d_inner = conv_w.shape[0]
        d_conv = conv_w.shape[-1]
        n = A_log.shape[0]
        xz = x @ W_in.T
        xi, z = jnp.split(xz, 2, axis=-1)
        xc = jnp.transpose(xi, (0, 2, 1))
        xc = jax.lax.conv_general_dilated(xc, conv_w, window_strides=(1,), padding=[(d_conv - 1, 0)], feature_group_count=d_inner, dimension_numbers=('NCH', 'OIH', 'NCH'))
        xc = xc + conv_b[None, :, None]
        u = jax.nn.silu(jnp.transpose(xc, (0, 2, 1)))
        bc = u @ W_x.T
        Bm, Cm = jnp.split(bc, 2, axis=-1)
        delta = jax.nn.softplus(u @ W_dt.T + b_dt)
        A = -jnp.exp(A_log)
        dA = jnp.exp(delta * A)
        dB = delta * Bm

        def step(h, inp):
            dA_t, dB_t, u_t, c_t = inp
            h = dA_t[:, None, :] * h + u_t[:, :, None] * dB_t[:, None, :]
            y = jnp.einsum('ben,bn->be', h, c_t)
            return (h, y)
        h0 = jnp.zeros((B, d_inner, n), x.dtype)
        xs = (jnp.swapaxes(dA, 0, 1), jnp.swapaxes(dB, 0, 1), jnp.swapaxes(u, 0, 1), jnp.swapaxes(Cm, 0, 1))
        _, ys = jax.lax.scan(step, h0, xs)
        y = jnp.swapaxes(ys, 0, 1) + u * D
        y = y * jax.nn.silu(z)
        return y @ W_out.T

    def _L0_ffn_ref(x, sW1, sb1, sW2, sb2, rW1, rb1, rW2, rb2, gW, gb):
        import jax, jax.numpy as jnp
        import numpy as np
        D_MODEL = 128
        D_FF = 512
        NUM_M = 2
        E_ROUTER = 8 * NUM_M - 1
        D_FF_R = D_FF // NUM_M
        TOP_K = NUM_M * 2 - 1
        B, T = (2, 256)

        def _expert_stack(x, W1, b1, W2, b2):
            h = jax.nn.gelu(jnp.einsum('btd,edf->ebtf', x, W1) + b1[:, None, None, :], approximate=False)
            return jnp.einsum('ebtf,efd->ebtd', h, W2) + b2[:, None, None, :]
        shared_enc = _expert_stack(x, sW1, sb1, sW2, sb2).sum(0)
        weights = jax.nn.softmax(x @ gW + gb, axis=-1)
        topv, topi = jax.lax.top_k(weights, TOP_K)
        gated = (jax.nn.one_hot(topi, E_ROUTER, dtype=weights.dtype) * topv[..., None]).sum(axis=-2)
        router_out = _expert_stack(x, rW1, rb1, rW2, rb2)
        router_enc = jnp.einsum('ebtd,bte->btd', router_out, gated)
        return shared_enc + router_enc + x
    x = L0_attn_x
    x = x + _L0_attn_ref(_layernorm(x, axis=-1), L0_attn_W_in, L0_attn_conv_w, L0_attn_conv_b, L0_attn_W_x, L0_attn_W_dt, L0_attn_b_dt, L0_attn_A_log, L0_attn_D, L0_attn_W_out)
    x = x + _L0_ffn_ref(_layernorm(x, axis=-1), L0_ffn_sW1, L0_ffn_sb1, L0_ffn_sW2, L0_ffn_sb2, L0_ffn_rW1, L0_ffn_rb1, L0_ffn_rW2, L0_ffn_rb2, L0_ffn_gW, L0_ffn_gb)
    return x

_drawn_inputs = setup_inputs


def setup_inputs(seed=0):
    import zlib

    import numpy as np

    out = dict(_drawn_inputs(seed))
    spreads = {'L0_attn_D': (1.0, 0.2)}
    factors = {'L0_ffn_sb1': 7.871,
     'L0_ffn_sb2': 5.338,
     'L0_ffn_rW1': 3.242,
     'L0_ffn_rb1': 8.0,
     'L0_ffn_rW2': 3.055,
     'L0_ffn_rb2': 8.0,
     'L0_ffn_gW': 3.329,
     'L0_ffn_gb': 8.0}
    for name, (base, spread) in spreads.items():
        noise = np.random.default_rng([zlib.crc32(name.encode()), seed]).standard_normal(out[name].shape)
        drawn = base * np.exp(spread * noise) if base else spread * noise
        out[name] = jnp.asarray(drawn.astype(out[name].dtype))
    for name, factor in factors.items():
        out[name] = (out[name] * factor).astype(out[name].dtype)
    return out
```

```python
from contextlib import ExitStack
import concourse.bass as bass
from concourse import mybir

FP32 = mybir.dt.float32
BF16 = mybir.dt.bfloat16
U32 = mybir.dt.uint32
I32 = mybir.dt.int32
ALU = mybir.AluOpType
ACT = mybir.ActivationFunctionType
AX = mybir.AxisListType

P = 128
NB = 8
L = 1024
C = L // P
N = 16
E = 256
EH = E // P
LV = 7
CG = 4
G = C // CG
HALF = P // 2
EPS = 1e-5
K_PARTS = [0, 0, 1, 1, 0, 2]
Q_PARTS = [0, 1, 0, 1, 2, 0]
NCMB = len(K_PARTS)
KR = NCMB * N


NX = 15
NE = 16
TOPK = 3
F = 256
FH = F // P
FS = 512
TOK = NB * L
REG = TOK + P
XW_ = P + 1
UN = 4
NT = -(-(TOK * TOPK // P + NX) // UN) * UN
SPARE = NT - TOK * TOPK // P
SKIP = 30000.0
QB = 512
NQ = TOK // QB


class Tile:

    def __init__(self, i, c, un):
        self.i, self.c, self.un = i, c, un

    def at(self, per, k):
        return self.i * (self.un * per) + (self.c * per + k)

    def uses(self, bufs, per):
        return self.i * (self.un // bufs * per) + (self.c // bufs + 1) * per

    def next(self, d=1):
        return Tile(self.i, self.c + d, self.un)

    def prior(self, bufs, per):
        return self.i * (self.un // bufs * per) + self.c // bufs * per

    def back(self):
        return self.i * (self.un // 2 * 16) + (self.c - 4 + 2) // 2 * 16

    def index(self):
        return self.i * self.un + self.c

    def pair(self):
        return self.i + self.c // 2, self.c % 2


def j_at(j):
    at = j.index()
    return slice(at, at + 1) if isinstance(at, int) else bass.ds(at, 1)


def every(eng, prologue, step, count, un):
    prologue()
    for c in range(un):
        step(Tile(0, c, un), 0)
    with eng.Fori(0, (count - 2 * un) // un) as i:
        for c in range(un, 2 * un):
            step(Tile(i, c, un), 0)
    for c in range(count - un, count):
        step(Tile(0, c, un), count - c)


class Batch:

    def __init__(self, i, c):
        self.i, self.c = i, c

    def at(self, per, k):
        return self.i * (2 * per) + (self.c * per + k)

    def uses(self, per):
        return self.i * per + (self.c // 2 + 1) * per

    @property
    def par(self):
        return self.c % 2

    def next(self, d=1):
        return Batch(self.i, self.c + d)

    def index(self):
        return self.i * 2 + self.c


def wait(eng, sem, value):
    if isinstance(value, int) and value <= 0:
        return
    eng.wait_ge(sem, value)


def wait_all(eng, *waits):
    ready = [(s, v if isinstance(v, int) else eng.snap(v)) for s, v in waits]
    for s, v in ready:
        wait(eng, s, v)


def build(nc, d, out):
    ctx, first, second = ExitStack(), ExitStack(), ExitStack()
    with ctx:
        stack = [ctx]

        def sb(name, shape, dt=FP32):
            return stack[0].enter_context(nc.sbuf_tensor(name, shape, dt))

        def pb(name, shape, dt=FP32):
            return ctx.enter_context(nc.psum_tensor(name, shape, dt))

        def sem(name):
            return ctx.enter_context(nc.semaphore(name))

        ident = sb("ident", [P, P]); GK = sb("GK", [P, NB, TOPK, C])
        TROW = sb("TROW", [1, NT], I32); TEXP = sb("TEXP", [1, NT], I32); TTAIL = sb("TTAIL", [1, NE], I32)
        gt = sb("gt", [1, 16]); zt = sb("zt", [P, XW_]); gtp = sb("gtp", [1, 10]); mh1 = sb("mh1", [1, 1])
        stack[0] = first
        onesm = sb("onesm", [P, P]); tlv = sb("tlv", [P, (LV + 1) * P]); tend = sb("tend", [P, P])
        msk = sb("msk", [P, 4, CG, HALF]); rowmask = sb("rowmask", [P, C])
        w_in = sb("w_in", [P, 2 * E]); conv_w = sb("conv_w", [P, EH, 4]); conv_b = sb("conv_b", [P, EH])
        w_bcd = sb("w_bcd", [P, EH, 3 * N]); bdt = sb("bdt", [P, N]); alog = sb("alog", [P, N]); aneg = sb("aneg", [P, N])
        dcol = sb("dcol", [P, EH]); w_out = sb("w_out", [P, EH, P]); mhalf = sb("mhalf", [P, C])
        aneg2 = sb("aneg2", [P, N])
        gw = sb("gw", [P, NE]); gb = sb("gb", [P, NE]); sb2 = sb("sb2", [P, P]); iota = sb("iota", [P, NE])
        idc = sb("idc", [P, TOPK, C]); ereg = sb("ereg", [P, NE]); tri = sb("tri", [P, P]); tilei = sb("tilei", [1, NT])
        XL = [sb(f"XL{k}", [P, C, P]) for k in range(2)]
        XR = [sb(f"XR{k}", [P, C, P]) for k in range(2)]
        XN = sb("XN", [P, C, P]); ST = sb("ST", [P, C, 6]); MV = sb("MV", [P, C, 2]); VE = sb("VE", [P, C]); RS = sb("RS", [P, C])
        XT = sb("XT", [P, L]); CA = sb("CA", [P, EH, L])
        U = [sb(f"U{k}", [P, EH, L]) for k in range(2)]
        ZS = [sb(f"ZS{k}", [P, EH, L]) for k in range(2)]
        UT = [sb(f"UT{k}", [P, C, E]) for k in range(2)]
        D0 = sb("D0", [P, C, N]); AB = sb("AB", [P, C, N]); LN1 = sb("LN1", [P, C, N]); DEL = sb("DEL", [P, C, N])
        GG = sb("GG", [P, C, N]); DB = sb("DB", [P, C, N]); CT = sb("CT", [P, C, N]); TM = sb("TM", [P, C, N]); M0 = sb("M0", [P, C])
        KE = sb("KE", [P, 2, C, N]); W = sb("W", [P, C * C * N]); EX = sb("EX", [P, LV + 1, P])
        X = sb("X", [P, LV, P]); R = sb("R", [P, LV, P]); PT = sb("PT", [P, 3, LV * P], BF16); PTQ = sb("PTQ", [P, 3, LV * HALF], BF16)
        QF = sb("QF", [P, P]); QM = [sb(f"QM{k}", [P, C, P]) for k in range(2)]
        XK = sb("XK", [KR, C, LV * P], BF16); XQ = sb("XQ", [KR, C, LV * HALF], BF16)
        DG = [sb(f"DG{k}", [P, CG, P]) for k in range(G)]
        MT = [sb(f"MT{k}", [P, CG, P]) for k in range(G)]
        HB = sb("HB", [P, E]); X1 = sb("X1", [P, C, P])
        XW = sb("XW", [P, TOPK, C, XW_]); ACC = sb("ACC", [P, C, P]); X2T = sb("X2T", [P, L]); IDR = sb("IDR", [P, TOPK, C])
        LG = sb("LG", [P, C, NE]); MX = sb("MX", [P, C, 8]); IX = sb("IX", [P, C, 8], U32); IXF = sb("IXF", [P, TOPK, C])
        DT = sb("DT", [P, C, NE + TOPK]); SE = sb("SE", [P, C]); RC = sb("RC", [P, C])
        OH = sb("OH", [P, TOPK, C, NE]); MKS = sb("MKS", [P, C, NE]); BT = sb("BT", [P, C + 1, NE]); PM_ = sb("PM_", [P, C, NE])
        PF = sb("PF", [P, TOPK, C]); PU = sb("PU", [P, TOPK, C], U32)
        CN = sb("CN", [1, 6, NE]); CI = sb("CI", [1, NE], I32); TF = sb("TF", [1, 4, NT])
        stack[0] = second
        first.close()
        W1B = sb("W1B", [P, NX, F + FH]); W2 = sb("W2", [P, NX, FH, P]); B2 = sb("B2", [P, NX, P])
        SW1 = sb("SW1", [P, FS]); SB1 = sb("SB1", [P, FS // P]); SW2 = sb("SW2", [P, FS // P, P])
        XS = [sb(f"XS{k}", [P, XW_]) for k in range(4)]; ID = [sb(f"ID{k}", [P, 1], U32) for k in range(4)]
        WS = [sb(f"WS{k}", [P, F + FH]) for k in range(2)]; XTT = [sb(f"XTT{k}", [P, P]) for k in range(2)]
        HT = [sb(f"HT{k}", [P, FH, P]) for k in range(2)]; YT = [sb(f"YT{k}", [P, P]) for k in range(2)]
        XQB = [sb(f"XQB{k}", [P, QB]) for k in range(2)]; AQ = [sb(f"AQ{k}", [P, QB // P, P]) for k in range(2)]
        YQ = [sb(f"YQ{k}", [P, TOPK, QB // P, P]) for k in range(2)]; HS = [sb(f"HS{k}", [P, FS // P, QB]) for k in range(2)]
        OQ = [sb(f"OQ{k}", [P, QB // P, P]) for k in range(2)]
        second.close()
        stack[0] = ctx
        WD = [pb(f"WD{k}", [P, 1024]) for k in range(2)]
        SM = pb("SM", [P, 512]); PA = pb("PA", [P, CG, P]); PM = [pb(f"PM{k}", [P, 2, CG, HALF]) for k in range(2)]
        dk = nc.dram_tensor("dk", [3, C, N, LV * P], BF16)
        dq = nc.dram_tensor("dq", [3, C, N, LV * HALF], BF16)

        dx2t = nc.dram_tensor("dx2t", [P, NB, L], FP32)
        dacc = nc.dram_tensor("dacc", [NB, C, P, P], FP32)
        dslot = nc.dram_tensor("dslot", [NX * REG + SPARE * P, XW_], FP32)
        dy = nc.dram_tensor("dy", [TOPK * TOK, P], FP32)

        d_st, d_sc, d_z, d_tail = sem("d_stored"), sem("d_dispatched"), sem("d_spare"), sem("d_tails")
        p_x2t, p_lg, p_rk = sem("pe_x2t"), sem("pe_logits"), sem("pe_ranks")
        a_xc, a_x2t, a_ex, a_end = sem("act_xcopies"), sem("act_x2t"), sem("act_gates"), sem("act_end")
        v_ve2, v_xw, v_ids, v_lg, v_mk, v_pos, v_tab, v_zt = [sem("dve_" + x) for x in "var2 xw ids logits masks slots tables zt".split()]
        d_ac = sem("d_acc")
        v_cq, g_s = sem("dve_combine_chain"), sem("pool_step_over")
        v_first, p_first, g_first, a_first = sem("dve_first_part"), sem("pe_first_part"), sem("pool_first_part"), sem("act_first_part")
        d_e = sem("d_expert_weights"); d_xs = [sem(f"d_rows{k}") for k in range(4)]; d_ys = [sem(f"d_result{k}") for k in range(2)]
        p_t, p_1, p_2 = sem("pe_rows"), sem("pe_hidden"), sem("pe_result")
        v_id, v_xt, v_ws, v_y = sem("dve_tile_ids"), sem("dve_tile_rows"), sem("dve_tile_weights"), sem("dve_tile_result")
        a_g = sem("act_gelu")
        d_q = [sem(f"d_block{k}") for k in range(2)]; d_o2 = [sem(f"d_out{k}") for k in range(2)]
        p_s1, p_s2, a_s, v_q = sem("pe_shared_hidden"), sem("pe_shared"), sem("act_shared"), sem("dve_combined")
        g_c2 = sem("pool_acc_first")
        g_rs2, g_acc = sem("pool_rstd2"), sem("pool_acc")
        d_c, d_w, d_r, d_o = sem("d_const"), sem("d_parts_written"), sem("d_parts_read"), sem("d_out")
        d_x = [sem(f"d_x{k}") for k in range(2)]; d_xr = [sem(f"d_xr{k}") for k in range(2)]
        (p_xnt, p_xi, p_z, p_bcd, p_ut, p_dec, p_lv, p_hb, p_a, p_m, p_y, p_out) = [
            sem("pe_" + s) for s in "xnt xi z bcd ut dec lv hb a m y out".split()]
        (a_k, a_xt, a_c0, a_z, a_u, a_hb, a_ut, a_sp, a_ln, a_ke, a_e, a_h, a_m) = [
            sem("act_" + s) for s in "const xt c0 z u hb ut sp ln ke e hi mid".split()]
        (v_k, v_ln, v_ve, v_conv, v_ab, v_g, v_m0, v_w, v_x, v_r, v_l, v_m, v_gate, v_x1, v_c) = [
            sem("dve_" + s) for s in "const ln var conv ab g m0 w x rest lo merge gate x1 chain".split()]
        g_rs, g_dg, g_qm, g_gate, g_c = [sem("pool_" + s) for s in "rstd diag qm gate chain".split()]
        n_const = 0
        xv = d["x"].rearrange("b (t p) e -> b p t e", p=P)
        ov = out.rearrange("b (t p) e -> b p t e", p=P)

        block = ctx.enter_context(nc.Block())

        def steps(eng, prologue, step):
            prologue(Batch(0, 0))
            for b in (0, 1):
                step(Batch(0, b))
            with eng.Fori(0, (NB - 4) // 2) as i:
                step(Batch(i, 2))
                step(Batch(i, 3))
            for b in (NB - 2, NB - 1, NB):
                step(Batch(0, b))

        def has(b):
            if not isinstance(b.i, int):
                return True, True, True
            return b.c < NB - 1, b.c < NB, b.c > 0

        SLOT = {"xnt": 0, "xi0": 1, "xi1": 0, "z0": 1, "z1": 0, "x2t": 1, "ua": 0, "ub": 1, "y0": 0, "lg": 1, "lv": 0, "rk": 1,
                "y1": 0, "out": 1}
        consts = [(ident, "ident"), (onesm, "onesm"), (tlv, "tlv"), (tend, "tend"), (msk, "msk"), (rowmask, "rowmask"),
                  (w_in, "w_in"), (conv_w, "conv_w"), (conv_b, "conv_b"), (w_bcd, "w_bcd"), (bdt, "bdt"), (alog, "alog"),
                  (dcol, "dcol"), (w_out, "w_out"), (gw, "gw"), (gb, "gb"), (sb2, "sb2"), (iota, "iota"), (idc, "idc"),
                  (ereg, "ereg"), (tri, "tri"), (tilei, "tilei")]
        NCONST = 16 * len(consts)

        @block.sync
        def _(sp):
            sp.dma_start(XL[0][:], xv[0]).then_inc(d_x[0], 16)
            for tile, name in consts:
                sp.dma_start(tile[:], d[name]).then_inc(d_c, 16)
            sp.dma_start(XL[1][:], xv[1]).then_inc(d_x[1], 16)

            def parts(n):
                fresh, merged, landed = n.at(1, 1), n.at(4, 0), n.at(32, 32)
                if not isinstance(n.i, int):
                    fresh, merged, landed = sp.snap(fresh), sp.snap(merged), sp.snap(landed)
                wait(sp, p_m, merged)
                sp.wait_ge(v_l, fresh)
                sp.dma_start(dk.ap().rearrange("q c n f -> (c n) q f"), PT[:]).then_inc(d_w, 16)
                sp.dma_start(dq.ap().rearrange("q c n f -> (c n) q f"), PTQ[:]).then_inc(d_w, 16)
                sp.wait_ge(d_w, landed)
                for k in range(NCMB):
                    sp.dma_start(XK[k * N:(k + 1) * N], dk[K_PARTS[k]].rearrange("c n f -> n c f")).then_inc(d_r, 16)
                    sp.dma_start(XQ[k * N:(k + 1) * N], dq[Q_PARTS[k]].rearrange("c n f -> n c f")).then_inc(d_r, 16)

            def number(b):
                return b.index() if isinstance(b.i, int) else sp.snap(b.index())

            def load(b):
                at = number(b.next(2))
                sp.wait_ge(v_ln, b.at(1, 1))
                sp.dma_start(XL[b.par][:], xv[at]).then_inc(d_x[b.par], 16)

            def residual(b):
                at = number(b)
                wait(sp, v_x1, b.at(1, -1))
                sp.dma_start(XR[b.par][:], xv[at]).then_inc(d_xr[b.par], 16)

            def store(m):
                at = number(m)
                sp.wait_ge(a_x2t, m.at(1, 1))
                sp.dma_start(dx2t[:, at, :], X2T[:]).then_inc(d_st, 16)

            def store_acc(b):
                at = number(b)
                sp.wait_ge(g_acc, b.at(1, 1))
                sp.dma_start(dacc[at].rearrange("c p e -> p c e"), ACC[:]).then_inc(d_ac, 16)

            def step(b):
                front, back, route = has(b)
                if front and route and not (isinstance(b.i, int) and b.c > NB - 3):
                    load(b)
                if back:
                    residual(b)
                if route:
                    store(b.next(-1))
                if front:
                    parts(b.next())
                if back:
                    store_acc(b)

            def prologue(b):
                sp.wait_ge(v_zt, 1)
                for k in range(SPARE):
                    sp.dma_start(dslot[NX * REG + k * P:NX * REG + (k + 1) * P], zt[:]).then_inc(d_z, 16)
                parts(b)
                load(b)

            steps(sp, prologue, step)

            sp.wait_ge(v_tab, 1)
            for e in range(NX):
                at = sp.value_load(TTAIL[0:1, e:e + 1], min_val=0, max_val=NX * REG - P)
                sp.dma_start(dslot[bass.ds(at, P)], zt[:]).then_inc(d_tail, 16)
            sp.wait_ge(v_first, 1)
            sp.wait_ge(p_first, 1)
            sp.wait_ge(a_first, 1)
            sp.wait_ge(d_sc, 16 * TOPK * C * NB)
            sp.wait_ge(d_ac, 16 * NB)
            sp.wait_ge(d_st, 16 * NB)
            for tile, name in ((W1B, "w1b"), (W2, "w2"), (B2, "b2"), (SW1, "sw1"), (SB1, "sb1"), (SW2, "sw2")):
                sp.dma_start(tile[:], d[name]).then_inc(d_e, 16)
            sp.wait_ge(d_tail, 16 * NX)
            sp.wait_ge(d_z, 16 * SPARE)

            def rows(j):
                at = sp.value_load(TROW[0:1, j_at(j)], min_val=0, max_val=NX * REG + SPARE * P - P)
                wait_all(sp, (p_t, j.at(1, -3)), (v_id, j.at(1, -3)))
                sp.dma_start(XS[j.c % 4][:], dslot[bass.ds(at, P)]).then_inc(d_xs[j.c % 4], 16)

            every(sp, lambda: None, lambda j, left: rows(j), NT, UN)

            def block_in(q):
                b, c = q.pair()
                wait_all(sp, (p_s1, q.at(4, -4)), (v_q, q.at(1, -1)))
                k = q.c % 2
                ts = slice(c * 4, c * 4 + 4)
                sp.dma_start(XQB[k][:], dx2t[:, b, c * QB:(c + 1) * QB]).then_inc(d_q[k], 16)
                sp.dma_start(AQ[k][:], dacc[b, ts].rearrange("c p e -> p c e")).then_inc(d_q[k], 16)
                for r in range(TOPK):
                    src = dy.ap().rearrange("(k b c p) e -> k b p c e", k=TOPK, b=NB, p=P)[r, b, :, ts]
                    sp.dma_start(YQ[k][:, r], src).then_inc(d_q[k], 16)

            def block_out(q):
                b, c = q.pair()
                sp.wait_ge(v_q, q.at(1, 1))
                sp.dma_start(ov[b, :, c * 4:c * 4 + 4], OQ[q.c % 2][:]).then_inc(d_o2[q.c % 2], 16)

            sp.wait_ge(d_ys[0], 16 * (NT // 2))
            sp.wait_ge(d_ys[1], 16 * (NT // 2))

            def block(q, left):
                if left != 1:
                    block_in(q.next())
                block_out(q)
            block_in(Tile(0, 0, 2))
            for c in range(NQ):
                block(Tile(0, c, 2), NQ - c)
            for k in range(2):
                sp.wait_ge(d_o2[k], 16 * (NQ // 2))
        @block.gpsimd
        def _(g):
            g.memset(mhalf[:], -0.5).then_inc(g_c, 1)
            g.memset(mh1[:], 0.0).then_inc(g_c, 1)
            g.wait_ge(g_c, 2)

            def rstd(n):
                g.wait_ge(v_ve, n.at(1, 1))
                g.tensor_tensor(RS[:], VE[:], mhalf[:], ALU.pow).then_inc(g_rs, 1)

            def diag(n):
                g.wait_ge(v_m0, n.at(1, 1))
                wait(g, v_m, n.at(2, 0))
                for k in range(G):
                    g.tensor_tensor(DG[k][:], ident[:].unsqueeze(1).broadcast_to([P, CG, P]),
                                    M0[:, k * CG:(k + 1) * CG].unsqueeze(2).broadcast_to([P, CG, P]), ALU.mult).then_inc(g_dg, 1)

            def qmask(n):
                g.wait_ge(v_x, n.at(1, 1))
                wait(g, p_y, n.at(2, -2))
                g.tensor_tensor(QM[n.par][:], QF[:].unsqueeze(1).broadcast_to([P, C, P]),
                                rowmask[:].unsqueeze(2).broadcast_to([P, C, P]), ALU.mult).then_inc(g_qm, 1)

            def gate(b, k):
                g.wait_ge(v_gate, b.at(2, k + 1))
                sl = slice(k * 512, k * 512 + 512)
                GT = U[b.par]
                g.tensor_tensor(GT[:, :, sl], GT[:, :, sl], ZS[b.par][:, :, sl], ALU.mult).then_inc(g_gate, 1)

            def rstd2(b):
                g.wait_ge(v_ve2, b.at(1, 1))
                g.tensor_tensor(RS[:], VE[:], mhalf[:], ALU.pow).then_inc(g_rs2, 1)

            def acc(b):
                g.wait_ge(v_xw, b.at(1, 1))
                wait(g, d_ac, b.at(16, 0))
                g.tensor_tensor(ACC[:], X1[:], XW[:, 0, :, 0:P], ALU.add).then_inc(g_c2, 1)
                g.wait_ge(g_c2, b.at(1, 1))
                g.tensor_tensor(ACC[:], ACC[:], sb2[:].unsqueeze(1).broadcast_to([P, C, P]), ALU.add).then_inc(g_acc, 1)

            def dispatch(m):
                g.wait_ge(v_pos, m.at(1, 1))
                g.wait_ge(a_xc, m.at(2, 2))
                g.wait_ge(v_ids, m.at(1, 1))
                g.tensor_tensor(gtp[:, m.par:m.par + 1], mh1[:], mh1[:], ALU.add)
                for k in range(TOPK):
                    for t in range(C):
                        g.indirect_dma_start(dslot.ap(), bass.IndirectOffsetOnAxis(ap=PU[:, k, t:t + 1], axis=0), XW[:, k, t, :], None).then_inc(d_sc, 16)

            def prologue(b):
                rstd(b)
                rstd(b.next()); diag(b); qmask(b)

            def step(b):
                front, back, route = has(b)
                if front:
                    diag(b.next())
                if back:
                    gate(b, 0)
                if front:
                    qmask(b.next())
                if route:
                    dispatch(b.next(-1))
                if back:
                    gate(b, 1)
                    rstd2(b)
                if front and not (isinstance(b.i, int) and b.c >= NB - 2):
                    rstd(b.next(2))
                if back:
                    acc(b)

            g.wait_ge(d_c, NCONST)
            steps(g, prologue, step)

            def result(j, left):
                g.wait_ge(v_y, j.at(1, 1))
                wait(g, g_s, j.at(1, 0))
                g.tensor_tensor(gtp[:, 2:3], mh1[:], mh1[:], ALU.add).then_inc(g_s, 1)
                g.indirect_dma_start(dy.ap(), bass.IndirectOffsetOnAxis(ap=ID[j.c % 4][:, 0:1], axis=0), YT[j.c % 2][:], None,
                                     bounds_check=TOPK * TOK - 1, oob_is_err=False).then_inc(d_ys[j.c % 2], 16)

            every(g, lambda: None, result, NT, UN)
            g.wait_ge(d_ys[0], 16 * (NT // 2))
            g.wait_ge(d_ys[1], 16 * (NT // 2))

        @block.scalar
        def _(a):
            a.wait_ge(d_c, NCONST)
            a.activation(aneg[:], alog[:], ACT.Exp).then_inc(a_k, 1)

            def wide(sl):
                return WD[sl]

            def front(n, s0):
                a.wait_ge(p_xnt, n.at(1, 1))
                wait(a, p_z, n.at(2, 0))
                a.activation(XT[:], WD[s0][:], ACT.Copy).then_inc(a_xt, 1)
                for h in range(EH):
                    a.wait_ge(p_xi, n.at(2, h + 1))
                    wait(a, a_u, n.at(2, 0))
                    a.activation(CA[:, h], WD[(s0 + 1 + h) % 2][:], ACT.Identity, scale=conv_w[:, h, 3:4], bias=conv_b[:, h:h + 1]).then_inc(a_c0, 1)

            def hb(b):
                a.wait_ge(p_hb, b.at(1, 1))
                wait(a, p_y, b.at(2, 0))
                a.activation(HB[:], SM[:, 0:E], ACT.Copy).then_inc(a_hb, 1)

            def silus(n, s0):
                for h in range(EH):
                    a.wait_ge(p_z, n.at(2, h + 1))
                    wait(a, g_gate, n.at(2, -2))
                    a.activation(ZS[n.par][:, h], WD[(s0 + 3 + h) % 2][:], ACT.Silu).then_inc(a_z, 1)
                for h in range(EH):
                    a.wait_ge(v_conv, n.at(2, h + 1))
                    wait(a, p_out, n.at(1, -1))
                    a.activation(U[n.par][:, h], CA[:, h], ACT.Silu).then_inc(a_u, 1)

            def ut(n, s5):
                for h in range(2):
                    a.wait_ge(p_ut, n.at(2, h + 1))
                    wait(a, p_y, n.at(2, -2))
                    a.activation(UT[n.par][:, 4 * h:4 * h + 4, :], WD[(s5 + h) % 2][:].rearrange("p (t e) -> p t e", e=E), ACT.Copy).then_inc(a_ut, 1)

            def soft(n):
                a.wait_ge(v_ab, n.at(1, 1))
                a.activation(AB[:], AB[:], ACT.Exp, scale=-1.0).then_inc(a_sp, 1)
                a.wait_ge(a_sp, n.at(1, 1))
                wait(a, v_g, n.at(1, 0))
                a.activation(LN1[:], AB[:], ACT.Ln, bias=1.0).then_inc(a_ln, 1)

            def expo(n, s8):
                a.wait_ge(p_dec, n.at(1, 1))
                wait(a, v_w, n.at(1, 0))
                a.activation(KE[:], SM[:, 0:2 * C * N].rearrange("p (a c n) -> p a c n", a=2, n=N), ACT.Exp).then_inc(a_ke, 1)
                a.wait_ge(p_lv, n.at(1, 1))
                wait(a, v_x, n.at(1, 0))
                a.activation(EX[:], WD[s8][:].rearrange("p (l t) -> p l t", t=P), ACT.Exp).then_inc(a_e, 1)

            def split(n):
                a.wait_ge(v_x, n.at(1, 1))
                wait(a, d_w, n.at(32, 0))
                a.activation(PT[:, 0], X[:].rearrange("p l t -> p (l t)"), ACT.Copy).then_inc(a_h, 1)
                a.wait_ge(v_r, n.at(1, 1))
                a.activation(PT[:, 1], R[:].rearrange("p l t -> p (l t)"), ACT.Copy).then_inc(a_m, 1)

            def copies(b):
                g_ = None
                a.wait_ge(v_xw, b.at(1, 1))
                for k in (1, 2):
                    a.activation(XW[:, k, :, 0:P], XW[:, 0, :, 0:P], ACT.Copy).then_inc(a_xc, 1)

            def x2t(m):
                a.wait_ge(p_x2t, m.at(1, 1))
                wait(a, p_lg, m.at(1, 0))
                wait(a, d_st, m.at(16, 0))
                a.activation(X2T[:], WD[SLOT["x2t"]][:], ACT.Copy).then_inc(a_x2t, 1)

            def gates(m):
                a.wait_ge(v_lg, m.at(1, 1))
                a.activation(DT[:], DT[:], ACT.Exp).then_inc(a_ex, 1)

            def prologue(b):
                front(b, 0); silus(b, 0); ut(b, SLOT["ua"]); soft(b); expo(b, SLOT["lv"]); split(b)

            def step(b):
                front_, back, route = has(b)
                n, m = b.next(), b.next(-1)
                if front_:
                    front(n, 0)
                if back:
                    hb(b)
                if front_:
                    silus(n, 0)
                if route:
                    x2t(m)
                if front_:
                    ut(n, SLOT["ua"]); soft(n)
                if route:
                    gates(m)
                if front_:
                    expo(n, SLOT["lv"]); split(n)
                if back:
                    copies(b)

            steps(a, prologue, step)
            a.wait_ge(a_xc, 2 * NB)
            a.wait_ge(a_ex, NB)
            a.sem_inc(a_first, 1)

            def hidden(j, left):
                a.wait_ge(p_1, j.at(1, 1))
                wait(a, p_2, j.at(1, -1))
                for h in range(FH):
                    x = a.activation(HT[j.c % 2][:, h], WD[1][:, (j.c % 2) * 512 + h * P:(j.c % 2) * 512 + (h + 1) * P], ACT.Gelu,
                                     bias=WS[j.c % 2][:, F + h:F + h + 1])
                x.then_inc(a_g, 1)

            every(a, lambda: None, hidden, NT, UN)

            def shared(q, left):
                for f in range(FS // P):
                    a.wait_ge(p_s1, q.at(4, f + 1))
                    if f == 0:
                        wait(a, p_s2, q.at(1, -1))
                    a.activation(HS[q.c % 2][:, f], WD[f // 2][:, (f % 2) * QB:(f % 2 + 1) * QB], ACT.Gelu, bias=SB1[:, f:f + 1]).then_inc(a_s, 1)

            every(a, lambda: None, shared, NQ, 2)

        @block.vector
        def _(v):
            chain = {"done": 0, "loop": None, "base": 0, "k": 0}
            gates_ = [0]

            def link(ins, b=None):
                ins.then_inc(v_c, 1)
                chain["k"] += 1
                v.wait_ge(v_c, chain["done"] + chain["k"] if chain["loop"] is None else chain["loop"].at(NCH, chain["base"] + chain["k"]))

            def step_over():
                v.memset(gt[:, gates_[0] % 16:gates_[0] % 16 + 1], 0.0)
                gates_[0] += 1

            def ln(n):
                v.wait_ge(d_x[n.par], n.uses(16))
                for t in range(C):
                    x = v.bn_stats(ST[:, t], XL[n.par][:, t])
                link(x)
                step_over()
                for t in range(C):
                    x = v.bn_aggr(MV[:, t], ST[:, t])
                link(x)
                wait(v, g_rs, n.at(1, 0))
                v.tensor_scalar(VE[:], MV[:, :, 1], EPS, None, ALU.add).then_inc(v_ve, 1)
                v.wait_ge(g_rs, n.at(1, 1))
                wait(v, p_xnt, n.at(1, 0))
                for t in range(C):
                    x = v.tensor_scalar(XN[:, t], XL[n.par][:, t], MV[:, t, 0:1], RS[:, t:t + 1], ALU.subtract, ALU.mult)
                x.then_inc(v_ln, 1)

            def conv(n, s0):
                for h in range(EH):
                    ps = WD[(s0 + 1 + h) % 2]
                    v.wait_ge(a_c0, n.at(2, h + 1))
                    for k in (2, 1, 0):
                        j = 3 - k
                        x = v.scalar_tensor_tensor(CA[:, h, j:], ps[:, 0:L - j], conv_w[:, h, k:k + 1], CA[:, h, j:], ALU.mult, ALU.add)
                        if k:
                            link(x)
                    x.then_inc(v_conv, 1)

            def merge(b, k):
                v.wait_ge(p_a, b.at(2, k + 1))
                v.wait_ge(g_dg, b.at(2, k + 1))
                wait(v, p_y, b.at(2, k - 1))
                link(v.tensor_tensor(MT[k][:], PA[:], DG[k][:], ALU.add))
                for l in (3, 2, 1, 0):
                    q = (3 - l) // 2
                    if l % 2:
                        v.wait_ge(p_m, b.at(4, 2 * k + q + 1))
                    step_over()
                    w = 1 << l
                    o = MT[k][:].rearrange("p c (k a j) -> p (c k) a j", a=2, j=w)[:, :, 1, :]
                    mk = msk[:, 3 - l].bitcast(mybir.dt.int32).rearrange("p c (k j) -> p (c k) j", j=w)
                    dt = PM[q][:, (3 - l) % 2].rearrange("p c (k j) -> p (c k) j", j=w)
                    x = v.copy_predicated(o, mk, dt)
                    if l:
                        link(x)
                x.then_inc(v_m, 1)

            def tok_a(n):
                sm = SM[:, 0:C * 3 * N].rearrange("p (c k n) -> p c k n", k=3, n=N)
                v.wait_ge(p_bcd, n.at(1, 1))
                link(v.tensor_tensor(D0[:], sm[:, :, 0], bdt[:].unsqueeze(1).broadcast_to([P, C, N]), ALU.add))
                wait(v, a_ln, n.at(1, 0))
                v.scalar_tensor_tensor(AB[:], D0[:], -1.0, D0[:], ALU.mult, ALU.max).then_inc(v_ab, 1)

            def tok_b(n):
                sm = SM[:, 0:C * 3 * N].rearrange("p (c k n) -> p c k n", k=3, n=N)
                v.wait_ge(a_ln, n.at(1, 1))
                link(v.scalar_tensor_tensor(DEL[:], D0[:], 0.0, LN1[:], ALU.max, ALU.add))
                wait(v, p_lv, n.at(1, 0))
                v.tensor_tensor(GG[:], DEL[:], aneg2[:].unsqueeze(1).broadcast_to([P, C, N]), ALU.mult)
                v.tensor_tensor(DB[:], DEL[:], sm[:, :, 1], ALU.mult)
                v.tensor_copy(CT[:], sm[:, :, 2]).then_inc(v_g, 1)
                v.wait_ge(v_g, n.at(1, 1))
                link(v.tensor_tensor(TM[:], DB[:], CT[:], ALU.mult))
                wait(v, g_dg, n.at(2, 0))
                v.tensor_reduce(M0[:], TM[:], AX.X, ALU.add).then_inc(v_m0, 1)

            def gate(b, k, s):
                v.wait_ge(p_y, b.at(2, k + 1))
                sl = slice(k * 512, k * 512 + 512)
                GT = U[b.par]
                for h in range(EH):
                    x = v.scalar_tensor_tensor(GT[:, h, sl], U[b.par][:, h, sl], dcol[:, h:h + 1], WD[s][:, h * 512:(h + 1) * 512], ALU.mult, ALU.add)
                x.then_inc(v_gate, 1)

            def facs(n):
                v.wait_ge(a_ke, n.at(1, 1))
                wait(v, p_hb, n.at(1, 0))
                wd = W[:, N:N + (C - 1) * (C + 1) * N].rearrange("p (c k) -> p c k", k=(C + 1) * N)[:, :, 0:N]
                link(v.tensor_tensor(wd, KE[:, 0, 0:C - 1], DB[:, 0:C - 1], ALU.mult))
                w4 = W[:].rearrange("p (a c n) -> p a c n", a=C, n=N)
                for c in range(1, C - 1):
                    x = v.tensor_tensor(w4[:, 0:c, c + 1], w4[:, 0:c, c], KE[:, 1, c].unsqueeze(1).broadcast_to([P, c, N]), ALU.mult)
                    if c < C - 2:
                        link(x)
                x.then_inc(v_w, 1)
                v.wait_ge(a_e, n.at(1, 1))
                wait(v, a_h, n.at(1, 0))
                dbt, ct = SM[:, 2 * P:3 * P], SM[:, 3 * P:4 * P]
                for l in range(LV):
                    f = lambda t: t.rearrange("p (k a j) -> p k a j", a=2, j=1 << l)
                    ex, xo = f(EX[:, l]), f(X[:, l])
                    v.tensor_tensor(xo[:, :, 0], ex[:, :, 0], f(dbt)[:, :, 0], ALU.mult)
                    v.tensor_tensor(xo[:, :, 1], ex[:, :, 1], f(ct)[:, :, 1], ALU.mult)
                wait(v, g_qm, n.at(1, 0))
                v.tensor_tensor(QF[:], EX[:, LV], ct, ALU.mult).then_inc(v_x, 1)

            def split(n):
                v.wait_ge(a_h, n.at(1, 1))
                v.tensor_tensor(R[:].rearrange("p l t -> p (l t)"), X[:].rearrange("p l t -> p (l t)"), PT[:, 0], ALU.subtract).then_inc(v_r, 1)
                v.wait_ge(a_m, n.at(1, 1))
                link(v.tensor_tensor(PT[:, 2], R[:].rearrange("p l t -> p (l t)"), PT[:, 1], ALU.subtract))
                for l in range(LV):
                    src = PT[:, :, l * P:(l + 1) * P].rearrange("p q (k a j) -> p q k a j", a=2, j=1 << l)[:, :, :, 1]
                    x = v.tensor_copy(PTQ[:, :, l * HALF:(l + 1) * HALF].rearrange("p q (k j) -> p q k j", j=1 << l), src)
                x.then_inc(v_l, 1)

            def x1(b, s):
                v.wait_ge(p_out, b.at(1, 1))
                v.wait_ge(d_xr[b.par], b.uses(16))
                wait(v, g_acc, b.at(1, 0))
                v.tensor_tensor(X1[:], WD[s][:].rearrange("p (t e) -> p t e", e=P), XR[b.par][:], ALU.add).then_inc(v_x1, 1)

            def ln2(b):
                v.wait_ge(v_x1, b.at(1, 1))
                step_over()
                for t in range(C):
                    x = v.bn_stats(ST[:, t], X1[:, t])
                link(x)
                step_over()
                for t in range(C):
                    x = v.bn_aggr(MV[:, t], ST[:, t])
                link(x)
                v.tensor_scalar(VE[:], MV[:, :, 1], EPS, None, ALU.add).then_inc(v_ve2, 1)
                v.wait_ge(g_rs2, b.at(1, 1))
                wait(v, d_sc, b.at(16 * TOPK * C, 0))
                for t in range(C):
                    x = v.tensor_scalar(XW[:, 0, t, 0:P], X1[:, t], MV[:, t, 0:1], RS[:, t:t + 1], ALU.subtract, ALU.mult)
                x.then_inc(v_xw, 1)
                v.tensor_copy(XW[:, :, :, P], IDR[:]).then_inc(v_ids, 1)
                v.wait_ge(v_ids, b.at(1, 1))
                link(v.tensor_scalar(IDR[:], IDR[:], float(L), None, ALU.add))

            def top(m):
                v.wait_ge(p_lg, m.at(1, 1))
                wait(v, v_pos, m.at(1, 0))
                link(v.tensor_tensor(LG[:], WD[SLOT["lg"]][:, 0:C * NE].rearrange("p (c e) -> p c e", e=NE),
                                     gb[:].unsqueeze(1).broadcast_to([P, C, NE]), ALU.add))
                step_over()
                for t in range(C):
                    x = v.max(MX[:, t], LG[:, t])
                link(x)
                step_over()
                for t in range(C):
                    x = v.max_index(IX[:, t], MX[:, t], LG[:, t])
                link(x)
                mx0 = MX[:, :, 0:1]
                v.tensor_tensor(DT[:, :, 0:NE], LG[:], mx0.broadcast_to([P, C, NE]), ALU.subtract)
                v.tensor_tensor(DT[:, :, NE:], MX[:, :, 0:TOPK], mx0.broadcast_to([P, C, TOPK]), ALU.subtract).then_inc(v_lg, 1)
                link(v.tensor_copy(IXF[:], IX[:, :, 0:TOPK].rearrange("p c k -> p k c")))
                link(v.tensor_tensor(OH[:].rearrange("p k c e -> p (k c) e"), iota[:].unsqueeze(1).broadcast_to([P, TOPK * C, NE]),
                                     IXF[:].rearrange("p k c -> p (k c)").unsqueeze(2).broadcast_to([P, TOPK * C, NE]), ALU.is_equal))
                link(v.tensor_tensor(MKS[:], OH[:, 0], OH[:, 1], ALU.add))
                v.tensor_tensor(MKS[:], MKS[:], OH[:, 2], ALU.add).then_inc(v_mk, 1)
                v.wait_ge(a_ex, m.at(1, 1))
                link(v.tensor_reduce(SE[:], DT[:, :, 0:NE], AX.X, ALU.add))
                link(v.reciprocal(RC[:], SE[:]))
                v.tensor_tensor(GK[:, m.index()], DT[:, :, NE:].rearrange("p c k -> p k c"),
                                RC[:].unsqueeze(1).broadcast_to([P, TOPK, C]), ALU.mult)

            def slots(m):
                v.wait_ge(p_rk, m.at(1, 1))
                rk = WD[SLOT["rk"]][:, 0:2 * C * NE].rearrange("p (a c e) -> p a c e", a=2, e=NE)
                for t in range(C):
                    link(v.tensor_tensor(BT[:, t + 1], BT[:, t], rk[:, 1, t], ALU.add))
                link(v.tensor_tensor(PM_[:], rk[:, 0], BT[:, 0:C], ALU.add))
                link(v.tensor_tensor(OH[:], OH[:], PM_[:].unsqueeze(1).broadcast_to([P, TOPK, C, NE]), ALU.mult))
                link(v.tensor_reduce(PF[:], OH[:], AX.X, ALU.add))
                wait(v, d_sc, m.at(16 * TOPK * C, 0))
                v.tensor_copy(BT[:, 0], BT[:, C])
                v.tensor_copy(PU[:], PF[:]).then_inc(v_pos, 1)

            v.memset(zt[:], 0.0).then_inc(v_k, 1)
            v.wait_ge(v_k, 1)
            v.memset(zt[:, P:], SKIP).then_inc(v_zt, 1)
            v.memset(W[:], 0.0).then_inc(v_k, 1)
            v.memset(PA[:], 0.0).then_inc(v_k, 1)
            v.wait_ge(a_k, 1)
            v.wait_ge(d_c, NCONST)
            v.tensor_scalar(aneg2[:], aneg[:], -1.0, None, ALU.mult).then_inc(v_k, 1)
            v.tensor_copy(IDR[:], idc[:]).then_inc(v_k, 1)
            v.tensor_copy(BT[:, 0], ereg[:]).then_inc(v_k, 1)
            v.wait_ge(v_k, 6)

            def prologue(z):
                ln(z); conv(z, 0); ln(z.next()); tok_a(z); tok_b(z); facs(z); split(z)

            NL = {"front": 4 + 1 + 2 + 6 + 1, "back": 8 + 3, "route": 8 + C + 3, "ln": 2}

            def step(b):
                front, back, route = has(b)
                n, m = b.next(), b.next(-1)
                normal = front and not (isinstance(b.i, int) and b.c >= NB - 2)
                if not isinstance(b.i, int):
                    if chain["loop"] is None:
                        chain["base"] = chain["done"] + chain["k"] - NCH * b.c
                    chain["loop"], chain["k"], chain["done"] = b, 0, 0
                elif chain["loop"] is not None:
                    chain["done"], chain["loop"], chain["k"] = chain["base"] + NCH * b.c, None, 0
                if front:
                    conv(n, 0)
                if back:
                    merge(b, 0)
                if front:
                    tok_a(n)
                if route:
                    top(m)
                if back:
                    merge(b, 1)
                if front:
                    tok_b(n)
                if back:
                    gate(b, 0, SLOT["y0"])
                if route:
                    slots(m)
                if front:
                    facs(n)
                    split(n)
                if back:
                    gate(b, 1, SLOT["y1"])
                    x1(b, SLOT["out"])
                    ln2(b)
                if normal:
                    ln(n.next())
                if not isinstance(b.i, int):
                    assert chain["k"] == NCH, chain["k"]

            NCH = sum(NL.values())
            steps(v, prologue, step)
            v.wait_ge(v_pos, NB)
            cnt, tiles, starts = CN[:, 0], CN[:, 1], CN[:, 2]
            link(v.tensor_tensor(cnt, BT[0:1, 0], ereg[0:1], ALU.subtract))
            link(v.tensor_scalar(cnt, cnt, float(P - 1), None, ALU.add))
            link(v.tensor_copy(CI[:], cnt))
            link(v.tensor_scalar(CI[:], CI[:], 7, None, ALU.arith_shift_right))
            link(v.tensor_copy(tiles, CI[:]))
            link(v.memset(CN[:, 3], 0.0))
            link(v.tensor_tensor_scan(starts, tiles, CN[:, 3], 0.0, ALU.add, ALU.add))
            ti = tilei[:].unsqueeze(2).broadcast_to([1, NT, NX])
            CMP = XK[0:1].rearrange("p c f -> p (c f)").bitcast(FP32)[:, 0:NT * NX].rearrange("p (t e) -> p t e", e=NX)
            link(v.tensor_tensor(CMP, starts[:, 0:NX].unsqueeze(1).broadcast_to([1, NT, NX]), ti, ALU.is_le))
            link(v.tensor_reduce(TF[:, 0], CMP, AX.X, ALU.add))
            link(v.tensor_tensor(CMP, CMP, tiles[:, 0:NX].unsqueeze(1).broadcast_to([1, NT, NX]), ALU.mult))
            link(v.tensor_reduce(TF[:, 1], CMP, AX.X, ALU.add))
            link(v.tensor_tensor(TF[:, 2], tilei[:], TF[:, 1], ALU.subtract))
            link(v.tensor_scalar(TF[:, 2], TF[:, 2], float(P), None, ALU.mult))
            link(v.tensor_scalar(TF[:, 3], TF[:, 0], float(REG), None, ALU.mult))
            link(v.tensor_tensor(TF[:, 2], TF[:, 2], TF[:, 3], ALU.add))
            link(v.tensor_scalar(TF[:, 0], TF[:, 0], float(NX - 1), None, ALU.min))
            v.tensor_copy(TROW[:], TF[:, 2])
            v.tensor_copy(TEXP[:], TF[:, 0])
            v.tensor_copy(TTAIL[:], BT[0:1, 0]).then_inc(v_tab, 1)
            v.wait_ge(v_tab, 1)
            v.sem_inc(v_first, 1)
            v.wait_ge(d_e, 16 * 6)

            def take(j):
                e = v.value_load(TEXP[0:1, j_at(j)], min_val=0, max_val=NX - 1)
                wait(v, p_1, j.at(1, -1))
                wait(v, a_g, j.at(1, -1))
                v.tensor_copy(WS[j.c % 2][:], W1B[:, e]).then_inc(v_ws, 1)
                v.wait_ge(d_xs[j.c % 4], j.uses(4, 16))
                wait(v, d_ys[j.c % 2], j.back())
                v.tensor_copy(ID[j.c % 4][:], XS[j.c % 4][:, P:]).then_inc(v_id, 1)
                v.wait_ge(p_t, j.at(1, 1))
                v.tensor_copy(XTT[j.c % 2][:], WD[0][:, (j.c % 2) * 512:(j.c % 2) * 512 + P]).then_inc(v_xt, 1)

            def give(j):
                e = v.value_load(TEXP[0:1, j_at(j)], min_val=0, max_val=NX - 1)
                v.wait_ge(p_2, j.at(1, 1))
                wait(v, d_ys[j.c % 2], j.prior(2, 16))
                v.tensor_tensor(YT[j.c % 2][:], PM[j.c % 2][:].rearrange("p a c t -> p (a c t)")[:, 0:P], B2[:, e], ALU.add).then_inc(v_y, 1)

            def tile(j, left):
                if not left or left > 2:
                    take(j.next(2))
                give(j)

            def first_two():
                take(Tile(0, 0, UN)); take(Tile(0, 1, UN))

            every(v, first_two, tile, NT, UN)

            def combine(q, left):
                b, c = q.pair()
                k = q.c % 2
                v.wait_ge(p_s2, q.at(1, 1))
                v.wait_ge(d_q[k], q.uses(2, 16 * 5))
                wait(v, d_o2[k], q.prior(2, 16))
                T = QB // P
                base = n2[0] if isinstance(q.i, int) and q.c < 4 else None
                def lnk(x):
                    x.then_inc(v_cq, 1)
                    n2[0] += 1
                    v.wait_ge(v_cq, q.at(TOPK, (n2[0] - 1) % TOPK + 1))
                lnk(v.tensor_tensor(OQ[k][:], PA[:], AQ[k][:], ALU.add))
                for r in range(TOPK):
                    for t in range(T):
                        x = v.scalar_tensor_tensor(OQ[k][:, t], YQ[k][:, r, t], GK[:, b, r, c * T + t:c * T + t + 1], OQ[k][:, t], ALU.mult, ALU.add)
                    if r < TOPK - 1:
                        lnk(x)
                x.then_inc(v_q, 1)

            n2 = [0]
            every(v, lambda: None, combine, NQ, 2)

        @block.tensor
        def _(t):
            t.wait_ge(d_c, NCONST)
            t.wait_ge(v_k, 2)

            release = {"xnt": (a_xt, 1, 1), "xi0": (v_conv, 2, 1), "xi1": (v_conv, 2, 2), "z0": (a_z, 2, 1), "z1": (a_z, 2, 2),
                       "x2t": (a_x2t, 1, 1), "lg": (v_lg, 1, 1), "rk": (v_pos, 1, 1), "ua": (a_ut, 2, 1), "ub": (a_ut, 2, 2), "lv": (a_e, 1, 1), "y0": (v_gate, 2, 1), "y1": (v_gate, 2, 2), "out": (v_x1, 1, 1)}
            last_use = {}

            def slot(name, b):
                k = SLOT[name]
                if k in last_use:
                    prev, of = last_use[k]
                    sem_, per, which = release[prev]
                    t.wait_ge(sem_, of.at(per, which))
                last_use[k] = (name, b)
                return WD[k]

            def p1(n):
                ps = slot("xnt", n)
                t.wait_ge(v_ln, n.at(1, 1))
                for c in range(C):
                    x = t.transpose(ps[:, c * P:(c + 1) * P], XN[:, c], ident[:])
                x.then_inc(p_xnt, 1)
                t.wait_ge(a_xt, n.at(1, 1))
                for m in range(4):
                    ps = slot(("xi0", "xi1", "z0", "z1")[m], n)
                    for k in range(2):
                        x = t.matmul(ps[:, k * 512:(k + 1) * 512], w_in[:, m * P:(m + 1) * P], XT[:, k * 512:(k + 1) * 512], start=True, stop=True)
                    x.then_inc(p_xi if m < 2 else p_z, 1)

            def p2(n, b):
                t.wait_ge(a_u, n.at(2, 2))
                if b is not None:
                    t.wait_ge(a_hb, b.at(1, 1))
                for c in range(C):
                    for h in range(EH):
                        x = t.matmul(SM[:, c * 3 * N:(c + 1) * 3 * N], U[n.par][:, h, c * P:(c + 1) * P], w_bcd[:, h], start=(h == 0), stop=(h == EH - 1))
                x.then_inc(p_bcd, 1)
                for k in range(2):
                    ps = slot(("ua", "ub")[k], n)
                    for c in range(4):
                        for h in range(EH):
                            o = (c * EH + h) * P
                            x = t.transpose(ps[:, o:o + P], U[n.par][:, h, (4 * k + c) * P:(4 * k + c + 1) * P], ident[:])
                    x.then_inc(p_ut, 1)

            def p3(n):
                t.wait_ge(v_g, n.at(1, 1))
                g2 = GG[:].rearrange("p c n -> p (c n)")
                ps = slot("lv", n)
                for k in range(2):
                    x = t.matmul(ps[:, k * 512:(k + 1) * 512], g2, tlv[:, k * 512:(k + 1) * 512], start=True, stop=True)
                x.then_inc(p_lv, 1)
                t.matmul(SM[:, 0:P], tend[:], g2, start=True, stop=True)
                t.matmul(SM[:, P:2 * P], onesm[:], g2, start=True, stop=True)
                t.transpose(SM[:, 2 * P:3 * P], DB[:].rearrange("p c n -> p (c n)"), ident[:])
                t.transpose(SM[:, 3 * P:4 * P], CT[:].rearrange("p c n -> p (c n)"), ident[:]).then_inc(p_dec, 1)

            def states(b):
                t.wait_ge(v_w, b.at(1, 1))
                t.wait_ge(v_x, b.at(1, 1))
                t.wait_ge(a_ut, b.at(2, 2))
                for c in range(C - 1):
                    x = t.matmul(SM[:, 0:E], W[:, c * P:(c + 1) * P], UT[b.par][:, c], start=(c == 0), stop=(c == C - 2))
                x.then_inc(p_hb, 1)

            def levels(b, k):
                if k == 0:
                    t.wait_ge(d_r, b.at(32 * NCMB, 32 * NCMB))
                wait(t, v_m, b.at(2, k))

                def pair(out_, c, l, s0, sn, t0, tn):
                    return t.matmul(out_, XK[:, c, l * P + s0:l * P + s0 + sn], XQ[:, c, l * HALF + t0:l * HALF + t0 + tn], start=True, stop=True)
                for cc in range(CG):
                    c = k * CG + cc
                    for l in (6, 5, 4):
                        w = 1 << l
                        for blk in range(P // (2 * w)):
                            s = blk * 2 * w
                            x = pair(PA[s:s + w, cc, s + w:s + 2 * w], c, l, s, w, blk * w, w)
                x.then_inc(p_a, 1)
                for q in range(2):
                    for l in (3 - 2 * q, 2 - 2 * q):
                        for cc in range(CG):
                            x = pair(PM[q][:, (3 - l) % 2, cc], k * CG + cc, l, 0, P, 0, HALF)
                    x.then_inc(p_m, 1)

            def ys(b, k):
                ps = slot(f"y{k}", b)
                t.wait_ge(v_m, b.at(2, k + 1))
                t.wait_ge(a_hb, b.at(1, 1))
                t.wait_ge(g_qm, b.at(1, 1))
                for cc in range(CG):
                    c = k * CG + cc
                    for h in range(EH):
                        o = ps[:, h * 512 + cc * P:h * 512 + (cc + 1) * P]
                        t.matmul(o, UT[b.par][:, c, h * P:(h + 1) * P], MT[k][:, cc], start=True, stop=False)
                        x = t.matmul(o, HB[:, h * P:(h + 1) * P], QM[b.par][:, c], start=False, stop=True)
                x.then_inc(p_y, 1)

            def x2t(m):
                t.wait_ge(v_xw, m.at(1, 1))
                ps = slot("x2t", m)
                for c in range(C):
                    x = t.transpose(ps[:, c * P:(c + 1) * P], XW[:, 0, c, 0:P], ident[:])
                x.then_inc(p_x2t, 1)

            def logits(m):
                t.wait_ge(a_x2t, m.at(1, 1))
                ps = slot("lg", m)
                for c in range(C):
                    x = t.matmul(ps[:, c * NE:(c + 1) * NE], X2T[:, c * P:(c + 1) * P], gw[:], start=True, stop=True)
                x.then_inc(p_lg, 1)

            def ranks(m):
                t.wait_ge(v_mk, m.at(1, 1))
                ps = slot("rk", m)
                mk = MKS[:].rearrange("p c e -> p (c e)")
                t.matmul(ps[:, 0:P], tri[:], mk, start=True, stop=True)
                t.matmul(ps[:, P:2 * P], onesm[:], mk, start=True, stop=True).then_inc(p_rk, 1)

            def outp(b):
                GT = U[b.par]
                ps = slot("out", b)
                t.wait_ge(g_gate, b.at(2, 2))
                for c in range(C):
                    for h in range(EH):
                        x = t.matmul(ps[:, c * P:(c + 1) * P], GT[:, h, c * P:(c + 1) * P], w_out[:, h], start=(h == 0), stop=(h == EH - 1))
                x.then_inc(p_out, 1)

            def step(b):
                front, back, route = has(b)
                n, m = b.next(), b.next(-1)
                if not isinstance(b.i, int) or b.c == NB - 2:
                    last_use.update({0: ("y1", m), 1: ("out", m)})
                if front:
                    p1(n)
                if back:
                    states(b)
                    levels(b, 0)
                if route:
                    x2t(m)
                if front:
                    p2(n, b)
                if back:
                    ys(b, 0)
                if route:
                    logits(m)
                if back:
                    levels(b, 1)
                if front:
                    p3(n)
                if route:
                    ranks(m)
                if back:
                    ys(b, 1)
                    outp(b)

            def prologue(b):
                p1(b); p2(b, None); p3(b)

            steps(t, prologue, step)
            t.wait_ge(p_rk, NB)
            t.sem_inc(p_first, 1)
            t.wait_ge(d_e, 16 * 6)
            t.wait_ge(v_tab, 1)

            def turn(j):
                t.wait_ge(d_xs[j.c % 4], j.uses(4, 16))
                wait(t, v_xt, j.at(1, -1))
                t.transpose(WD[0][:, (j.c % 2) * 512:(j.c % 2) * 512 + P], XS[j.c % 4][:, 0:P], ident[:]).then_inc(p_t, 1)

            def up(j):
                t.wait_ge(v_xt, j.at(1, 1))
                t.wait_ge(v_ws, j.at(1, 1))
                wait(t, a_g, j.at(1, -1))
                for h in range(FH):
                    o = (j.c % 2) * 512 + h * P
                    x = t.matmul(WD[1][:, o:o + P], WS[j.c % 2][:, h * P:(h + 1) * P], XTT[j.c % 2][:], start=True, stop=True)
                x.then_inc(p_1, 1)

            def down(j):
                e = t.value_load(TEXP[0:1, j_at(j)], min_val=0, max_val=NX - 1)
                t.wait_ge(a_g, j.at(1, 1))
                wait(t, v_y, j.at(1, -1))
                o = PM[j.c % 2][:].rearrange("p a c t -> p (a c t)")[:, 0:P]
                for h in range(FH):
                    x = t.matmul(o, HT[j.c % 2][:, h], W2[:, e, h], start=(h == 0), stop=(h == FH - 1))
                x.then_inc(p_2, 1)

            def tile(j, left):
                if not left or left > 2:
                    turn(j.next(2))
                if left != 1:
                    up(j.next())
                down(j)

            def first_two():
                turn(Tile(0, 0, UN)); turn(Tile(0, 1, UN)); up(Tile(0, 0, UN))

            t.wait_ge(v_pos, NB)
            every(t, first_two, tile, NT, UN)

            def s_up(q):
                t.wait_ge(d_q[q.c % 2], q.uses(2, 16 * 5))
                for f in range(FS // P):
                    wait(t, a_s, q.at(4, f + 1 - 4))
                    t.matmul(WD[f // 2][:, (f % 2) * QB:(f % 2 + 1) * QB], SW1[:, f * P:(f + 1) * P], XQB[q.c % 2][:], start=True, stop=True).then_inc(p_s1, 1)

            def s_down(q):
                t.wait_ge(a_s, q.at(4, 4))
                wait(t, v_q, q.at(1, 0))
                for c in range(QB // P):
                    for f in range(FS // P):
                        x = t.matmul(PA[:, c], HS[q.c % 2][:, f, c * P:(c + 1) * P], SW2[:, f], start=(f == 0), stop=(f == FS // P - 1))
                x.then_inc(p_s2, 1)

            def block(q, left):
                if left != 1:
                    s_up(q.next())
                s_down(q)
            t.wait_ge(v_y, NT)
            every(t, lambda: s_up(Tile(0, 0, 2)), block, NQ, 2)


def kernel(**inputs):
    import numpy as np
    import concourse.bacc as _bacc
    from concourse import mybir as _mybir
    from concourse.bass_utils import run_bass_kernel_spmd as _run

    def two(a):
        return np.ascontiguousarray(a.reshape(2, 128, -1).transpose(1, 0, 2))

    g = {k.replace("L0_attn_", "").replace("L0_ffn_", "f_"): np.asarray(v) for k, v in inputs.items()}
    idx = np.arange(128)
    f32 = np.float32
    tl = np.zeros((128, 8, 128), f32)
    mk = np.zeros((128, 4, 4, 64), f32)
    for l in range(7):
        mid = (idx >> (l + 1) << (l + 1)) + (1 << l)
        right = (idx >> l) & 1 == 1
        i, t = idx[:, None], idx[None, :]
        tl[:, l] = np.where(right[None, :], (i >= mid[None, :]) & (i <= t), (i > t) & (i < mid[None, :]))
        if l < 4:
            tr = idx[right]
            mk[:, 3 - l] = ((~right)[:, None] & ((idx >> (l + 1))[:, None] == (tr >> (l + 1))[None, :])).astype(f32)[:, None, :]
    tl[:, 7] = idx[:, None] <= idx[None, :]
    w_bcd = np.concatenate([g["W_dt"], g["W_x"]], 0).T
    arr = {
        "x": g["x"], "ident": np.eye(128, dtype=f32), "onesm": np.ones((128, 128), f32), "tlv": tl.reshape(128, 1024),
        "tend": (idx[:, None] > idx[None, :]).astype(f32), "msk": mk,
        "rowmask": (idx[:, None] // 16 == np.arange(8)[None, :]).astype(f32),
        "w_in": g["W_in"].T, "conv_w": two(g["conv_w"].reshape(256, 4)), "conv_b": two(g["conv_b"])[:, :, 0],
        "w_bcd": two(w_bcd), "bdt": np.broadcast_to(g["b_dt"], (128, 16)), "alog": np.broadcast_to(g["A_log"], (128, 16)),
        "gw": np.concatenate([g["f_gW"], np.zeros((128, 1), f32)], 1),
        "gb": np.broadcast_to(np.concatenate([g["f_gb"], np.full(1, -1e30, f32)]), (128, NE)),
        "sb2": np.broadcast_to(g["f_sb2"], (128, 128)), "iota": np.broadcast_to(np.arange(NE, dtype=f32), (128, NE)),
        "idc": (np.arange(TOPK)[None, :, None] * TOK + np.arange(C)[None, None, :] * P + idx[:, None, None]).astype(f32),
        "ereg": np.broadcast_to(np.arange(NE, dtype=f32) * REG, (128, NE)), "tri": (idx[:, None] < idx[None, :]).astype(f32),
        "tilei": np.arange(NT, dtype=f32)[None],
        "w1b": np.concatenate([g["f_rW1"].transpose(1, 0, 2), g["f_rb1"].reshape(NX, FH, P).transpose(2, 0, 1)], 2),
        "w2": g["f_rW2"].reshape(NX, FH, P, P).transpose(2, 0, 1, 3), "b2": np.broadcast_to(g["f_rb2"], (128, NX, P)),
        "sw1": g["f_sW1"][0], "sb1": g["f_sb1"].reshape(FS // P, P).T, "sw2": g["f_sW2"].reshape(FS // P, P, P).transpose(1, 0, 2),
        "dcol": two(g["D"])[:, :, 0], "w_out": two(g["W_out"].T),
    }
    nc = _bacc.Bacc("TRN2", target_bir_lowering=False, num_devices=1)
    arrays, d = {}, {}
    for k, a in arr.items():
        a = np.ascontiguousarray(a)
        arrays[f"in_{k}_dram"] = a
        d[k] = nc.dram_tensor(f"in_{k}_dram", a.shape, _mybir.dt.from_np(a.dtype), kind="ExternalInput").ap()
    out = nc.dram_tensor("out_0_dram", (8, 1024, 128), _mybir.dt.float32, kind="ExternalOutput").ap()
    build(nc, d, out)
    r = _run(nc, [arrays], core_ids=[0])
    return r.results[0]["out_0_dram"]
```

```python
from contextlib import ExitStack
import concourse.bass as bass
from concourse import mybir

FP32 = mybir.dt.float32
BF16 = mybir.dt.bfloat16
U32 = mybir.dt.uint32
I32 = mybir.dt.int32
ALU = mybir.AluOpType
ACT = mybir.ActivationFunctionType
AX = mybir.AxisListType

P = 128
NB = 8
L = 1024
C = L // P
N = 16
E = 256
EH = E // P
LV = 7
CG = 4
G = C // CG
HALF = P // 2
EPS = 1e-5
K_PARTS = [0, 0, 1, 1, 0, 2]
Q_PARTS = [0, 1, 0, 1, 2, 0]
NCMB = len(K_PARTS)
KR = NCMB * N


NX = 15
NE = 16
TOPK = 3
F = 256
FH = F // P
NWE = F + FH + P + FH * P
FS = 512
TOK = NB * L
REG = TOK + P
XW_ = P + 1
UN = 8
NT = -(-(TOK * TOPK // P + NX) // UN) * UN
SPARE = NT - TOK * TOPK // P
SKIP = 30000.0
QD = 4
QB = 512
NQ = TOK // QB


class Tile:

    def __init__(self, i, c, un):
        self.i, self.c, self.un = i, c, un

    def at(self, per, k):
        return self.i * (self.un * per) + (self.c * per + k)

    def uses(self, bufs, per):
        return self.i * (self.un // bufs * per) + (self.c // bufs + 1) * per

    def next(self, d=1):
        return Tile(self.i, self.c + d, self.un)

    def prior(self, bufs, per):
        return self.i * (self.un // bufs * per) + self.c // bufs * per

    def index(self):
        return self.i * self.un + self.c

    def pair(self):
        return self.i * (self.un // 2) + self.c // 2, self.c % 2


def j_at(j):
    at = j.index()
    return slice(at, at + 1) if isinstance(at, int) else bass.ds(at, 1)


def every(eng, prologue, step, count, un):
    prologue()
    for c in range(un):
        step(Tile(0, c, un), 0)
    with eng.Fori(0, (count - 2 * un) // un) as i:
        for c in range(un, 2 * un):
            step(Tile(i, c, un), 0)
    for c in range(count - un, count):
        step(Tile(0, c, un), count - c)


class Batch:

    def __init__(self, i, c):
        self.i, self.c = i, c

    def at(self, per, k):
        return self.i * (2 * per) + (self.c * per + k)

    def uses(self, per):
        return self.i * per + (self.c // 2 + 1) * per

    @property
    def par(self):
        return self.c % 2

    def next(self, d=1):
        return Batch(self.i, self.c + d)

    def index(self):
        return self.i * 2 + self.c


def wait(eng, sem, value):
    if isinstance(value, int) and value <= 0:
        return
    eng.wait_ge(sem, value)


def wait_all(eng, *waits):
    ready = [(s, v if isinstance(v, int) else eng.snap(v)) for s, v in waits]
    for s, v in ready:
        wait(eng, s, v)


def build(nc, d, out):
    ctx, first, second = ExitStack(), ExitStack(), ExitStack()
    with ctx:
        stack = [ctx]

        def sb(name, shape, dt=FP32):
            return stack[0].enter_context(nc.sbuf_tensor(name, shape, dt))

        def pb(name, shape, dt=FP32):
            return ctx.enter_context(nc.psum_tensor(name, shape, dt))

        def sem(name):
            return ctx.enter_context(nc.semaphore(name))

        ident = sb("ident", [P, P]); GK = sb("GK", [P, NB, TOPK, C])
        TROW = sb("TROW", [1, NT], I32); TEXP = sb("TEXP", [1, NT], I32); TTAIL = sb("TTAIL", [1, NE], I32)
        gt = sb("gt", [1, 16]); zt = sb("zt", [P, XW_]); gtp = sb("gtp", [1, 10]); mh1 = sb("mh1", [1, 1])
        stack[0] = first
        XL = [sb(f"XL{k}", [P, C, P]) for k in range(2)]
        XN = sb("XN", [P, C, P]); XT = sb("XT", [P, L]); CA = sb("CA", [P, EH, L])
        U = [sb("U0", [P, EH, L])]; ZS = [sb("ZS0", [P, EH, L])]
        onesm = sb("onesm", [P, P]); tlv = sb("tlv", [P, (LV + 1) * P]); tend = sb("tend", [P, P])
        msk = sb("msk", [P, 4, CG, HALF]); rowmask = sb("rowmask", [P, C])
        w_in = sb("w_in", [P, 2 * E]); conv_w = sb("conv_w", [P, EH, 4]); conv_b = sb("conv_b", [P, EH])
        w_bcd = sb("w_bcd", [P, EH, 3 * N]); bdt = sb("bdt", [P, N]); alog = sb("alog", [P, N]); aneg = sb("aneg", [P, N])
        dcol = sb("dcol", [P, EH]); w_out = sb("w_out", [P, EH, P]); mhalf = sb("mhalf", [P, C])
        aneg2 = sb("aneg2", [P, N])
        gw = sb("gw", [P, NE]); gb = sb("gb", [P, NE]); sb2 = sb("sb2", [P, P]); iota = sb("iota", [P, NE])
        idc = sb("idc", [P, TOPK, C]); ereg = sb("ereg", [P, NE]); tri = sb("tri", [P, P]); tilei = sb("tilei", [1, NT])
        XR = [sb(f"XR{k}", [P, C, P]) for k in range(2)]
        ST = sb("ST", [P, C, 6]); MV = sb("MV", [P, C, 2]); VE = sb("VE", [P, C]); RS = sb("RS", [P, C])
        U.append(sb("U1", [P, EH, L])); ZS.append(sb("ZS1", [P, EH, L]))
        UT = [sb(f"UT{k}", [P, C, E]) for k in range(2)]
        D0 = sb("D0", [P, C, N]); AB = sb("AB", [P, C, N]); LN1 = sb("LN1", [P, C, N]); DEL = sb("DEL", [P, C, N])
        GG = sb("GG", [P, C, N]); DB = sb("DB", [P, C, N]); CT = sb("CT", [P, C, N]); TM = sb("TM", [P, C, N]); M0 = sb("M0", [P, C])
        KE = sb("KE", [P, 2, C, N]); W = sb("W", [P, C * C * N]); EX = sb("EX", [P, LV + 1, P])
        X = sb("X", [P, LV, P]); R = sb("R", [P, LV, P]); PT = sb("PT", [P, 3, LV * P], BF16); PTQ = sb("PTQ", [P, 3, LV * HALF], BF16)
        QF = sb("QF", [P, P]); QM = [sb(f"QM{k}", [P, C, P]) for k in range(2)]
        XK = sb("XK", [KR, C, LV * P], BF16); XQ = sb("XQ", [KR, C, LV * HALF], BF16)
        DG = [sb(f"DG{k}", [P, CG, P]) for k in range(G)]
        MT = [sb(f"MT{k}", [P, CG, P]) for k in range(G)]
        HB = sb("HB", [P, E]); X1 = sb("X1", [P, C, P])
        XWB = [sb(f"XW{k}", [P, TOPK, C, XW_]) for k in range(2)]; ACC = sb("ACC", [P, C, P]); X2T = sb("X2T", [P, L]); IDR = sb("IDR", [P, TOPK, C])
        LG = sb("LG", [P, C, NE]); MX = sb("MX", [P, C, 8]); IX = sb("IX", [P, C, 8], U32); IXF = sb("IXF", [P, TOPK, C])
        DT = sb("DT", [P, C, NE + TOPK]); SE = sb("SE", [P, C]); RC = sb("RC", [P, C])
        OH = sb("OH", [P, TOPK, C, NE]); MKS = sb("MKS", [P, C, NE]); BT = sb("BT", [P, C + 1, NE]); PM_ = sb("PM_", [P, C, NE])
        PF = sb("PF", [P, TOPK, C]); PU = sb("PU", [P, TOPK, C], U32)
        CN = sb("CN", [1, 6, NE]); CI = sb("CI", [1, NE], I32)
        TF = R[0:1].rearrange("p l f -> p (l f)")[:, 0:4 * NT].rearrange("p (k n) -> p k n", k=4)
        stack[0] = second
        first.close()
        WE = sb("WE", [P, NX, NWE])
        SW1 = sb("SW1", [P, FS]); SB1 = sb("SB1", [P, FS // P]); SW2 = sb("SW2", [P, FS // P, P])
        XS = [sb(f"XS{k}", [P, XW_]) for k in range(UN)]; ID = [sb(f"ID{k}", [P, 1], U32) for k in range(UN)]
        WS = [sb(f"WS{k}", [P, NWE]) for k in range(UN)]; XTT = [sb(f"XTT{k}", [P, P]) for k in range(4)]
        HT = [sb(f"HT{k}", [P, FH, P]) for k in range(4)]; YT = [sb(f"YT{k}", [P, P]) for k in range(UN)]
        XQB = [sb(f"XQB{k}", [P, QB]) for k in range(QD)]; AQ = [sb(f"AQ{k}", [P, QB // P, P]) for k in range(QD)]
        YQ = [sb(f"YQ{k}", [P, TOPK, QB // P, P]) for k in range(QD)]; HS = [sb(f"HS{k}", [P, FS // P, QB]) for k in range(2)]
        OQ = [sb(f"OQ{k}", [P, QB // P, P]) for k in range(2)]
        second.close()
        stack[0] = ctx
        WD = [pb(f"WD{k}", [P, 1024]) for k in range(2)]
        SM = pb("SM", [P, 512]); PA = pb("PA", [P, CG, P]); PM = [pb(f"PM{k}", [P, 2, CG, HALF]) for k in range(2)]
        dk = nc.dram_tensor("dk", [3, C, N, LV * P], BF16)
        dq = nc.dram_tensor("dq", [3, C, N, LV * HALF], BF16)

        dx2t = nc.dram_tensor("dx2t", [P, NB, L], FP32)
        dacc = nc.dram_tensor("dacc", [NB, C, P, P], FP32)
        dslot = nc.dram_tensor("dslot", [NX * REG + SPARE * P, XW_], FP32)
        dy = nc.dram_tensor("dy", [TOPK * TOK, P], FP32)

        d_st, d_sc, d_z, d_tail = sem("d_stored"), sem("d_dispatched"), sem("d_spare"), sem("d_tails")
        p_x2t, p_lg, p_rk = sem("pe_x2t"), sem("pe_logits"), sem("pe_ranks")
        a_xc, a_x2t, a_ex, a_end = sem("act_xcopies"), sem("act_x2t"), sem("act_gates"), sem("act_end")
        v_ve2, v_xw, v_ids, v_lg, v_mk, v_pos, v_tab, v_zt = [sem("dve_" + x) for x in "var2 xw ids logits masks slots tables zt".split()]
        d_ac = sem("d_acc")
        v_cq, g_s = sem("dve_combine_chain"), sem("pool_step_over")
        v_first, p_first, g_first, a_first = sem("dve_first_part"), sem("pe_first_part"), sem("pool_first_part"), sem("act_first_part")
        d_e, d_sw, a_id = sem("d_expert_weights"), sem("d_shared_weights"), sem("act_tile_ids"); d_xs = [sem(f"d_rows{k}") for k in range(UN)]; d_ys = [sem(f"d_result{k}") for k in range(UN)]
        p_t, p_1, p_2 = sem("pe_rows"), sem("pe_hidden"), sem("pe_result")
        v_xt, v_ws, v_y = sem("dve_tile_rows"), sem("dve_tile_weights"), sem("dve_tile_result")
        a_g = sem("act_gelu")
        d_q = [sem(f"d_block{k}") for k in range(QD)]; d_qy = [sem(f"d_block_results{k}") for k in range(QD)]; d_o2 = [sem(f"d_out{k}") for k in range(2)]
        p_s1, p_s2, a_s, v_q = sem("pe_shared_hidden"), sem("pe_shared"), sem("act_shared"), sem("dve_combined")
        g_c2 = sem("pool_acc_first")
        g_rs2, g_acc, v_gated = sem("pool_rstd2"), sem("pool_acc"), sem("dve_gated")
        d_c, d_w, d_r, d_o = sem("d_const"), sem("d_parts_written"), sem("d_parts_read"), sem("d_out")
        d_x = [sem(f"d_x{k}") for k in range(2)]; d_xr = [sem(f"d_xr{k}") for k in range(2)]
        (p_xnt, p_xi, p_z, p_bcd, p_ut, p_dec, p_lv, p_hb, p_a, p_m, p_y, p_out) = [
            sem("pe_" + s) for s in "xnt xi z bcd ut dec lv hb a m y out".split()]
        (a_k, a_xt, a_c0, a_z, a_u, a_hb, a_ut, a_sp, a_ln, a_ke, a_e, a_h, a_m) = [
            sem("act_" + s) for s in "const xt c0 z u hb ut sp ln ke e hi mid".split()]
        (v_k, v_ln, v_ve, v_conv, v_ab, v_g, v_m0, v_w, v_x, v_r, v_l, v_m, v_gate, v_x1, v_c) = [
            sem("dve_" + s) for s in "const ln var conv ab g m0 w x rest lo merge gate x1 chain".split()]
        g_rs, g_dg, g_qm, g_gate, g_c = [sem("pool_" + s) for s in "rstd diag qm gate chain".split()]
        n_const = 0
        xv = d["x"].rearrange("b (t p) e -> b p t e", p=P)
        ov = out.rearrange("b (t p) e -> b p t e", p=P)

        def t_slot(j):
            o = j.c % 2 * 512
            return WD[0][:, o:o + P]

        def h_slot(j, h):
            k = j.c % 4
            bank = WD[1][:, k * 512:(k + 1) * 512] if k < 2 else SM[:] if k == 2 else PA[:].rearrange("p c t -> p (c t)")
            return bank[:, h * P:(h + 1) * P]

        def o_slot(j):
            return PM[j.c % 2][:].rearrange("p a c t -> p (a c t)")[:, 0:P]

        block = ctx.enter_context(nc.Block())

        def steps(eng, prologue, step):
            prologue(Batch(0, 0))
            for b in (0, 1):
                step(Batch(0, b))
            with eng.Fori(0, (NB - 4) // 2) as i:
                step(Batch(i, 2))
                step(Batch(i, 3))
            for b in (NB - 2, NB - 1, NB):
                step(Batch(0, b))

        def has(b):
            if not isinstance(b.i, int):
                return True, True, True
            return b.c < NB - 1, b.c < NB, b.c > 0

        SLOT = {"xnt": 0, "out": 1, "xi0": 0, "xi1": 1, "z0": 0, "z1": 1, "ua": 0, "ub": 1, "x2t": 0, "y0": 1, "lg": 0, "lv": 1,
                "rk": 0, "y1": 1}
        consts = [(ident, "ident"), (onesm, "onesm"), (tlv, "tlv"), (tend, "tend"), (msk, "msk"), (rowmask, "rowmask"),
                  (w_in, "w_in"), (conv_w, "conv_w"), (conv_b, "conv_b"), (w_bcd, "w_bcd"), (bdt, "bdt"), (alog, "alog"),
                  (dcol, "dcol"), (w_out, "w_out"), (gw, "gw"), (gb, "gb"), (sb2, "sb2"), (iota, "iota"), (idc, "idc"),
                  (ereg, "ereg"), (tri, "tri"), (tilei, "tilei")]
        NCONST = 16 * len(consts)

        @block.sync
        def _(sp):
            sp.dma_start(XL[0][:], xv[0]).then_inc(d_x[0], 16)
            for tile, name in consts:
                sp.dma_start(tile[:], d[name]).then_inc(d_c, 16)
            sp.dma_start(XL[1][:], xv[1]).then_inc(d_x[1], 16)

            def parts(n):
                fresh, merged, landed = n.at(1, 1), n.at(4, 0), n.at(32, 32)
                if not isinstance(n.i, int):
                    fresh, merged, landed = sp.snap(fresh), sp.snap(merged), sp.snap(landed)
                wait(sp, p_m, merged)
                sp.wait_ge(v_l, fresh)
                sp.dma_start(dk.ap().rearrange("q c n f -> (c n) q f"), PT[:]).then_inc(d_w, 16)
                sp.dma_start(dq.ap().rearrange("q c n f -> (c n) q f"), PTQ[:]).then_inc(d_w, 16)
                sp.wait_ge(d_w, landed)
                for k in range(NCMB):
                    sp.dma_start(XK[k * N:(k + 1) * N], dk[K_PARTS[k]].rearrange("c n f -> n c f")).then_inc(d_r, 16)
                    sp.dma_start(XQ[k * N:(k + 1) * N], dq[Q_PARTS[k]].rearrange("c n f -> n c f")).then_inc(d_r, 16)

            def number(b):
                return b.index() if isinstance(b.i, int) else sp.snap(b.index())

            def load(b):
                at = number(b.next(2))
                sp.wait_ge(v_ln, b.at(1, 1))
                sp.dma_start(XL[b.par][:], xv[at]).then_inc(d_x[b.par], 16)

            def residual(b):
                at = number(b)
                wait(sp, v_x1, b.at(1, -1))
                sp.dma_start(XR[b.par][:], xv[at]).then_inc(d_xr[b.par], 16)

            def store(m):
                at = number(m)
                sp.wait_ge(a_x2t, m.at(1, 1))
                sp.dma_start(dx2t[:, at, :], X2T[:]).then_inc(d_st, 16)

            def store_acc(b):
                at = number(b)
                sp.wait_ge(g_acc, b.at(1, 1))
                sp.dma_start(dacc[at].rearrange("c p e -> p c e"), ACC[:]).then_inc(d_ac, 16)

            def expert_weights():
                sp.wait_ge(v_ln, NB)
                sp.wait_ge(p_xnt, NB)
                sp.wait_ge(p_z, 2 * NB)
                sp.wait_ge(a_u, 2 * NB)
                sp.wait_ge(v_gated, 2 * (NB - 1))
                sp.wait_ge(p_out, NB - 1)
                sp.dma_start(WE[:], d["we"]).then_inc(d_e, 16)

            def step(b):
                front, back, route = has(b)
                if front and route and not (isinstance(b.i, int) and b.c > NB - 3):
                    load(b)
                if back:
                    residual(b)
                if isinstance(b.i, int) and b.c == NB - 1:
                    expert_weights()
                if route:
                    store_acc(b.next(-1))
                    store(b.next(-1))
                if front:
                    parts(b.next())

            def prologue(b):
                sp.wait_ge(v_zt, 1)
                for k in range(SPARE):
                    sp.dma_start(dslot[NX * REG + k * P:NX * REG + (k + 1) * P], zt[:]).then_inc(d_z, 16)
                parts(b)
                load(b)

            steps(sp, prologue, step)

            sp.wait_ge(v_tab, 1)
            for e in range(NX):
                at = sp.value_load(TTAIL[0:1, e:e + 1], min_val=0, max_val=NX * REG - P)
                sp.dma_start(dslot[bass.ds(at, P)], zt[:]).then_inc(d_tail, 16)
            sp.wait_ge(v_first, 1)
            sp.wait_ge(p_first, 1)
            sp.wait_ge(a_first, 1)
            sp.wait_ge(d_sc, 16 * TOPK * C * NB)
            sp.wait_ge(d_ac, 16 * NB)
            sp.wait_ge(d_st, 16 * NB)
            for tile, name in ((SW1, "sw1"), (SB1, "sb1"), (SW2, "sw2")):
                sp.dma_start(tile[:], d[name]).then_inc(d_sw, 16)
            sp.wait_ge(d_tail, 16 * NX)
            sp.wait_ge(d_z, 16 * SPARE)

            def rows(j):
                at = sp.value_load(TROW[0:1, j_at(j)], min_val=0, max_val=NX * REG + SPARE * P - P)
                wait(sp, a_id, j.at(1, 1 - UN))
                sp.dma_start(XS[j.c % UN][:], dslot[bass.ds(at, P)]).then_inc(d_xs[j.c % UN], 16)

            every(sp, lambda: None, lambda j, left: rows(j), NT, UN)

            def block_in(q):
                b, c = q.pair()
                wait(sp, p_s1, q.at(FS // P, FS // P * (1 - QD)))
                wait(sp, v_q, q.at(1, 1 - QD))
                k = q.c % QD
                ts = slice(c * 4, c * 4 + 4)
                sp.dma_start(XQB[k][:], dx2t[:, b, c * QB:(c + 1) * QB]).then_inc(d_q[k], 16)
                sp.dma_start(AQ[k][:], dacc[b, ts].rearrange("c p e -> p c e")).then_inc(d_q[k], 16)

            def results_in(q):
                b, c = q.pair()
                k = q.c % QD
                for r in range(TOPK):
                    src = dy.ap().rearrange("(k b c p) e -> k b p c e", k=TOPK, b=NB, p=P)[r, b, :, c * 4:c * 4 + 4]
                    sp.dma_start(YQ[k][:, r], src).then_inc(d_qy[k], 16)

            def block_out(q):
                b, c = q.pair()
                sp.wait_ge(v_q, q.at(1, 1))
                sp.dma_start(ov[b, :, c * 4:c * 4 + 4], OQ[q.c % 2][:]).then_inc(d_o2[q.c % 2], 16)

            for c in range(QD - 1):
                block_in(Tile(0, c, QD))
            for k in range(UN):
                sp.wait_ge(d_ys[k], 16 * (NT // UN))
            for c in range(QD - 1):
                results_in(Tile(0, c, QD))
            for c in range(NQ):
                if c + QD - 1 < NQ:
                    block_in(Tile(0, c + QD - 1, QD))
                    results_in(Tile(0, c + QD - 1, QD))
                block_out(Tile(0, c, QD))
            for k in range(2):
                sp.wait_ge(d_o2[k], 16 * (NQ // 2))
        @block.gpsimd
        def _(g):
            g.memset(mhalf[:], -0.5).then_inc(g_c, 1)
            g.memset(mh1[:], 0.0).then_inc(g_c, 1)
            g.wait_ge(g_c, 2)

            def rstd(n):
                g.wait_ge(v_ve, n.at(1, 1))
                g.tensor_tensor(RS[:], VE[:], mhalf[:], ALU.pow).then_inc(g_rs, 1)

            def rstd2(b):
                g.wait_ge(v_ve2, b.at(1, 1))
                g.tensor_tensor(RS[:], VE[:], mhalf[:], ALU.pow).then_inc(g_rs2, 1)

            def diag(n):
                g.wait_ge(v_m0, n.at(1, 1))
                wait(g, v_m, n.at(2, 0))
                for k in range(G):
                    g.tensor_tensor(DG[k][:], ident[:].unsqueeze(1).broadcast_to([P, CG, P]),
                                    M0[:, k * CG:(k + 1) * CG].unsqueeze(2).broadcast_to([P, CG, P]), ALU.mult).then_inc(g_dg, 1)

            def qmask(n):
                g.wait_ge(v_x, n.at(1, 1))
                wait(g, p_y, n.at(2, -2))
                g.tensor_tensor(QM[n.par][:], QF[:].unsqueeze(1).broadcast_to([P, C, P]),
                                rowmask[:].unsqueeze(2).broadcast_to([P, C, P]), ALU.mult).then_inc(g_qm, 1)

            def acc(b):
                XW = XWB[b.par]
                g.wait_ge(v_xw, b.at(1, 1))
                wait(g, d_ac, b.at(16, 0))
                g.tensor_tensor(ACC[:], X1[:], XW[:, 0, :, 0:P], ALU.add).then_inc(g_c2, 1)
                g.wait_ge(g_c2, b.at(1, 1))
                g.tensor_tensor(ACC[:], ACC[:], sb2[:].unsqueeze(1).broadcast_to([P, C, P]), ALU.add).then_inc(g_acc, 1)

            def dispatch(m, choices):
                XW = XWB[m.par]
                if choices[0] == 0:
                    g.wait_ge(v_pos, m.at(1, 1))
                    g.wait_ge(a_xc, m.at(2, 2))
                    g.wait_ge(v_ids, m.at(1, 1))
                    g.tensor_tensor(gtp[:, m.par:m.par + 1], mh1[:], mh1[:], ALU.add)
                for k in choices:
                    for t in range(C):
                        g.indirect_dma_start(dslot.ap(), bass.IndirectOffsetOnAxis(ap=PU[:, k, t:t + 1], axis=0), XW[:, k, t, :], None).then_inc(d_sc, 16)

            def prologue(b):
                rstd(b); rstd(b.next()); diag(b); qmask(b)

            def step(b):
                front, back, route = has(b)
                late = route and (not isinstance(b.i, int) or b.c > 1)
                if late:
                    dispatch(b.next(-2), (0,))
                if route:
                    rstd2(b.next(-1))
                if late:
                    dispatch(b.next(-2), (1,))
                if route:
                    acc(b.next(-1))
                if front and not (isinstance(b.i, int) and b.c >= NB - 2):
                    rstd(b.next(2))
                if late:
                    dispatch(b.next(-2), (2,))
                if front:
                    diag(b.next())
                    qmask(b.next())
                if isinstance(b.i, int) and b.c == NB:
                    dispatch(b.next(-1), (0, 1, 2))

            g.wait_ge(d_c, NCONST)
            steps(g, prologue, step)

            def result(j, left):
                g.wait_ge(v_y, j.at(1, 1))
                g.wait_ge(a_id, j.at(1, 1))
                wait(g, g_s, j.at(1, 0))
                g.tensor_tensor(gtp[:, 2:3], mh1[:], mh1[:], ALU.add).then_inc(g_s, 1)
                g.indirect_dma_start(dy.ap(), bass.IndirectOffsetOnAxis(ap=ID[j.c % UN][:, 0:1], axis=0), YT[j.c % UN][:], None,
                                     bounds_check=TOPK * TOK - 1, oob_is_err=False).then_inc(d_ys[j.c % UN], 16)

            every(g, lambda: None, result, NT, UN)
            for k in range(UN):
                g.wait_ge(d_ys[k], 16 * (NT // UN))

        @block.scalar
        def _(a):
            a.wait_ge(d_c, NCONST)
            a.activation(aneg[:], alog[:], ACT.Exp).then_inc(a_k, 1)

            def wide(sl):
                return WD[sl]

            def front(n, s0):
                a.wait_ge(p_xnt, n.at(1, 1))
                wait(a, p_z, n.at(2, 0))
                a.activation(XT[:], WD[s0][:], ACT.Copy).then_inc(a_xt, 1)
                for h in range(EH):
                    a.wait_ge(p_xi, n.at(2, h + 1))
                    wait(a, a_u, n.at(2, 0))
                    a.activation(CA[:, h], WD[SLOT[f"xi{h}"]][:], ACT.Identity, scale=conv_w[:, h, 3:4], bias=conv_b[:, h:h + 1]).then_inc(a_c0, 1)

            def hb(b):
                a.wait_ge(p_hb, b.at(1, 1))
                wait(a, p_y, b.at(2, 0))
                a.activation(HB[:], SM[:, 0:E], ACT.Copy).then_inc(a_hb, 1)

            def silus(n, s0):
                for h in range(EH):
                    a.wait_ge(v_conv, n.at(2, h + 1))
                    wait(a, p_out, n.at(1, -1))
                    a.activation(U[n.par][:, h], CA[:, h], ACT.Silu).then_inc(a_u, 1)
                for h in range(EH):
                    a.wait_ge(p_z, n.at(2, h + 1))
                    wait(a, v_gated, n.at(2, -2))
                    a.activation(ZS[n.par][:, h], WD[SLOT[f"z{h}"]][:], ACT.Silu).then_inc(a_z, 1)

            def ut(n, s5):
                for h in range(2):
                    a.wait_ge(p_ut, n.at(2, h + 1))
                    wait(a, p_y, n.at(2, -2))
                    a.activation(UT[n.par][:, 4 * h:4 * h + 4, :], WD[(s5 + h) % 2][:].rearrange("p (t e) -> p t e", e=E), ACT.Copy).then_inc(a_ut, 1)

            def soft(n):
                a.wait_ge(v_ab, n.at(1, 1))
                a.activation(AB[:], AB[:], ACT.Exp, scale=-1.0).then_inc(a_sp, 1)
                a.wait_ge(a_sp, n.at(1, 1))
                wait(a, v_g, n.at(1, 0))
                a.activation(LN1[:], AB[:], ACT.Ln, bias=1.0).then_inc(a_ln, 1)

            def expo(n, s8):
                a.wait_ge(p_dec, n.at(1, 1))
                wait(a, v_w, n.at(1, 0))
                a.activation(KE[:], SM[:, 0:2 * C * N].rearrange("p (a c n) -> p a c n", a=2, n=N), ACT.Exp).then_inc(a_ke, 1)
                a.wait_ge(p_lv, n.at(1, 1))
                wait(a, v_x, n.at(1, 0))
                a.activation(EX[:], WD[s8][:].rearrange("p (l t) -> p l t", t=P), ACT.Exp).then_inc(a_e, 1)

            def split(n):
                a.wait_ge(v_x, n.at(1, 1))
                wait(a, d_w, n.at(32, 0))
                a.activation(PT[:, 0], X[:].rearrange("p l t -> p (l t)"), ACT.Copy).then_inc(a_h, 1)
                a.wait_ge(v_r, n.at(1, 1))
                a.activation(PT[:, 1], R[:].rearrange("p l t -> p (l t)"), ACT.Copy).then_inc(a_m, 1)

            def copies(b):
                XW = XWB[b.par]
                a.wait_ge(v_xw, b.at(1, 1))
                for k in (1, 2):
                    a.activation(XW[:, k, :, 0:P], XW[:, 0, :, 0:P], ACT.Copy).then_inc(a_xc, 1)

            def x2t(m):
                a.wait_ge(p_x2t, m.at(1, 1))
                wait(a, p_lg, m.at(1, 0))
                wait(a, d_st, m.at(16, 0))
                a.activation(X2T[:], WD[SLOT["x2t"]][:], ACT.Copy).then_inc(a_x2t, 1)

            def gates(m):
                a.wait_ge(v_lg, m.at(1, 1))
                a.activation(DT[:], DT[:], ACT.Exp).then_inc(a_ex, 1)

            def prologue(b):
                front(b, 0); silus(b, 0); ut(b, SLOT["ua"]); soft(b); expo(b, SLOT["lv"]); split(b)

            def step(b):
                front_, back, route = has(b)
                n, m = b.next(), b.next(-1)
                if front_:
                    front(n, 0)
                if back:
                    hb(b)
                if front_:
                    silus(n, 0)
                if front_:
                    ut(n, SLOT["ua"])
                if route:
                    x2t(m)
                if front_:
                    soft(n)
                if route:
                    copies(m)
                    gates(m)
                if front_:
                    expo(n, SLOT["lv"]); split(n)

            steps(a, prologue, step)
            a.wait_ge(a_xc, 2 * NB)
            a.wait_ge(a_ex, NB)
            a.sem_inc(a_first, 1)

            def hidden(j, left):
                a.wait_ge(p_1, j.at(1, 1))
                wait(a, p_2, j.at(1, -3))
                for h in range(FH):
                    x = a.activation(HT[j.c % 4][:, h], h_slot(j, h), ACT.Gelu, bias=WS[j.c % UN][:, F + h:F + h + 1])
                x.then_inc(a_g, 1)
                a.wait_ge(d_xs[j.c % UN], j.uses(UN, 16))
                wait(a, d_ys[j.c % UN], j.prior(UN, 16))
                a.activation(ID[j.c % UN][:], XS[j.c % UN][:, P:], ACT.Copy).then_inc(a_id, 1)

            every(a, lambda: None, hidden, NT, UN)

            def shared(q, left):
                for f in range(FS // P):
                    a.wait_ge(p_s1, q.at(4, f + 1))
                    if f == 0:
                        wait(a, p_s2, q.at(1, -1))
                    a.activation(HS[q.c % 2][:, f], WD[f // 2][:, (f % 2) * QB:(f % 2 + 1) * QB], ACT.Gelu, bias=SB1[:, f:f + 1]).then_inc(a_s, 1)

            every(a, lambda: None, shared, NQ, QD)

        @block.vector
        def _(v):
            chain = {"done": 0, "loop": None, "base": 0, "k": 0}
            gates_ = [0]

            def link(ins, b=None):
                ins.then_inc(v_c, 1)
                chain["k"] += 1
                v.wait_ge(v_c, chain["done"] + chain["k"] if chain["loop"] is None else chain["loop"].at(NCH, chain["base"] + chain["k"]))

            def step_over():
                v.memset(gt[:, gates_[0] % 16:gates_[0] % 16 + 1], 0.0)
                gates_[0] += 1

            def ln(n):
                v.wait_ge(d_x[n.par], n.uses(16))
                for t in range(C):
                    x = v.bn_stats(ST[:, t], XL[n.par][:, t])
                link(x)
                step_over()
                for t in range(C):
                    x = v.bn_aggr(MV[:, t], ST[:, t])
                link(x)
                wait(v, g_rs, n.at(1, 0))
                v.tensor_scalar(VE[:], MV[:, :, 1], EPS, None, ALU.add).then_inc(v_ve, 1)

            def ln_apply(n):
                v.wait_ge(g_rs, n.at(1, 1))
                wait(v, p_xnt, n.at(1, 0))
                for t in range(C):
                    x = v.tensor_scalar(XN[:, t], XL[n.par][:, t], MV[:, t, 0:1], RS[:, t:t + 1], ALU.subtract, ALU.mult)
                x.then_inc(v_ln, 1)

            def conv(n, h):
                if True:
                    ps = WD[SLOT[f"xi{h}"]]
                    v.wait_ge(a_c0, n.at(2, h + 1))
                    for k in (2, 1, 0):
                        j = 3 - k
                        x = v.scalar_tensor_tensor(CA[:, h, j:], ps[:, 0:L - j], conv_w[:, h, k:k + 1], CA[:, h, j:], ALU.mult, ALU.add)
                        if k:
                            link(x)
                    x.then_inc(v_conv, 1)

            def merge(b, k):
                v.wait_ge(p_a, b.at(2, k + 1))
                v.wait_ge(g_dg, b.at(2, k + 1))
                wait(v, p_y, b.at(2, k - 1))
                link(v.tensor_tensor(MT[k][:], PA[:], DG[k][:], ALU.add))
                for l in (3, 2, 1, 0):
                    q = (3 - l) // 2
                    if l % 2:
                        v.wait_ge(p_m, b.at(4, 2 * k + q + 1))
                    step_over()
                    w = 1 << l
                    o = MT[k][:].rearrange("p c (k a j) -> p (c k) a j", a=2, j=w)[:, :, 1, :]
                    mk = msk[:, 3 - l].bitcast(mybir.dt.int32).rearrange("p c (k j) -> p (c k) j", j=w)
                    dt = PM[q][:, (3 - l) % 2].rearrange("p c (k j) -> p (c k) j", j=w)
                    x = v.copy_predicated(o, mk, dt)
                    if l:
                        link(x)
                x.then_inc(v_m, 1)

            def tok_a(n):
                sm = SM[:, 0:C * 3 * N].rearrange("p (c k n) -> p c k n", k=3, n=N)
                v.wait_ge(p_bcd, n.at(1, 1))
                link(v.tensor_tensor(D0[:], sm[:, :, 0], bdt[:].unsqueeze(1).broadcast_to([P, C, N]), ALU.add))
                wait(v, a_ln, n.at(1, 0))
                v.scalar_tensor_tensor(AB[:], D0[:], -1.0, D0[:], ALU.mult, ALU.max).then_inc(v_ab, 1)

            def tok_b(n):
                sm = SM[:, 0:C * 3 * N].rearrange("p (c k n) -> p c k n", k=3, n=N)
                v.wait_ge(a_ln, n.at(1, 1))
                link(v.scalar_tensor_tensor(DEL[:], D0[:], 0.0, LN1[:], ALU.max, ALU.add))
                wait(v, p_lv, n.at(1, 0))
                v.tensor_tensor(GG[:], DEL[:], aneg2[:].unsqueeze(1).broadcast_to([P, C, N]), ALU.mult)
                v.tensor_tensor(DB[:], DEL[:], sm[:, :, 1], ALU.mult)
                v.tensor_copy(CT[:], sm[:, :, 2]).then_inc(v_g, 1)
                v.wait_ge(v_g, n.at(1, 1))
                link(v.tensor_tensor(TM[:], DB[:], CT[:], ALU.mult))
                wait(v, g_dg, n.at(2, 0))
                v.tensor_reduce(M0[:], TM[:], AX.X, ALU.add).then_inc(v_m0, 1)

            def gate(b, k, s):
                v.wait_ge(p_y, b.at(2, k + 1))
                sl = slice(k * 512, k * 512 + 512)
                GT = U[b.par]
                for h in range(EH):
                    x = v.scalar_tensor_tensor(GT[:, h, sl], U[b.par][:, h, sl], dcol[:, h:h + 1], WD[s][:, h * 512:(h + 1) * 512], ALU.mult, ALU.add)
                x.then_inc(v_gate, 1)
                v.wait_ge(v_gate, b.at(2, k + 1))
                v.tensor_tensor(GT[:, :, sl], GT[:, :, sl], ZS[b.par][:, :, sl], ALU.mult).then_inc(v_gated, 1)

            def facs(n):
                v.wait_ge(a_ke, n.at(1, 1))
                wait(v, p_hb, n.at(1, 0))
                wd = W[:, N:N + (C - 1) * (C + 1) * N].rearrange("p (c k) -> p c k", k=(C + 1) * N)[:, :, 0:N]
                link(v.tensor_tensor(wd, KE[:, 0, 0:C - 1], DB[:, 0:C - 1], ALU.mult))
                w4 = W[:].rearrange("p (a c n) -> p a c n", a=C, n=N)
                for c in range(1, C - 1):
                    x = v.tensor_tensor(w4[:, 0:c, c + 1], w4[:, 0:c, c], KE[:, 1, c].unsqueeze(1).broadcast_to([P, c, N]), ALU.mult)
                    if c < C - 2:
                        link(x)
                x.then_inc(v_w, 1)
                v.wait_ge(a_e, n.at(1, 1))
                wait(v, a_h, n.at(1, 0))
                dbt, ct = SM[:, 2 * P:3 * P], SM[:, 3 * P:4 * P]
                for l in range(LV):
                    f = lambda t: t.rearrange("p (k a j) -> p k a j", a=2, j=1 << l)
                    ex, xo = f(EX[:, l]), f(X[:, l])
                    v.tensor_tensor(xo[:, :, 0], ex[:, :, 0], f(dbt)[:, :, 0], ALU.mult)
                    v.tensor_tensor(xo[:, :, 1], ex[:, :, 1], f(ct)[:, :, 1], ALU.mult)
                wait(v, g_qm, n.at(1, 0))
                v.tensor_tensor(QF[:], EX[:, LV], ct, ALU.mult).then_inc(v_x, 1)

            def split_middle(n):
                v.wait_ge(a_h, n.at(1, 1))
                v.tensor_tensor(R[:].rearrange("p l t -> p (l t)"), X[:].rearrange("p l t -> p (l t)"), PT[:, 0], ALU.subtract).then_inc(v_r, 1)

            def split_low(n):
                v.wait_ge(a_m, n.at(1, 1))
                link(v.tensor_tensor(PT[:, 2], R[:].rearrange("p l t -> p (l t)"), PT[:, 1], ALU.subtract))
                for l in range(LV):
                    src = PT[:, :, l * P:(l + 1) * P].rearrange("p q (k a j) -> p q k a j", a=2, j=1 << l)[:, :, :, 1]
                    x = v.tensor_copy(PTQ[:, :, l * HALF:(l + 1) * HALF].rearrange("p q (k j) -> p q k j", j=1 << l), src)
                x.then_inc(v_l, 1)

            def x1(b, s):
                v.wait_ge(p_out, b.at(1, 1))
                v.wait_ge(d_xr[b.par], b.uses(16))
                wait(v, g_acc, b.at(1, 0))
                v.tensor_tensor(X1[:], WD[s][:].rearrange("p (t e) -> p t e", e=P), XR[b.par][:], ALU.add).then_inc(v_x1, 1)

            def ln2(b):
                v.wait_ge(v_x1, b.at(1, 1))
                step_over()
                for t in range(C):
                    x = v.bn_stats(ST[:, t], X1[:, t])
                link(x)
                step_over()
                for t in range(C):
                    x = v.bn_aggr(MV[:, t], ST[:, t])
                link(x)
                v.tensor_scalar(VE[:], MV[:, :, 1], EPS, None, ALU.add).then_inc(v_ve2, 1)

            def ln2_apply(b):
                XW = XWB[b.par]
                v.wait_ge(g_rs2, b.at(1, 1))
                wait(v, d_sc, b.at(16 * TOPK * C, -16 * TOPK * C))
                for t in range(C):
                    x = v.tensor_scalar(XW[:, 0, t, 0:P], X1[:, t], MV[:, t, 0:1], RS[:, t:t + 1], ALU.subtract, ALU.mult)
                x.then_inc(v_xw, 1)
                v.tensor_copy(XW[:, :, :, P], IDR[:]).then_inc(v_ids, 1)
                v.wait_ge(v_ids, b.at(1, 1))
                link(v.tensor_scalar(IDR[:], IDR[:], float(L), None, ALU.add))

            def top(m):
                v.wait_ge(p_lg, m.at(1, 1))
                wait(v, v_pos, m.at(1, 0))
                link(v.tensor_tensor(LG[:], WD[SLOT["lg"]][:, 0:C * NE].rearrange("p (c e) -> p c e", e=NE),
                                     gb[:].unsqueeze(1).broadcast_to([P, C, NE]), ALU.add))
                step_over()
                for t in range(C):
                    x = v.max(MX[:, t], LG[:, t])
                link(x)
                step_over()
                for t in range(C):
                    x = v.max_index(IX[:, t], MX[:, t], LG[:, t])
                link(x)
                mx0 = MX[:, :, 0:1]
                v.tensor_tensor(DT[:, :, 0:NE], LG[:], mx0.broadcast_to([P, C, NE]), ALU.subtract)
                v.tensor_tensor(DT[:, :, NE:], MX[:, :, 0:TOPK], mx0.broadcast_to([P, C, TOPK]), ALU.subtract).then_inc(v_lg, 1)
                link(v.tensor_copy(IXF[:], IX[:, :, 0:TOPK].rearrange("p c k -> p k c")))
                link(v.tensor_tensor(OH[:].rearrange("p k c e -> p (k c) e"), iota[:].unsqueeze(1).broadcast_to([P, TOPK * C, NE]),
                                     IXF[:].rearrange("p k c -> p (k c)").unsqueeze(2).broadcast_to([P, TOPK * C, NE]), ALU.is_equal))
                link(v.tensor_tensor(MKS[:], OH[:, 0], OH[:, 1], ALU.add))
                v.tensor_tensor(MKS[:], MKS[:], OH[:, 2], ALU.add).then_inc(v_mk, 1)
                v.wait_ge(a_ex, m.at(1, 1))
                link(v.tensor_reduce(SE[:], DT[:, :, 0:NE], AX.X, ALU.add))
                link(v.reciprocal(RC[:], SE[:]))
                v.tensor_tensor(GK[:, m.index()], DT[:, :, NE:].rearrange("p c k -> p k c"),
                                RC[:].unsqueeze(1).broadcast_to([P, TOPK, C]), ALU.mult)

            def slots(m):
                v.wait_ge(p_rk, m.at(1, 1))
                rk = WD[SLOT["rk"]][:, 0:2 * C * NE].rearrange("p (a c e) -> p a c e", a=2, e=NE)
                for t in range(C):
                    link(v.tensor_tensor(BT[:, t + 1], BT[:, t], rk[:, 1, t], ALU.add))
                link(v.tensor_tensor(PM_[:], rk[:, 0], BT[:, 0:C], ALU.add))
                link(v.tensor_tensor(OH[:], OH[:], PM_[:].unsqueeze(1).broadcast_to([P, TOPK, C, NE]), ALU.mult))
                link(v.tensor_reduce(PF[:], OH[:], AX.X, ALU.add))
                wait(v, d_sc, m.at(16 * TOPK * C, 0))
                v.tensor_copy(BT[:, 0], BT[:, C])
                v.tensor_copy(PU[:], PF[:]).then_inc(v_pos, 1)

            v.memset(zt[:], 0.0).then_inc(v_k, 1)
            v.wait_ge(v_k, 1)
            v.memset(zt[:, P:], SKIP).then_inc(v_zt, 1)
            v.memset(W[:], 0.0).then_inc(v_k, 1)
            v.memset(PA[:], 0.0).then_inc(v_k, 1)
            v.wait_ge(a_k, 1)
            v.wait_ge(d_c, NCONST)
            v.tensor_scalar(aneg2[:], aneg[:], -1.0, None, ALU.mult).then_inc(v_k, 1)
            v.tensor_copy(IDR[:], idc[:]).then_inc(v_k, 1)
            v.tensor_copy(BT[:, 0], ereg[:]).then_inc(v_k, 1)
            v.wait_ge(v_k, 6)

            def prologue(z):
                ln(z); ln_apply(z); conv(z, 0); conv(z, 1); ln(z.next()); ln_apply(z.next()); tok_a(z); tok_b(z); facs(z); split_middle(z); split_low(z)

            NL = {"front": 4 + 1 + 2 + 6 + 1, "back": 8 + 3, "route": 8 + C + 3, "ln": 2}

            def step(b):
                front, back, route = has(b)
                n, m = b.next(), b.next(-1)
                normal = front and not (isinstance(b.i, int) and b.c >= NB - 2)
                if not isinstance(b.i, int):
                    if chain["loop"] is None:
                        chain["base"] = chain["done"] + chain["k"] - NCH * b.c
                    chain["loop"], chain["k"], chain["done"] = b, 0, 0
                elif chain["loop"] is not None:
                    chain["done"], chain["loop"], chain["k"] = chain["base"] + NCH * b.c, None, 0
                if route:
                    x1(m, SLOT["out"])
                    ln2(m)
                if front:
                    conv(n, 0)
                    conv(n, 1)
                if route:
                    ln2_apply(m)
                if back:
                    merge(b, 0)
                if front:
                    tok_a(n)
                if normal:
                    ln(n.next())
                if back:
                    gate(b, 0, SLOT["y0"])
                    merge(b, 1)
                if front:
                    tok_b(n)
                if normal:
                    ln_apply(n.next())
                if route:
                    top(m)
                if front:
                    facs(n)
                if route:
                    slots(m)
                if front:
                    split_middle(n)
                if back:
                    gate(b, 1, SLOT["y1"])
                if front:
                    split_low(n)
                if not isinstance(b.i, int):
                    assert chain["k"] == NCH, chain["k"]

            NCH = sum(NL.values())
            steps(v, prologue, step)
            v.wait_ge(v_pos, NB)
            cnt, tiles, starts = CN[:, 0], CN[:, 1], CN[:, 2]
            link(v.tensor_tensor(cnt, BT[0:1, 0], ereg[0:1], ALU.subtract))
            link(v.tensor_scalar(cnt, cnt, float(P - 1), None, ALU.add))
            link(v.tensor_copy(CI[:], cnt))
            link(v.tensor_scalar(CI[:], CI[:], 7, None, ALU.arith_shift_right))
            link(v.tensor_copy(tiles, CI[:]))
            link(v.memset(CN[:, 3], 0.0))
            link(v.tensor_tensor_scan(starts, tiles, CN[:, 3], 0.0, ALU.add, ALU.add))
            ti = tilei[:].unsqueeze(2).broadcast_to([1, NT, NX])
            CMP = XK[0:1].rearrange("p c f -> p (c f)").bitcast(FP32)[:, 0:NT * NX].rearrange("p (t e) -> p t e", e=NX)
            link(v.tensor_tensor(CMP, starts[:, 0:NX].unsqueeze(1).broadcast_to([1, NT, NX]), ti, ALU.is_le))
            link(v.tensor_reduce(TF[:, 0], CMP, AX.X, ALU.add))
            link(v.tensor_tensor(CMP, CMP, tiles[:, 0:NX].unsqueeze(1).broadcast_to([1, NT, NX]), ALU.mult))
            link(v.tensor_reduce(TF[:, 1], CMP, AX.X, ALU.add))
            link(v.tensor_tensor(TF[:, 2], tilei[:], TF[:, 1], ALU.subtract))
            link(v.tensor_scalar(TF[:, 2], TF[:, 2], float(P), None, ALU.mult))
            link(v.tensor_scalar(TF[:, 3], TF[:, 0], float(REG), None, ALU.mult))
            link(v.tensor_tensor(TF[:, 2], TF[:, 2], TF[:, 3], ALU.add))
            link(v.tensor_scalar(TF[:, 0], TF[:, 0], float(NX - 1), None, ALU.min))
            v.tensor_copy(TROW[:], TF[:, 2])
            v.tensor_copy(TEXP[:], TF[:, 0])
            v.tensor_copy(TTAIL[:], BT[0:1, 0]).then_inc(v_tab, 1)
            v.wait_ge(v_tab, 1)
            v.sem_inc(v_first, 1)
            v.wait_ge(d_e, 16)

            def take(j):
                e = v.value_load(TEXP[0:1, j_at(j)], min_val=0, max_val=NX - 1)
                wait(v, p_2, j.at(1, 1 - UN))
                v.tensor_copy(WS[j.c % UN][:], WE[:, e]).then_inc(v_ws, 1)
                v.wait_ge(p_t, j.at(1, 1))
                wait(v, p_1, j.at(1, -3))
                v.tensor_copy(XTT[j.c % 4][:], t_slot(j)).then_inc(v_xt, 1)

            def give(j):
                v.wait_ge(p_2, j.at(1, 1))
                wait(v, d_ys[j.c % UN], j.prior(UN, 16))
                v.tensor_tensor(YT[j.c % UN][:], o_slot(j), WS[j.c % UN][:, F + FH:F + FH + P], ALU.add).then_inc(v_y, 1)

            def tile(j, left):
                if not left or left > 3:
                    take(j.next(3))
                give(j)

            def first_two():
                for c in range(3):
                    take(Tile(0, c, UN))

            every(v, first_two, tile, NT, UN)

            def combine(q, left):
                b, c = q.pair()
                k = q.c % QD
                v.wait_ge(p_s2, q.at(1, 1))
                v.wait_ge(d_q[k], q.uses(QD, 16 * 2))
                v.wait_ge(d_qy[k], q.uses(QD, 16 * TOPK))
                wait(v, d_o2[q.c % 2], q.prior(2, 16))
                T = QB // P
                base = n2[0] if isinstance(q.i, int) and q.c < 4 else None
                def lnk(x):
                    x.then_inc(v_cq, 1)
                    n2[0] += 1
                    v.wait_ge(v_cq, q.at(TOPK, (n2[0] - 1) % TOPK + 1))
                lnk(v.tensor_tensor(OQ[q.c % 2][:], PA[:], AQ[k][:], ALU.add))
                for r in range(TOPK):
                    for t in range(T):
                        x = v.scalar_tensor_tensor(OQ[q.c % 2][:, t], YQ[k][:, r, t], GK[:, b, r, c * T + t:c * T + t + 1], OQ[q.c % 2][:, t], ALU.mult, ALU.add)
                    if r < TOPK - 1:
                        lnk(x)
                x.then_inc(v_q, 1)

            n2 = [0]
            every(v, lambda: None, combine, NQ, QD)

        @block.tensor
        def _(t):
            t.wait_ge(d_c, NCONST)
            t.wait_ge(v_k, 3)

            release = {"xnt": (a_xt, 1, 1), "xi0": (v_conv, 2, 1), "xi1": (v_conv, 2, 2), "z0": (a_z, 2, 1), "z1": (a_z, 2, 2),
                       "x2t": (a_x2t, 1, 1), "lg": (v_lg, 1, 1), "rk": (v_pos, 1, 1), "ua": (a_ut, 2, 1), "ub": (a_ut, 2, 2), "lv": (a_e, 1, 1), "y0": (v_gate, 2, 1), "y1": (v_gate, 2, 2), "out": (v_x1, 1, 1)}
            last_use = {}

            def slot(name, b):
                k = SLOT[name]
                if k in last_use:
                    prev, of = last_use[k]
                    sem_, per, which = release[prev]
                    t.wait_ge(sem_, of.at(per, which))
                last_use[k] = (name, b)
                return WD[k]

            def p1(n):
                ps = slot("xnt", n)
                t.wait_ge(v_ln, n.at(1, 1))
                for c in range(C):
                    x = t.transpose(ps[:, c * P:(c + 1) * P], XN[:, c], ident[:])
                x.then_inc(p_xnt, 1)
                t.wait_ge(a_xt, n.at(1, 1))

            def inner(n, which):
                for m in which:
                    ps = slot(("xi0", "xi1", "z0", "z1")[m], n)
                    for k in range(2):
                        x = t.matmul(ps[:, k * 512:(k + 1) * 512], w_in[:, m * P:(m + 1) * P], XT[:, k * 512:(k + 1) * 512], start=True, stop=True)
                    x.then_inc(p_xi if m < 2 else p_z, 1)

            def p2(n, b):
                t.wait_ge(a_u, n.at(2, 2))
                if b is not None:
                    t.wait_ge(a_hb, b.at(1, 1))
                for c in range(C):
                    for h in range(EH):
                        x = t.matmul(SM[:, c * 3 * N:(c + 1) * 3 * N], U[n.par][:, h, c * P:(c + 1) * P], w_bcd[:, h], start=(h == 0), stop=(h == EH - 1))
                x.then_inc(p_bcd, 1)
                for k in range(2):
                    ps = slot(("ua", "ub")[k], n)
                    for c in range(4):
                        for h in range(EH):
                            o = (c * EH + h) * P
                            x = t.transpose(ps[:, o:o + P], U[n.par][:, h, (4 * k + c) * P:(4 * k + c + 1) * P], ident[:])
                    x.then_inc(p_ut, 1)

            def p3(n):
                t.wait_ge(v_g, n.at(1, 1))
                g2 = GG[:].rearrange("p c n -> p (c n)")
                ps = slot("lv", n)
                for k in range(2):
                    x = t.matmul(ps[:, k * 512:(k + 1) * 512], g2, tlv[:, k * 512:(k + 1) * 512], start=True, stop=True)
                x.then_inc(p_lv, 1)
                t.matmul(SM[:, 0:P], tend[:], g2, start=True, stop=True)
                t.matmul(SM[:, P:2 * P], onesm[:], g2, start=True, stop=True)
                t.transpose(SM[:, 2 * P:3 * P], DB[:].rearrange("p c n -> p (c n)"), ident[:])
                t.transpose(SM[:, 3 * P:4 * P], CT[:].rearrange("p c n -> p (c n)"), ident[:]).then_inc(p_dec, 1)

            def states(b):
                t.wait_ge(v_w, b.at(1, 1))
                t.wait_ge(v_x, b.at(1, 1))
                t.wait_ge(a_ut, b.at(2, 2))
                for c in range(C - 1):
                    x = t.matmul(SM[:, 0:E], W[:, c * P:(c + 1) * P], UT[b.par][:, c], start=(c == 0), stop=(c == C - 2))
                x.then_inc(p_hb, 1)

            def levels(b, k):
                if k == 0:
                    t.wait_ge(d_r, b.at(32 * NCMB, 32 * NCMB))
                wait(t, v_m, b.at(2, k))

                def pair(out_, c, l, s0, sn, t0, tn):
                    return t.matmul(out_, XK[:, c, l * P + s0:l * P + s0 + sn], XQ[:, c, l * HALF + t0:l * HALF + t0 + tn], start=True, stop=True)
                for cc in range(CG):
                    c = k * CG + cc
                    for l in (6, 5, 4):
                        w = 1 << l
                        for blk in range(P // (2 * w)):
                            s = blk * 2 * w
                            x = pair(PA[s:s + w, cc, s + w:s + 2 * w], c, l, s, w, blk * w, w)
                x.then_inc(p_a, 1)
                for q in range(2):
                    for l in (3 - 2 * q, 2 - 2 * q):
                        for cc in range(CG):
                            x = pair(PM[q][:, (3 - l) % 2, cc], k * CG + cc, l, 0, P, 0, HALF)
                    x.then_inc(p_m, 1)

            def ys(b, k):
                ps = slot(f"y{k}", b)
                t.wait_ge(v_m, b.at(2, k + 1))
                t.wait_ge(a_hb, b.at(1, 1))
                t.wait_ge(g_qm, b.at(1, 1))
                for cc in range(CG):
                    c = k * CG + cc
                    for h in range(EH):
                        o = ps[:, h * 512 + cc * P:h * 512 + (cc + 1) * P]
                        t.matmul(o, UT[b.par][:, c, h * P:(h + 1) * P], MT[k][:, cc], start=True, stop=False)
                        x = t.matmul(o, HB[:, h * P:(h + 1) * P], QM[b.par][:, c], start=False, stop=True)
                x.then_inc(p_y, 1)

            def x2t(m):
                XW = XWB[m.par]
                t.wait_ge(v_xw, m.at(1, 1))
                ps = slot("x2t", m)
                for c in range(C):
                    x = t.transpose(ps[:, c * P:(c + 1) * P], XW[:, 0, c, 0:P], ident[:])
                x.then_inc(p_x2t, 1)

            def logits(m):
                t.wait_ge(a_x2t, m.at(1, 1))
                ps = slot("lg", m)
                for c in range(C):
                    x = t.matmul(ps[:, c * NE:(c + 1) * NE], X2T[:, c * P:(c + 1) * P], gw[:], start=True, stop=True)
                x.then_inc(p_lg, 1)

            def ranks(m):
                t.wait_ge(v_mk, m.at(1, 1))
                ps = slot("rk", m)
                mk = MKS[:].rearrange("p c e -> p (c e)")
                t.matmul(ps[:, 0:P], tri[:], mk, start=True, stop=True)
                t.matmul(ps[:, P:2 * P], onesm[:], mk, start=True, stop=True).then_inc(p_rk, 1)

            def outp(b):
                GT = U[b.par]
                ps = slot("out", b)
                t.wait_ge(v_gated, b.at(2, 2))
                for c in range(C):
                    for h in range(EH):
                        x = t.matmul(ps[:, c * P:(c + 1) * P], GT[:, h, c * P:(c + 1) * P], w_out[:, h], start=(h == 0), stop=(h == EH - 1))
                x.then_inc(p_out, 1)

            def step(b):
                front, back, route = has(b)
                n, m = b.next(), b.next(-1)
                if not isinstance(b.i, int) or b.c == NB - 2:
                    last_use.update({0: ("rk", m.next(-1)), 1: ("y1", m)})
                if front:
                    p1(n)
                if route:
                    outp(m)
                if front:
                    inner(n, (0, 1))
                if back:
                    states(b)
                    levels(b, 0)
                if front:
                    inner(n, (2, 3))
                    p2(n, b)
                if route:
                    x2t(m)
                if back:
                    ys(b, 0)
                if route:
                    logits(m)
                if back:
                    levels(b, 1)
                if front:
                    p3(n)
                if route:
                    ranks(m)
                if back:
                    ys(b, 1)

            def prologue(b):
                p1(b); inner(b, (0, 1, 2, 3)); p2(b, None); p3(b)

            steps(t, prologue, step)
            t.wait_ge(p_rk, NB)
            t.sem_inc(p_first, 1)
            t.wait_ge(v_tab, 1)

            def turn(j):
                t.wait_ge(d_xs[j.c % UN], j.uses(UN, 16))
                wait(t, v_xt, j.at(1, -1))
                t.transpose(t_slot(j), XS[j.c % UN][:, 0:P], ident[:]).then_inc(p_t, 1)

            def up(j):
                t.wait_ge(v_xt, j.at(1, 1))
                t.wait_ge(v_ws, j.at(1, 1))
                wait(t, a_g, j.at(1, -3))
                for h in range(FH):
                    x = t.matmul(h_slot(j, h), WS[j.c % UN][:, h * P:(h + 1) * P], XTT[j.c % 4][:], start=True, stop=True)
                x.then_inc(p_1, 1)

            def down(j):
                t.wait_ge(a_g, j.at(1, 1))
                wait(t, v_y, j.at(1, -1))
                for h in range(FH):
                    x = t.matmul(o_slot(j), HT[j.c % 4][:, h], WS[j.c % UN][:, F + FH + P + h * P:F + FH + P + (h + 1) * P], start=(h == 0), stop=(h == FH - 1))
                x.then_inc(p_2, 1)

            def tile(j, left):
                if not left or left > 3:
                    turn(j.next(3))
                if not left or left > 2:
                    up(j.next(2))
                down(j)

            def first_two():
                for c in range(3):
                    turn(Tile(0, c, UN))
                for c in range(2):
                    up(Tile(0, c, UN))

            t.wait_ge(v_pos, NB)
            every(t, first_two, tile, NT, UN)

            def s_up(q):
                t.wait_ge(d_q[q.c % QD], q.uses(QD, 16 * 2))
                for f in range(FS // P):
                    wait(t, a_s, q.at(4, f + 1 - 4))
                    t.matmul(WD[f // 2][:, (f % 2) * QB:(f % 2 + 1) * QB], SW1[:, f * P:(f + 1) * P], XQB[q.c % QD][:], start=True, stop=True).then_inc(p_s1, 1)

            def s_down(q):
                t.wait_ge(a_s, q.at(4, 4))
                wait(t, v_q, q.at(1, 0))
                for c in range(QB // P):
                    for f in range(FS // P):
                        x = t.matmul(PA[:, c], HS[q.c % 2][:, f, c * P:(c + 1) * P], SW2[:, f], start=(f == 0), stop=(f == FS // P - 1))
                x.then_inc(p_s2, 1)

            def block(q, left):
                if left != 1:
                    s_up(q.next())
                s_down(q)
            t.wait_ge(v_y, NT)
            t.wait_ge(d_sw, 16 * 3)
            every(t, lambda: s_up(Tile(0, 0, QD)), block, NQ, QD)


def kernel(**inputs):
    import numpy as np
    import concourse.bacc as _bacc
    from concourse import mybir as _mybir
    from concourse.bass_utils import run_bass_kernel_spmd as _run

    def two(a):
        return np.ascontiguousarray(a.reshape(2, 128, -1).transpose(1, 0, 2))

    g = {k.replace("L0_attn_", "").replace("L0_ffn_", "f_"): np.asarray(v) for k, v in inputs.items()}
    idx = np.arange(128)
    f32 = np.float32
    tl = np.zeros((128, 8, 128), f32)
    mk = np.zeros((128, 4, 4, 64), f32)
    for l in range(7):
        mid = (idx >> (l + 1) << (l + 1)) + (1 << l)
        right = (idx >> l) & 1 == 1
        i, t = idx[:, None], idx[None, :]
        tl[:, l] = np.where(right[None, :], (i >= mid[None, :]) & (i <= t), (i > t) & (i < mid[None, :]))
        if l < 4:
            tr = idx[right]
            mk[:, 3 - l] = ((~right)[:, None] & ((idx >> (l + 1))[:, None] == (tr >> (l + 1))[None, :])).astype(f32)[:, None, :]
    tl[:, 7] = idx[:, None] <= idx[None, :]
    w_bcd = np.concatenate([g["W_dt"], g["W_x"]], 0).T
    arr = {
        "x": g["x"], "ident": np.eye(128, dtype=f32), "onesm": np.ones((128, 128), f32), "tlv": tl.reshape(128, 1024),
        "tend": (idx[:, None] > idx[None, :]).astype(f32), "msk": mk,
        "rowmask": (idx[:, None] // 16 == np.arange(8)[None, :]).astype(f32),
        "w_in": g["W_in"].T, "conv_w": two(g["conv_w"].reshape(256, 4)), "conv_b": two(g["conv_b"])[:, :, 0],
        "w_bcd": two(w_bcd), "bdt": np.broadcast_to(g["b_dt"], (128, 16)), "alog": np.broadcast_to(g["A_log"], (128, 16)),
        "gw": np.concatenate([g["f_gW"], np.zeros((128, 1), f32)], 1),
        "gb": np.broadcast_to(np.concatenate([g["f_gb"], np.full(1, -1e30, f32)]), (128, NE)),
        "sb2": np.broadcast_to(g["f_sb2"], (128, 128)), "iota": np.broadcast_to(np.arange(NE, dtype=f32), (128, NE)),
        "idc": (np.arange(TOPK)[None, :, None] * TOK + np.arange(C)[None, None, :] * P + idx[:, None, None]).astype(f32),
        "ereg": np.broadcast_to(np.arange(NE, dtype=f32) * REG, (128, NE)), "tri": (idx[:, None] < idx[None, :]).astype(f32),
        "tilei": np.arange(NT, dtype=f32)[None],
        "we": np.concatenate([g["f_rW1"].transpose(1, 0, 2), g["f_rb1"].reshape(NX, FH, P).transpose(2, 0, 1),
                              np.broadcast_to(g["f_rb2"], (128, NX, P)),
                              g["f_rW2"].reshape(NX, FH, P, P).transpose(2, 0, 1, 3).reshape(P, NX, FH * P)], 2),
        "sw1": g["f_sW1"][0], "sb1": g["f_sb1"].reshape(FS // P, P).T, "sw2": g["f_sW2"].reshape(FS // P, P, P).transpose(1, 0, 2),
        "dcol": two(g["D"])[:, :, 0], "w_out": two(g["W_out"].T),
    }
    nc = _bacc.Bacc("TRN2", target_bir_lowering=False, num_devices=1)
    arrays, d = {}, {}
    for k, a in arr.items():
        a = np.ascontiguousarray(a)
        arrays[f"in_{k}_dram"] = a
        d[k] = nc.dram_tensor(f"in_{k}_dram", a.shape, _mybir.dt.from_np(a.dtype), kind="ExternalInput").ap()
    out = nc.dram_tensor("out_0_dram", (8, 1024, 128), _mybir.dt.float32, kind="ExternalOutput").ap()
    build(nc, d, out)
    r = _run(nc, [arrays], core_ids=[0])
    return r.results[0]["out_0_dram"]
```

```python
from contextlib import ExitStack
import concourse.bass as bass
from concourse import mybir

FP32 = mybir.dt.float32
BF16 = mybir.dt.bfloat16
U32 = mybir.dt.uint32
I32 = mybir.dt.int32
ALU = mybir.AluOpType
ACT = mybir.ActivationFunctionType
AX = mybir.AxisListType

P = 128
NB = 8
L = 1024
C = L // P
N = 16
E = 256
EH = E // P
LV = 7
CG = 4
G = C // CG
HALF = P // 2
EPS = 1e-5
K_PARTS = [0, 0, 1, 1, 0, 2]
Q_PARTS = [0, 1, 0, 1, 2, 0]
NCMB = len(K_PARTS)
KR = NCMB * N


NX = 15
NE = 16
TOPK = 3
F = 256
FH = F // P
NWE = F + FH + P + FH * P
FS = 512
TOK = NB * L
REG = TOK + P
XW_ = P + 1
UN = 8
NT = -(-(TOK * TOPK // P + NX) // UN) * UN
SPARE = NT - TOK * TOPK // P
SKIP = 30000.0
QD = 4
QB = 512
NQ = TOK // QB
NQE = 6


class Tile:

    def __init__(self, i, c, un):
        self.i, self.c, self.un = i, c, un

    def at(self, per, k):
        return self.i * (self.un * per) + (self.c * per + k)

    def uses(self, bufs, per):
        return self.i * (self.un // bufs * per) + (self.c // bufs + 1) * per

    def next(self, d=1):
        return Tile(self.i, self.c + d, self.un)

    def prior(self, bufs, per):
        return self.i * (self.un // bufs * per) + self.c // bufs * per

    def index(self):
        return self.i * self.un + self.c

    def pair(self):
        return self.i * (self.un // 2) + self.c // 2, self.c % 2


def j_at(j):
    at = j.index()
    return slice(at, at + 1) if isinstance(at, int) else bass.ds(at, 1)


def every(eng, prologue, step, count, un):
    prologue()
    for c in range(un):
        step(Tile(0, c, un), 0)
    with eng.Fori(0, (count - 2 * un) // un) as i:
        for c in range(un, 2 * un):
            step(Tile(i, c, un), 0)
    for c in range(count - un, count):
        step(Tile(0, c, un), count - c)


class Batch:

    def __init__(self, i, c):
        self.i, self.c = i, c

    def at(self, per, k):
        return self.i * (2 * per) + (self.c * per + k)

    def uses(self, per):
        return self.i * per + (self.c // 2 + 1) * per

    @property
    def par(self):
        return self.c % 2

    def next(self, d=1):
        return Batch(self.i, self.c + d)

    def index(self):
        return self.i * 2 + self.c


def wait(eng, sem, value):
    if isinstance(value, int) and value <= 0:
        return
    eng.wait_ge(sem, value)


def build(nc, d, out):
    ctx, first, second = ExitStack(), ExitStack(), ExitStack()
    with ctx:
        stack = [ctx]

        def sb(name, shape, dt=FP32):
            return stack[0].enter_context(nc.sbuf_tensor(name, shape, dt))

        def pb(name, shape, dt=FP32):
            return ctx.enter_context(nc.psum_tensor(name, shape, dt))

        def sem(name):
            return ctx.enter_context(nc.semaphore(name))

        ident = sb("ident", [P, P]); GK = sb("GK", [P, NB, TOPK, C])
        TROW = sb("TROW", [1, NT], I32); TEXP = sb("TEXP", [1, NT], I32); TTAIL = sb("TTAIL", [1, NE], I32)
        gt = sb("gt", [1, 16]); zt = sb("zt", [P, XW_]); gtp = sb("gtp", [1, 10]); mh1 = sb("mh1", [1, 1])
        stack[0] = first
        XL = [sb(f"XL{k}", [P, C, P]) for k in range(2)]
        XN = sb("XN", [P, C, P]); XT = sb("XT", [P, L]); CA = sb("CA", [P, EH, L])
        U = [sb("U0", [P, EH, L])]; ZS = [sb("ZS0", [P, EH, L])]
        UT = [sb(f"UT{k}", [P, C, E]) for k in range(2)]
        QM = [sb(f"QM{k}", [P, C, P]) for k in range(2)]
        DG = [sb(f"DG{k}", [P, CG, P]) for k in range(G)]
        MT = [sb(f"MT{k}", [P, CG, P]) for k in range(G)]
        XQ = sb("XQ", [KR, C, LV * HALF], BF16); W = sb("W", [P, C * C * N])
        onesm = sb("onesm", [P, P]); tlv = sb("tlv", [P, (LV + 1) * P]); tend = sb("tend", [P, P])
        msk = sb("msk", [P, 4, CG, HALF]); rowmask = sb("rowmask", [P, C])
        w_in = sb("w_in", [P, 2 * E]); conv_w = sb("conv_w", [P, EH, 4]); conv_b = sb("conv_b", [P, EH])
        w_bcd = sb("w_bcd", [P, EH, 3 * N]); bdt = sb("bdt", [P, N]); alog = sb("alog", [P, N]); aneg = sb("aneg", [P, N])
        dcol = sb("dcol", [P, EH]); w_out = sb("w_out", [P, EH, P]); mhalf = sb("mhalf", [P, C])
        aneg2 = sb("aneg2", [P, N])
        gw = sb("gw", [P, NE]); gb = sb("gb", [P, NE]); sb2 = sb("sb2", [P, P]); iota = sb("iota", [P, NE])
        idc = sb("idc", [P, TOPK, C]); ereg = sb("ereg", [P, NE]); tri = sb("tri", [P, P]); tilei = sb("tilei", [1, NT])
        XR = [sb(f"XR{k}", [P, C, P]) for k in range(2)]
        ST = sb("ST", [P, C, 6]); MV = sb("MV", [P, C, 2]); VE = sb("VE", [P, C]); RS = sb("RS", [P, C])
        U.append(sb("U1", [P, EH, L])); ZS.append(sb("ZS1", [P, EH, L]))
        D0 = sb("D0", [P, C, N]); AB = sb("AB", [P, C, N]); LN1 = sb("LN1", [P, C, N]); DEL = sb("DEL", [P, C, N])
        GG = sb("GG", [P, C, N]); DB = sb("DB", [P, C, N]); CT = sb("CT", [P, C, N]); TM = sb("TM", [P, C, N]); M0 = sb("M0", [P, C])
        KE = sb("KE", [P, 2, C, N]); EX = sb("EX", [P, LV + 1, P])
        X = sb("X", [P, LV, P]); R = sb("R", [P, LV, P]); PT = sb("PT", [P, 3, LV * P], BF16); PTQ = sb("PTQ", [P, 3, LV * HALF], BF16)
        QF = sb("QF", [P, P])
        XK = sb("XK", [KR, C, LV * P], BF16)
        HB = sb("HB", [P, E]); X1 = sb("X1", [P, C, P])
        XWB = [sb(f"XW{k}", [P, TOPK, C, XW_]) for k in range(2)]; ACC = sb("ACC", [P, C, P]); X2T = sb("X2T", [P, L]); IDR = sb("IDR", [P, TOPK, C])
        LG = sb("LG", [P, C, NE]); MX = sb("MX", [P, C, 8]); IX = sb("IX", [P, C, 8], U32); IXF = sb("IXF", [P, TOPK, C])
        DT = sb("DT", [P, C, NE + TOPK]); SE = sb("SE", [P, C]); RC = sb("RC", [P, C])
        OH = sb("OH", [P, TOPK, C, NE]); MKS = sb("MKS", [P, C, NE]); BT = sb("BT", [P, C + 1, NE]); PM_ = sb("PM_", [P, C, NE])
        PF = sb("PF", [P, TOPK, C]); PU = sb("PU", [P, TOPK, C], U32)
        CN = sb("CN", [1, 6, NE]); CI = sb("CI", [1, NE], I32)
        TF = R[0:1].rearrange("p l f -> p (l f)")[:, 0:4 * NT].rearrange("p (k n) -> p k n", k=4)
        stack[0] = second
        first.close()
        WE = sb("WE", [P, NX, NWE])
        SW1 = sb("SW1", [P, FS]); SB1 = sb("SB1", [P, FS // P]); SW2 = sb("SW2", [P, FS // P, P])
        XQB = [sb(f"XQB{k}", [P, QB]) for k in range(QD)]; HS = [sb(f"HS{k}", [P, FS // P, QB]) for k in range(2)]
        YSH = sb("YSH", [P, NQ, QB // P, P])
        XS = [sb(f"XS{k}", [P, XW_]) for k in range(UN)]; ID = [sb(f"ID{k}", [P, 1], U32) for k in range(UN)]
        WS = [sb(f"WS{k}", [P, NWE]) for k in range(UN)]; XTT = [sb(f"XTT{k}", [P, P]) for k in range(4)]
        HT = [sb(f"HT{k}", [P, FH, P]) for k in range(4)]; YT = [sb(f"YT{k}", [P, P]) for k in range(UN)]
        AQ = [sb(f"AQ{k}", [P, QB // P, P]) for k in range(QD)]
        YQ = [sb(f"YQ{k}", [P, TOPK, QB // P, P]) for k in range(QD)]
        OQ = [sb(f"OQ{k}", [P, QB // P, P]) for k in range(2)]
        second.close()
        stack[0] = ctx
        WD = [pb(f"WD{k}", [P, 1024]) for k in range(2)]
        SM = pb("SM", [P, 512]); PA = pb("PA", [P, CG, P]); PM = [pb(f"PM{k}", [P, 2, CG, HALF]) for k in range(2)]
        dk = nc.dram_tensor("dk", [3, C, N, LV * P], BF16)
        dq = nc.dram_tensor("dq", [3, C, N, LV * HALF], BF16)

        dx2t = nc.dram_tensor("dx2t", [P, NB, L], FP32)
        dacc = nc.dram_tensor("dacc", [NB, C, P, P], FP32)
        dslot = nc.dram_tensor("dslot", [NX * REG + SPARE * P, XW_], FP32)
        dy = nc.dram_tensor("dy", [TOPK * TOK, P], FP32)

        d_st, d_sc, d_z, d_tail = sem("d_stored"), sem("d_dispatched"), sem("d_spare"), sem("d_tails")
        p_x2t, p_lg, p_rk = sem("pe_x2t"), sem("pe_logits"), sem("pe_ranks")
        a_xc, a_x2t, a_ex = sem("act_xcopies"), sem("act_x2t"), sem("act_gates")
        v_ve2, v_xw, v_ids, v_lg, v_mk, v_pos, v_tab, v_zt = [sem("dve_" + x) for x in "var2 xw ids logits masks slots tables zt".split()]
        d_ac = sem("d_acc")
        v_cq, g_s = sem("dve_combine_chain"), sem("pool_step_over")
        v_first, p_first, a_first = sem("dve_first_part"), sem("pe_first_part"), sem("act_first_part")
        d_e, d_sw, a_id = sem("d_expert_weights"), sem("d_shared_weights"), sem("act_tile_ids"); d_xs = [sem(f"d_rows{k}") for k in range(UN)]; d_ys = [sem(f"d_result{k}") for k in range(UN)]
        p_t, p_1, p_2 = sem("pe_rows"), sem("pe_hidden"), sem("pe_result")
        a_tt, v_ws, v_y = sem("act_tile_rows"), sem("dve_tile_weights"), sem("dve_tile_result")
        a_g = sem("act_gelu")
        d_q = [sem(f"d_block{k}") for k in range(QD)]; d_qy = [sem(f"d_block_results{k}") for k in range(QD)]; a_ysh, g_sum = sem("act_shared_results"), sem("pool_block_sums"); d_aq = [sem(f"d_block_sums{k}") for k in range(QD)]; d_o2 = [sem(f"d_out{k}") for k in range(2)]
        p_s1, p_s2, a_s, v_q = sem("pe_shared_hidden"), sem("pe_shared"), sem("act_shared"), sem("dve_combined")
        g_c2 = sem("pool_acc_first")
        g_rs2, g_acc, v_gated = sem("pool_rstd2"), sem("pool_acc"), sem("dve_gated")
        d_c, d_w, d_r = sem("d_const"), sem("d_parts_written"), sem("d_parts_read")
        d_x = [sem(f"d_x{k}") for k in range(2)]; d_xr = [sem(f"d_xr{k}") for k in range(2)]
        (p_xnt, p_xi, p_z, p_bcd, p_ut, p_dec, p_lv, p_hb, p_a, p_m, p_y, p_out) = [
            sem("pe_" + s) for s in "xnt xi z bcd ut dec lv hb a m y out".split()]
        (a_k, a_xt, a_c0, a_z, a_u, a_hb, a_ut, a_sp, a_ln, a_ke, a_e, a_h, a_m) = [
            sem("act_" + s) for s in "const xt c0 z u hb ut sp ln ke e hi mid".split()]
        (v_k, v_ln, v_ve, v_conv, v_ab, v_g, v_m0, v_w, v_x, v_r, v_l, v_m, v_gate, v_x1, v_c) = [
            sem("dve_" + s) for s in "const ln var conv ab g m0 w x rest lo merge gate x1 chain".split()]
        g_rs, g_dg, g_qm, g_c = [sem("pool_" + s) for s in "rstd diag qm masks".split()]
        xv = d["x"].rearrange("b (t p) e -> b p t e", p=P)
        ov = out.rearrange("b (t p) e -> b p t e", p=P)

        def t_slot(j):
            o = j.c % 2 * 512
            return WD[0][:, o:o + P]

        def h_slot(j, h):
            k = j.c % 4
            bank = WD[1][:, k * 512:(k + 1) * 512] if k < 2 else SM[:] if k == 2 else PA[:].rearrange("p c t -> p (c t)")
            return bank[:, h * P:(h + 1) * P]

        def s_slot(f):
            return (WD[1][:, 0:512], WD[1][:, 512:], WD[0][:, 512:], PM[1][:].rearrange("p a c t -> p (a c t)"))[f]

        def o_slot(j):
            return PM[j.c % 2][:].rearrange("p a c t -> p (a c t)")[:, 0:P]

        block = ctx.enter_context(nc.Block())

        def steps(eng, prologue, step):
            prologue(Batch(0, 0))
            for b in (0, 1):
                step(Batch(0, b))
            with eng.Fori(0, (NB - 4) // 2) as i:
                step(Batch(i, 2))
                step(Batch(i, 3))
            for b in (NB - 2, NB - 1, NB):
                step(Batch(0, b))

        def has(b):
            if not isinstance(b.i, int):
                return True, True, True
            return b.c < NB - 1, b.c < NB, b.c > 0

        SLOT = {"xnt": 0, "out": 1, "xi0": 0, "xi1": 1, "z0": 0, "z1": 1, "ua": 0, "ub": 1, "x2t": 0, "lv": 1, "y0": 1, "lg": 0,
                "y1": 1}
        consts = [(ident, "ident"), (onesm, "onesm"), (tlv, "tlv"), (tend, "tend"), (msk, "msk"), (rowmask, "rowmask"),
                  (w_in, "w_in"), (conv_w, "conv_w"), (conv_b, "conv_b"), (w_bcd, "w_bcd"), (bdt, "bdt"), (alog, "alog"),
                  (dcol, "dcol"), (w_out, "w_out"), (gw, "gw"), (gb, "gb"), (sb2, "sb2"), (iota, "iota"), (idc, "idc"),
                  (ereg, "ereg"), (tri, "tri"), (tilei, "tilei")]
        NCONST = 16 * len(consts)

        @block.sync
        def _(sp):
            sp.dma_start(XL[0][:], xv[0]).then_inc(d_x[0], 16)
            for tile, name in consts:
                sp.dma_start(tile[:], d[name]).then_inc(d_c, 16)
            sp.dma_start(XL[1][:], xv[1]).then_inc(d_x[1], 16)

            def parts(n):
                fresh, merged, landed = n.at(1, 1), n.at(4, 0), n.at(32, 32)
                if not isinstance(n.i, int):
                    fresh, merged, landed = sp.snap(fresh), sp.snap(merged), sp.snap(landed)
                wait(sp, p_m, merged)
                sp.wait_ge(v_l, fresh)
                sp.dma_start(dk.ap().rearrange("q c n f -> (c n) q f"), PT[:]).then_inc(d_w, 16)
                sp.dma_start(dq.ap().rearrange("q c n f -> (c n) q f"), PTQ[:]).then_inc(d_w, 16)
                sp.wait_ge(d_w, landed)
                for k in range(NCMB):
                    sp.dma_start(XK[k * N:(k + 1) * N], dk[K_PARTS[k]].rearrange("c n f -> n c f")).then_inc(d_r, 16)
                    sp.dma_start(XQ[k * N:(k + 1) * N], dq[Q_PARTS[k]].rearrange("c n f -> n c f")).then_inc(d_r, 16)

            def number(b):
                return b.index() if isinstance(b.i, int) else sp.snap(b.index())

            def load(b):
                at = number(b.next(2))
                sp.wait_ge(v_ln, b.at(1, 1))
                sp.dma_start(XL[b.par][:], xv[at]).then_inc(d_x[b.par], 16)

            def residual(b):
                at = number(b)
                wait(sp, v_x1, b.at(1, -1))
                sp.dma_start(XR[b.par][:], xv[at]).then_inc(d_xr[b.par], 16)

            def store(m):
                at = number(m)
                sp.wait_ge(a_x2t, m.at(1, 1))
                sp.dma_start(dx2t[:, at, :], X2T[:]).then_inc(d_st, 16)

            def store_acc(b):
                at = number(b)
                sp.wait_ge(g_acc, b.at(1, 1))
                sp.dma_start(dacc[at].rearrange("c p e -> p c e"), ACC[:]).then_inc(d_ac, 16)

            def expert_weights():
                sp.wait_ge(v_ln, NB)
                sp.wait_ge(p_xnt, NB)
                sp.wait_ge(p_z, 2 * NB)
                sp.wait_ge(a_u, 2 * NB)
                sp.wait_ge(v_gated, 2 * (NB - 1))
                sp.wait_ge(p_out, NB - 1)
                sp.dma_start(WE[:], d["we"]).then_inc(d_e, 16)

            def shared_in(q):
                b, c = q.pair()
                wait(sp, p_s1, q.at(FS // P, FS // P * (1 - QD)))
                sp.dma_start(XQB[q.c % QD][:], dx2t[:, b, c * QB:(c + 1) * QB]).then_inc(d_q[q.c % QD], 16)

            def shared_start():
                sp.wait_ge(p_y, 2 * NB)
                for tile, name in ((SW1, "sw1"), (SB1, "sb1"), (SW2, "sw2")):
                    sp.dma_start(tile[:], d[name]).then_inc(d_sw, 16)
                sp.wait_ge(d_st, 16 * -(-NQE // 2))
                for c in range(QD):
                    shared_in(Tile(0, c, QD))

            def step(b):
                front, back, route = has(b)
                if front and route and not (isinstance(b.i, int) and b.c > NB - 3):
                    load(b)
                if back:
                    residual(b)
                if isinstance(b.i, int) and b.c == NB - 1:
                    expert_weights()
                if isinstance(b.i, int) and b.c == NB:
                    shared_start()
                if route:
                    store_acc(b.next(-1))
                    store(b.next(-1))
                if front:
                    parts(b.next())

            def prologue(b):
                sp.wait_ge(v_zt, 1)
                for k in range(SPARE):
                    sp.dma_start(dslot[NX * REG + k * P:NX * REG + (k + 1) * P], zt[:]).then_inc(d_z, 16)
                parts(b)
                load(b)

            steps(sp, prologue, step)

            for c in range(QD, NQE):
                shared_in(Tile(0, c, QD))
            sp.wait_ge(v_tab, 1)
            for e in range(NX):
                at = sp.value_load(TTAIL[0:1, e:e + 1], min_val=0, max_val=NX * REG - P)
                sp.dma_start(dslot[bass.ds(at, P)], zt[:]).then_inc(d_tail, 16)
            sp.wait_ge(v_tab, 2)
            sp.wait_ge(v_first, 1)
            sp.wait_ge(p_first, 1)
            sp.wait_ge(a_first, 1)
            sp.wait_ge(d_sc, 16 * TOPK * C * NB)
            sp.wait_ge(d_ac, 16 * NB)
            sp.wait_ge(d_st, 16 * NB)
            sp.wait_ge(d_tail, 16 * NX)
            sp.wait_ge(d_z, 16 * SPARE)

            def rows(j):
                at = sp.value_load(TROW[0:1, j_at(j)], min_val=0, max_val=NX * REG + SPARE * P - P)
                wait(sp, a_id, j.at(1, 1 - UN))
                sp.dma_start(XS[j.c % UN][:], dslot[bass.ds(at, P)]).then_inc(d_xs[j.c % UN], 16)

            every(sp, lambda: None, lambda j, left: rows(j), NT, UN)

            def sums_in(q):
                b, c = q.pair()
                wait(sp, g_sum, q.at(1, 1 - QD))
                sp.dma_start(AQ[q.c % QD][:], dacc[b, c * 4:c * 4 + 4].rearrange("c p e -> p c e")).then_inc(d_aq[q.c % QD], 16)

            def results_in(q):
                b, c = q.pair()
                k = q.c % QD
                ts = slice(c * 4, c * 4 + 4)
                wait(sp, v_q, q.at(1, 1 - QD))
                for r in range(TOPK):
                    src = dy.ap().rearrange("(k b c p) e -> k b p c e", k=TOPK, b=NB, p=P)[r, b, :, ts]
                    sp.dma_start(YQ[k][:, r], src).then_inc(d_qy[k], 16)

            def block_out(q):
                b, c = q.pair()
                sp.wait_ge(v_q, q.at(1, 1))
                sp.dma_start(ov[b, :, c * 4:c * 4 + 4], OQ[q.c % 2][:]).then_inc(d_o2[q.c % 2], 16)

            for c in range(NQE, NQE + QD):
                shared_in(Tile(0, c, QD))
            for c in range(QD):
                sums_in(Tile(0, c, QD))
            for k in range(UN):
                sp.wait_ge(d_ys[k], 16 * (NT // UN))
            for c in range(QD - 1):
                results_in(Tile(0, c, QD))
            for c in range(NQ):
                if c + QD - 1 < NQ:
                    results_in(Tile(0, c + QD - 1, QD))
                if c + QD < NQ:
                    sums_in(Tile(0, c + QD, QD))
                block_out(Tile(0, c, QD))
                if NQE + QD + c < NQ:
                    shared_in(Tile(0, NQE + QD + c, QD))
            for k in range(2):
                sp.wait_ge(d_o2[k], 16 * (NQ // 2))
        @block.gpsimd
        def _(g):
            g.memset(mhalf[:], -0.5).then_inc(g_c, 1)
            g.memset(mh1[:], 0.0).then_inc(g_c, 1)
            g.wait_ge(g_c, 2)

            def rstd(n):
                g.wait_ge(v_ve, n.at(1, 1))
                g.tensor_tensor(RS[:], VE[:], mhalf[:], ALU.pow).then_inc(g_rs, 1)

            def rstd2(b):
                g.wait_ge(v_ve2, b.at(1, 1))
                g.tensor_tensor(RS[:], VE[:], mhalf[:], ALU.pow).then_inc(g_rs2, 1)

            def diag(n):
                g.wait_ge(v_m0, n.at(1, 1))
                wait(g, v_m, n.at(2, 0))
                for k in range(G):
                    g.tensor_tensor(DG[k][:], ident[:].unsqueeze(1).broadcast_to([P, CG, P]),
                                    M0[:, k * CG:(k + 1) * CG].unsqueeze(2).broadcast_to([P, CG, P]), ALU.mult).then_inc(g_dg, 1)

            def qmask(n):
                g.wait_ge(v_x, n.at(1, 1))
                wait(g, p_y, n.at(2, -2))
                g.tensor_tensor(QM[n.par][:], QF[:].unsqueeze(1).broadcast_to([P, C, P]),
                                rowmask[:].unsqueeze(2).broadcast_to([P, C, P]), ALU.mult).then_inc(g_qm, 1)

            def acc(b):
                XW = XWB[b.par]
                g.wait_ge(v_xw, b.at(1, 1))
                wait(g, d_ac, b.at(16, 0))
                g.tensor_tensor(ACC[:], X1[:], XW[:, 0, :, 0:P], ALU.add).then_inc(g_c2, 1)
                g.wait_ge(g_c2, b.at(1, 1))
                g.tensor_tensor(ACC[:], ACC[:], sb2[:].unsqueeze(1).broadcast_to([P, C, P]), ALU.add).then_inc(g_acc, 1)

            def dispatch(m, choices):
                XW = XWB[m.par]
                if choices[0] == 0:
                    g.wait_ge(v_pos, m.at(1, 1))
                    g.wait_ge(a_xc, m.at(2, 2))
                    g.wait_ge(v_ids, m.at(1, 1))
                    g.tensor_tensor(gtp[:, m.par:m.par + 1], mh1[:], mh1[:], ALU.add)
                for k in choices:
                    for t in range(C):
                        g.indirect_dma_start(dslot.ap(), bass.IndirectOffsetOnAxis(ap=PU[:, k, t:t + 1], axis=0), XW[:, k, t, :], None).then_inc(d_sc, 16)

            def prologue(b):
                rstd(b)
                g.wait_ge(d_c, NCONST)
                rstd(b.next()); diag(b); qmask(b)

            def step(b):
                front, back, route = has(b)
                late = route and (not isinstance(b.i, int) or b.c > 1)
                if not back:
                    dispatch(b.next(-2), (0,))
                    rstd2(b.next(-1))
                    dispatch(b.next(-2), (1,))
                    acc(b.next(-1))
                    dispatch(b.next(-2), (2,))
                    dispatch(b.next(-1), (0, 1, 2))
                    return
                if route:
                    rstd2(b.next(-1))
                if late:
                    dispatch(b.next(-2), (0,))
                if front and not (isinstance(b.i, int) and b.c >= NB - 2):
                    rstd(b.next(2))
                if route:
                    acc(b.next(-1))
                if late:
                    dispatch(b.next(-2), (1, 2))
                if front:
                    diag(b.next())
                    qmask(b.next())

            steps(g, prologue, step)

            def result(j, left):
                g.wait_ge(v_y, j.at(1, 1))
                g.wait_ge(a_id, j.at(1, 1))
                wait(g, g_s, j.at(1, 0))
                g.tensor_tensor(gtp[:, 2:3], mh1[:], mh1[:], ALU.add).then_inc(g_s, 1)
                g.indirect_dma_start(dy.ap(), bass.IndirectOffsetOnAxis(ap=ID[j.c % UN][:, 0:1], axis=0), YT[j.c % UN][:], None,
                                     bounds_check=TOPK * TOK - 1, oob_is_err=False).then_inc(d_ys[j.c % UN], 16)

            every(g, lambda: None, result, NT, UN)

            def add_up(q, left):
                g.wait_ge(a_ysh, q.at(1, 1))
                g.wait_ge(d_aq[q.c % QD], q.uses(QD, 16))
                g.tensor_tensor(YSH[:, q.index()], YSH[:, q.index()], AQ[q.c % QD][:], ALU.add).then_inc(g_sum, 1)

            every(g, lambda: None, add_up, NQ, QD)
            for k in range(UN):
                g.wait_ge(d_ys[k], 16 * (NT // UN))

        @block.scalar
        def _(a):
            a.wait_ge(d_c, NCONST)
            a.activation(aneg[:], alog[:], ACT.Exp).then_inc(a_k, 1)

            def front(n):
                a.wait_ge(p_xnt, n.at(1, 1))
                wait(a, p_z, n.at(2, 0))
                a.activation(XT[:], WD[SLOT["xnt"]][:], ACT.Copy).then_inc(a_xt, 1)

            def taps(n):
                for h in range(EH):
                    a.wait_ge(p_xi, n.at(2, h + 1))
                    wait(a, a_u, n.at(2, 0))
                    a.activation(CA[:, h], WD[SLOT[f"xi{h}"]][:], ACT.Identity, scale=conv_w[:, h, 3:4], bias=conv_b[:, h:h + 1]).then_inc(a_c0, 1)

            def hb(b):
                a.wait_ge(p_hb, b.at(1, 1))
                wait(a, p_y, b.at(2, 0))
                a.activation(HB[:], SM[:, 0:E], ACT.Copy).then_inc(a_hb, 1)

            def silus(n):
                for h in range(EH):
                    a.wait_ge(v_conv, n.at(2, h + 1))
                    wait(a, p_out, n.at(1, -1))
                    a.activation(U[n.par][:, h], CA[:, h], ACT.Silu).then_inc(a_u, 1)
                for h in range(EH):
                    a.wait_ge(p_z, n.at(2, h + 1))
                    wait(a, v_gated, n.at(2, -2))
                    a.activation(ZS[n.par][:, h], WD[SLOT[f"z{h}"]][:], ACT.Silu).then_inc(a_z, 1)

            def ut(n):
                for h in range(2):
                    a.wait_ge(p_ut, n.at(2, h + 1))
                    wait(a, p_y, n.at(2, -2))
                    a.activation(UT[n.par][:, 4 * h:4 * h + 4, :], WD[SLOT[("ua", "ub")[h]]][:].rearrange("p (t e) -> p t e", e=E), ACT.Copy).then_inc(a_ut, 1)

            def soft(n):
                a.wait_ge(v_ab, n.at(1, 1))
                a.activation(AB[:], AB[:], ACT.Exp, scale=-1.0).then_inc(a_sp, 1)
                a.wait_ge(a_sp, n.at(1, 1))
                wait(a, v_g, n.at(1, 0))
                a.activation(LN1[:], AB[:], ACT.Ln, bias=1.0).then_inc(a_ln, 1)

            def expo(n):
                a.wait_ge(p_dec, n.at(1, 1))
                wait(a, v_w, n.at(1, 0))
                a.activation(KE[:], SM[:, 0:2 * C * N].rearrange("p (a c n) -> p a c n", a=2, n=N), ACT.Exp).then_inc(a_ke, 1)
                a.wait_ge(p_lv, n.at(1, 1))
                wait(a, v_x, n.at(1, 0))
                a.activation(EX[:], WD[SLOT["lv"]][:].rearrange("p (l t) -> p l t", t=P), ACT.Exp).then_inc(a_e, 1)

            def split(n):
                a.wait_ge(v_x, n.at(1, 1))
                wait(a, d_w, n.at(32, 0))
                a.activation(PT[:, 0], X[:].rearrange("p l t -> p (l t)"), ACT.Copy).then_inc(a_h, 1)

            def middle(n):
                a.wait_ge(v_r, n.at(1, 1))
                a.activation(PT[:, 1], R[:].rearrange("p l t -> p (l t)"), ACT.Copy).then_inc(a_m, 1)

            def copies(b):
                XW = XWB[b.par]
                a.wait_ge(v_xw, b.at(1, 1))
                for k in (1, 2):
                    a.activation(XW[:, k, :, 0:P], XW[:, 0, :, 0:P], ACT.Copy).then_inc(a_xc, 1)

            def x2t(m):
                a.wait_ge(p_x2t, m.at(1, 1))
                wait(a, p_lg, m.at(1, 0))
                wait(a, d_st, m.at(16, 0))
                a.activation(X2T[:], WD[SLOT["x2t"]][:], ACT.Copy).then_inc(a_x2t, 1)

            def gates(m):
                a.wait_ge(v_lg, m.at(1, 1))
                a.activation(DT[:], DT[:], ACT.Exp).then_inc(a_ex, 1)

            def prologue(b):
                front(b); taps(b); silus(b); soft(b); ut(b); expo(b); split(b); middle(b)

            def shared(q):
                for f in range(FS // P):
                    a.wait_ge(p_s1, q.at(4, f + 1))
                    if f == 0:
                        wait(a, p_s2, q.at(1, -1))
                    a.activation(HS[q.c % 2][:, f], s_slot(f), ACT.Gelu, bias=SB1[:, f:f + 1]).then_inc(a_s, 1)

            def kept(q, left):
                if left != 1:
                    shared(q.next())
                a.wait_ge(p_s2, q.at(1, 1))
                a.activation(YSH[:, q.c], PA[:], ACT.Copy).then_inc(a_ysh, 1)

            def step(b):
                front_, back, route = has(b)
                n, m = b.next(), b.next(-1)
                if not back:
                    a.wait_ge(d_sw, 16 * 3)
                    shared(Tile(0, 0, QD))
                    kept(Tile(0, 0, QD), 1)
                if front_:
                    front(n)
                if front_:
                    taps(n)
                if back:
                    hb(b)
                if front_:
                    silus(n)
                if front_:
                    soft(n)
                    ut(n)
                if route:
                    x2t(m)
                if front_:
                    expo(n); split(n); middle(n)
                if route:
                    copies(m)
                    gates(m)

            steps(a, prologue, step)
            a.wait_ge(a_xc, 2 * NB)
            a.wait_ge(a_ex, NB)
            a.sem_inc(a_first, 1)

            shared(Tile(0, 1, QD))
            for c in range(1, NQE):
                kept(Tile(0, c, QD), NQE - c)

            def turned(j):
                a.wait_ge(p_t, j.at(1, 1))
                wait(a, p_1, j.at(1, -3))
                a.activation(XTT[j.c % 4][:], t_slot(j), ACT.Copy).then_inc(a_tt, 1)

            def hidden(j, left):
                a.wait_ge(p_1, j.at(1, 1))
                wait(a, p_2, j.at(1, -3))
                for h in range(FH):
                    x = a.activation(HT[j.c % 4][:, h], h_slot(j, h), ACT.Gelu, bias=WS[j.c % UN][:, F + h:F + h + 1])
                x.then_inc(a_g, 1)
                a.wait_ge(d_xs[j.c % UN], j.uses(UN, 16))
                wait(a, d_ys[j.c % UN], j.prior(UN, 16))
                a.activation(ID[j.c % UN][:], XS[j.c % UN][:, P:], ACT.Copy).then_inc(a_id, 1)
                if not left or left > 3:
                    turned(j.next(3))

            def first_tiles():
                for c in range(3):
                    turned(Tile(0, c, UN))

            every(a, first_tiles, hidden, NT, UN)

            shared(Tile(0, NQE, QD))
            for c in range(NQE, NQ):
                kept(Tile(0, c, QD), NQ - c)

        @block.vector
        def _(v):
            chain = {"done": 0, "loop": None, "base": 0, "k": 0}
            gates_ = [0]

            def link(ins, b=None):
                ins.then_inc(v_c, 1)
                chain["k"] += 1
                v.wait_ge(v_c, chain["done"] + chain["k"] if chain["loop"] is None else chain["loop"].at(NCH, chain["base"] + chain["k"]))

            def step_over():
                v.memset(gt[:, gates_[0] % 16:gates_[0] % 16 + 1], 0.0)
                gates_[0] += 1

            def ln(n):
                v.wait_ge(d_x[n.par], n.uses(16))
                for t in range(C):
                    x = v.bn_stats(ST[:, t], XL[n.par][:, t])
                link(x)
                step_over()
                for t in range(C):
                    x = v.bn_aggr(MV[:, t], ST[:, t])
                link(x)
                wait(v, g_rs, n.at(1, 0))
                v.tensor_scalar(VE[:], MV[:, :, 1], EPS, None, ALU.add).then_inc(v_ve, 1)

            def ln_apply(n):
                v.wait_ge(g_rs, n.at(1, 1))
                wait(v, p_xnt, n.at(1, 0))
                for t in range(C):
                    x = v.tensor_scalar(XN[:, t], XL[n.par][:, t], MV[:, t, 0:1], RS[:, t:t + 1], ALU.subtract, ALU.mult)
                x.then_inc(v_ln, 1)

            def conv(n, h):
                ps = WD[SLOT[f"xi{h}"]]
                v.wait_ge(a_c0, n.at(2, h + 1))
                for k in (2, 1, 0):
                    j = 3 - k
                    x = v.scalar_tensor_tensor(CA[:, h, j:], ps[:, 0:L - j], conv_w[:, h, k:k + 1], CA[:, h, j:], ALU.mult, ALU.add)
                    if k:
                        link(x)
                x.then_inc(v_conv, 1)

            def merge(b, k):
                v.wait_ge(p_a, b.at(2, k + 1))
                v.wait_ge(g_dg, b.at(2, k + 1))
                wait(v, p_y, b.at(2, k - 1))
                link(v.tensor_tensor(MT[k][:], PA[:], DG[k][:], ALU.add))
                for l in (3, 2, 1, 0):
                    q = (3 - l) // 2
                    if l % 2:
                        v.wait_ge(p_m, b.at(4, 2 * k + q + 1))
                    step_over()
                    w = 1 << l
                    o = MT[k][:].rearrange("p c (k a j) -> p (c k) a j", a=2, j=w)[:, :, 1, :]
                    mk = msk[:, 3 - l].bitcast(mybir.dt.int32).rearrange("p c (k j) -> p (c k) j", j=w)
                    dt = PM[q][:, (3 - l) % 2].rearrange("p c (k j) -> p (c k) j", j=w)
                    x = v.copy_predicated(o, mk, dt)
                    if l:
                        link(x)
                x.then_inc(v_m, 1)

            def tok_a(n):
                sm = SM[:, 0:C * 3 * N].rearrange("p (c k n) -> p c k n", k=3, n=N)
                v.wait_ge(p_bcd, n.at(1, 1))
                link(v.tensor_tensor(D0[:], sm[:, :, 0], bdt[:].unsqueeze(1).broadcast_to([P, C, N]), ALU.add))
                wait(v, a_ln, n.at(1, 0))
                v.scalar_tensor_tensor(AB[:], D0[:], -1.0, D0[:], ALU.mult, ALU.max).then_inc(v_ab, 1)

            def tok_b(n):
                sm = SM[:, 0:C * 3 * N].rearrange("p (c k n) -> p c k n", k=3, n=N)
                v.wait_ge(a_ln, n.at(1, 1))
                link(v.scalar_tensor_tensor(DEL[:], D0[:], 0.0, LN1[:], ALU.max, ALU.add))
                wait(v, p_lv, n.at(1, 0))
                v.tensor_tensor(GG[:], DEL[:], aneg2[:].unsqueeze(1).broadcast_to([P, C, N]), ALU.mult)
                v.tensor_tensor(DB[:], DEL[:], sm[:, :, 1], ALU.mult)
                v.tensor_copy(CT[:], sm[:, :, 2]).then_inc(v_g, 1)
                v.wait_ge(v_g, n.at(1, 1))
                link(v.tensor_tensor(TM[:], DB[:], CT[:], ALU.mult))
                wait(v, g_dg, n.at(2, 0))
                v.tensor_reduce(M0[:], TM[:], AX.X, ALU.add).then_inc(v_m0, 1)

            def gate(b, k, s):
                v.wait_ge(p_y, b.at(2, k + 1))
                sl = slice(k * 512, k * 512 + 512)
                for h in range(EH):
                    x = v.scalar_tensor_tensor(U[b.par][:, h, sl], U[b.par][:, h, sl], dcol[:, h:h + 1], WD[s][:, h * 512:(h + 1) * 512], ALU.mult, ALU.add)
                x.then_inc(v_gate, 1)

            def gate_z(b, k):
                sl = slice(k * 512, k * 512 + 512)
                v.wait_ge(v_gate, b.at(2, k + 1))
                v.tensor_tensor(U[b.par][:, :, sl], U[b.par][:, :, sl], ZS[b.par][:, :, sl], ALU.mult).then_inc(v_gated, 1)

            def facs(n):
                v.wait_ge(a_ke, n.at(1, 1))
                wait(v, p_hb, n.at(1, 0))
                wd = W[:, N:N + (C - 1) * (C + 1) * N].rearrange("p (c k) -> p c k", k=(C + 1) * N)[:, :, 0:N]
                link(v.tensor_tensor(wd, KE[:, 0, 0:C - 1], DB[:, 0:C - 1], ALU.mult))
                w4 = W[:].rearrange("p (a c n) -> p a c n", a=C, n=N)
                for c in range(1, C - 1):
                    x = v.tensor_tensor(w4[:, 0:c, c + 1], w4[:, 0:c, c], KE[:, 1, c].unsqueeze(1).broadcast_to([P, c, N]), ALU.mult)
                    if c < C - 2:
                        link(x)
                x.then_inc(v_w, 1)
                v.wait_ge(a_e, n.at(1, 1))
                wait(v, a_h, n.at(1, 0))
                dbt, ct = SM[:, 2 * P:3 * P], SM[:, 3 * P:4 * P]
                for l in range(LV):
                    f = lambda t: t.rearrange("p (k a j) -> p k a j", a=2, j=1 << l)
                    ex, xo = f(EX[:, l]), f(X[:, l])
                    v.tensor_tensor(xo[:, :, 0], ex[:, :, 0], f(dbt)[:, :, 0], ALU.mult)
                    v.tensor_tensor(xo[:, :, 1], ex[:, :, 1], f(ct)[:, :, 1], ALU.mult)
                wait(v, g_qm, n.at(1, 0))
                v.tensor_tensor(QF[:], EX[:, LV], ct, ALU.mult).then_inc(v_x, 1)

            def split_middle(n):
                v.wait_ge(a_h, n.at(1, 1))
                v.tensor_tensor(R[:].rearrange("p l t -> p (l t)"), X[:].rearrange("p l t -> p (l t)"), PT[:, 0], ALU.subtract).then_inc(v_r, 1)

            def split_low(n):
                v.wait_ge(a_m, n.at(1, 1))
                link(v.tensor_tensor(PT[:, 2], R[:].rearrange("p l t -> p (l t)"), PT[:, 1], ALU.subtract))
                for l in range(LV):
                    src = PT[:, :, l * P:(l + 1) * P].rearrange("p q (k a j) -> p q k a j", a=2, j=1 << l)[:, :, :, 1]
                    x = v.tensor_copy(PTQ[:, :, l * HALF:(l + 1) * HALF].rearrange("p q (k j) -> p q k j", j=1 << l), src)
                x.then_inc(v_l, 1)

            def x1(b, s):
                v.wait_ge(p_out, b.at(1, 1))
                v.wait_ge(d_xr[b.par], b.uses(16))
                wait(v, g_acc, b.at(1, 0))
                v.tensor_tensor(X1[:], WD[s][:].rearrange("p (t e) -> p t e", e=P), XR[b.par][:], ALU.add).then_inc(v_x1, 1)

            def ln2(b):
                v.wait_ge(v_x1, b.at(1, 1))
                step_over()
                for t in range(C):
                    x = v.bn_stats(ST[:, t], X1[:, t])
                link(x)
                step_over()
                for t in range(C):
                    x = v.bn_aggr(MV[:, t], ST[:, t])
                link(x)
                v.tensor_scalar(VE[:], MV[:, :, 1], EPS, None, ALU.add).then_inc(v_ve2, 1)

            def ln2_apply(b):
                XW = XWB[b.par]
                v.wait_ge(g_rs2, b.at(1, 1))
                wait(v, d_sc, b.at(16 * TOPK * C, -16 * TOPK * C))
                for t in range(C):
                    x = v.tensor_scalar(XW[:, 0, t, 0:P], X1[:, t], MV[:, t, 0:1], RS[:, t:t + 1], ALU.subtract, ALU.mult)
                x.then_inc(v_xw, 1)
                v.tensor_copy(XW[:, :, :, P], IDR[:]).then_inc(v_ids, 1)
                v.wait_ge(v_ids, b.at(1, 1))
                link(v.tensor_scalar(IDR[:], IDR[:], float(L), None, ALU.add))

            def top(m):
                v.wait_ge(p_lg, m.at(1, 1))
                wait(v, v_pos, m.at(1, 0))
                link(v.tensor_tensor(LG[:], WD[SLOT["lg"]][:, 0:C * NE].rearrange("p (c e) -> p c e", e=NE),
                                     gb[:].unsqueeze(1).broadcast_to([P, C, NE]), ALU.add))
                step_over()
                for t in range(C):
                    x = v.max(MX[:, t], LG[:, t])
                link(x)
                step_over()
                for t in range(C):
                    x = v.max_index(IX[:, t], MX[:, t], LG[:, t])
                link(x)
                mx0 = MX[:, :, 0:1]
                v.tensor_tensor(DT[:, :, 0:NE], LG[:], mx0.broadcast_to([P, C, NE]), ALU.subtract)
                v.tensor_tensor(DT[:, :, NE:], MX[:, :, 0:TOPK], mx0.broadcast_to([P, C, TOPK]), ALU.subtract).then_inc(v_lg, 1)
                link(v.tensor_copy(IXF[:], IX[:, :, 0:TOPK].rearrange("p c k -> p k c")))
                link(v.tensor_tensor(OH[:].rearrange("p k c e -> p (k c) e"), iota[:].unsqueeze(1).broadcast_to([P, TOPK * C, NE]),
                                     IXF[:].rearrange("p k c -> p (k c)").unsqueeze(2).broadcast_to([P, TOPK * C, NE]), ALU.is_equal))
                link(v.tensor_tensor(MKS[:], OH[:, 0], OH[:, 1], ALU.add))
                v.tensor_tensor(MKS[:], MKS[:], OH[:, 2], ALU.add).then_inc(v_mk, 1)
                v.wait_ge(a_ex, m.at(1, 1))
                link(v.tensor_reduce(SE[:], DT[:, :, 0:NE], AX.X, ALU.add))
                link(v.reciprocal(RC[:], SE[:]))
                v.tensor_tensor(GK[:, m.index()], DT[:, :, NE:].rearrange("p c k -> p k c"),
                                RC[:].unsqueeze(1).broadcast_to([P, TOPK, C]), ALU.mult)

            def slots(m):
                v.wait_ge(p_rk, m.at(1, 1))
                rk = PM[0][:].rearrange("p a c t -> p (a c t)")[:, 0:2 * C * NE].rearrange("p (a c e) -> p a c e", a=2, e=NE)
                for t in range(C):
                    link(v.tensor_tensor(BT[:, t + 1], BT[:, t], rk[:, 1, t], ALU.add))
                link(v.tensor_tensor(PM_[:], rk[:, 0], BT[:, 0:C], ALU.add))
                link(v.tensor_tensor(OH[:], OH[:], PM_[:].unsqueeze(1).broadcast_to([P, TOPK, C, NE]), ALU.mult))
                link(v.tensor_reduce(PF[:], OH[:], AX.X, ALU.add))
                wait(v, d_sc, m.at(16 * TOPK * C, 0))
                v.tensor_copy(BT[:, 0], BT[:, C])
                v.tensor_copy(PU[:], PF[:]).then_inc(v_pos, 1)

            v.memset(zt[:], 0.0).then_inc(v_k, 1)
            v.wait_ge(v_k, 1)
            v.memset(zt[:, P:], SKIP).then_inc(v_zt, 1)
            v.memset(W[:], 0.0).then_inc(v_k, 1)
            v.memset(PA[:], 0.0).then_inc(v_k, 1)

            def constants():
                v.wait_ge(a_k, 1)
                v.wait_ge(d_c, NCONST)
                v.tensor_scalar(aneg2[:], aneg[:], -1.0, None, ALU.mult).then_inc(v_k, 1)
                v.tensor_copy(IDR[:], idc[:]).then_inc(v_k, 1)
                v.tensor_copy(BT[:, 0], ereg[:]).then_inc(v_k, 1)
                v.wait_ge(v_k, 6)

            def prologue(z):
                ln(z); constants(); ln_apply(z); conv(z, 0); conv(z, 1); ln(z.next()); tok_a(z); ln_apply(z.next()); tok_b(z); facs(z); split_middle(z); split_low(z)

            NL = {"front": 4 + 1 + 2 + 6 + 1, "back": 8 + 3, "route": 8 + C + 3, "ln": 2}

            def step(b):
                front, back, route = has(b)
                n, m = b.next(), b.next(-1)
                normal = front and not (isinstance(b.i, int) and b.c >= NB - 2)
                if not isinstance(b.i, int):
                    if chain["loop"] is None:
                        chain["base"] = chain["done"] + chain["k"] - NCH * b.c
                    chain["loop"], chain["k"], chain["done"] = b, 0, 0
                elif chain["loop"] is not None:
                    chain["done"], chain["loop"], chain["k"] = chain["base"] + NCH * b.c, None, 0
                if front:
                    conv(n, 0)
                if route:
                    x1(m, SLOT["out"])
                    ln2(m)
                if front:
                    conv(n, 1)
                if route and (not isinstance(b.i, int) or 1 < b.c < NB):
                    slots(m.next(-1))
                if route:
                    ln2_apply(m)
                if front:
                    tok_a(n)
                if normal:
                    ln(n.next())
                if back:
                    merge(b, 0)
                if front:
                    tok_b(n)
                if normal:
                    ln_apply(n.next())
                if front:
                    facs(n)
                if back:
                    gate(b, 0, SLOT["y0"])
                    merge(b, 1)
                if front:
                    split_middle(n)
                if back:
                    gate_z(b, 0)
                if front:
                    split_low(n)
                if route:
                    top(m)
                if isinstance(b.i, int) and b.c >= NB - 1:
                    slots(m)
                if back:
                    gate(b, 1, SLOT["y1"])
                    gate_z(b, 1)
                if not isinstance(b.i, int):
                    assert chain["k"] == NCH, chain["k"]

            NCH = sum(NL.values())
            steps(v, prologue, step)
            v.wait_ge(v_pos, NB)
            cnt, tiles, starts = CN[:, 0], CN[:, 1], CN[:, 2]
            v.tensor_copy(TTAIL[:], BT[0:1, 0]).then_inc(v_tab, 1)
            link(v.tensor_tensor(cnt, BT[0:1, 0], ereg[0:1], ALU.subtract))
            link(v.tensor_scalar(cnt, cnt, float(P - 1), None, ALU.add))
            link(v.tensor_copy(CI[:], cnt))
            link(v.tensor_scalar(CI[:], CI[:], 7, None, ALU.arith_shift_right))
            link(v.tensor_copy(tiles, CI[:]))
            link(v.memset(CN[:, 3], 0.0))
            link(v.tensor_tensor_scan(starts, tiles, CN[:, 3], 0.0, ALU.add, ALU.add))
            ti = tilei[:].unsqueeze(2).broadcast_to([1, NT, NX])
            CMP = XK[0:1].rearrange("p c f -> p (c f)").bitcast(FP32)[:, 0:NT * NX].rearrange("p (t e) -> p t e", e=NX)
            link(v.tensor_tensor(CMP, starts[:, 0:NX].unsqueeze(1).broadcast_to([1, NT, NX]), ti, ALU.is_le))
            link(v.tensor_reduce(TF[:, 0], CMP, AX.X, ALU.add))
            link(v.tensor_tensor(CMP, CMP, tiles[:, 0:NX].unsqueeze(1).broadcast_to([1, NT, NX]), ALU.mult))
            link(v.tensor_reduce(TF[:, 1], CMP, AX.X, ALU.add))
            link(v.tensor_tensor(TF[:, 2], tilei[:], TF[:, 1], ALU.subtract))
            link(v.tensor_scalar(TF[:, 2], TF[:, 2], float(P), None, ALU.mult))
            link(v.tensor_scalar(TF[:, 3], TF[:, 0], float(REG), None, ALU.mult))
            link(v.tensor_tensor(TF[:, 2], TF[:, 2], TF[:, 3], ALU.add))
            link(v.tensor_scalar(TF[:, 0], TF[:, 0], float(NX - 1), None, ALU.min))
            v.tensor_copy(TROW[:], TF[:, 2])
            v.tensor_copy(TEXP[:], TF[:, 0]).then_inc(v_tab, 1)
            v.wait_ge(v_tab, 2)
            v.sem_inc(v_first, 1)
            v.wait_ge(g_acc, NB)
            v.wait_ge(p_first, 1)
            v.wait_ge(a_first, 1)
            v.wait_ge(d_sc, 16 * TOPK * C * NB)
            v.wait_ge(d_ac, 16 * NB)
            v.wait_ge(d_st, 16 * NB)
            v.wait_ge(d_e, 16)

            def take(j):
                e = v.value_load(TEXP[0:1, j_at(j)], min_val=0, max_val=NX - 1)
                wait(v, p_2, j.at(1, 1 - UN))
                v.tensor_copy(WS[j.c % UN][:], WE[:, e]).then_inc(v_ws, 1)

            def give(j):
                v.wait_ge(p_2, j.at(1, 1))
                wait(v, d_ys[j.c % UN], j.prior(UN, 16))
                v.tensor_tensor(YT[j.c % UN][:], o_slot(j), WS[j.c % UN][:, F + FH:F + FH + P], ALU.add).then_inc(v_y, 1)

            def tile(j, left):
                if not left or left > 3:
                    take(j.next(3))
                give(j)

            def first_tiles():
                for c in range(3):
                    take(Tile(0, c, UN))

            every(v, first_tiles, tile, NT, UN)

            def combine(q, left):
                b, c = q.pair()
                k = q.c % QD
                T = QB // P
                YO = OQ[q.c % 2]
                v.wait_ge(g_sum, q.at(1, 1))
                v.wait_ge(d_qy[k], q.uses(QD, 16 * TOPK))
                wait(v, d_o2[q.c % 2], q.prior(2, 16))
                for r in range(TOPK):
                    for t in range(T):
                        so_far = YSH[:, q.index(), t] if r == 0 else YO[:, t]
                        x = v.scalar_tensor_tensor(YO[:, t], YQ[k][:, r, t], GK[:, b, r, c * T + t:c * T + t + 1], so_far, ALU.mult, ALU.add)
                    if r < TOPK - 1:
                        x.then_inc(v_cq, 1)
                        v.wait_ge(v_cq, q.at(TOPK - 1, r + 1))
                x.then_inc(v_q, 1)

            every(v, lambda: None, combine, NQ, QD)

        @block.tensor
        def _(t):
            t.wait_ge(d_c, NCONST)
            t.wait_ge(v_k, 3)

            release = {"xnt": (a_xt, 1, 1), "xi0": (v_conv, 2, 1), "xi1": (v_conv, 2, 2), "z0": (a_z, 2, 1), "z1": (a_z, 2, 2),
                       "x2t": (a_x2t, 1, 1), "lg": (v_lg, 1, 1), "ua": (a_ut, 2, 1), "ub": (a_ut, 2, 2), "lv": (a_e, 1, 1), "y0": (v_gate, 2, 1), "y1": (v_gate, 2, 2), "out": (v_x1, 1, 1)}
            last_use = {}

            def slot(name, b):
                k = SLOT[name]
                if k in last_use:
                    prev, of = last_use[k]
                    sem_, per, which = release[prev]
                    t.wait_ge(sem_, of.at(per, which))
                last_use[k] = (name, b)
                return WD[k]

            def p1(n):
                ps = slot("xnt", n)
                t.wait_ge(v_ln, n.at(1, 1))
                for c in range(C):
                    x = t.transpose(ps[:, c * P:(c + 1) * P], XN[:, c], ident[:])
                x.then_inc(p_xnt, 1)
                t.wait_ge(a_xt, n.at(1, 1))

            def inner(n, which):
                for m in which:
                    ps = slot(("xi0", "xi1", "z0", "z1")[m], n)
                    for k in range(2):
                        x = t.matmul(ps[:, k * 512:(k + 1) * 512], w_in[:, m * P:(m + 1) * P], XT[:, k * 512:(k + 1) * 512], start=True, stop=True)
                    x.then_inc(p_xi if m < 2 else p_z, 1)

            def p2(n, b):
                t.wait_ge(a_u, n.at(2, 2))
                if b is not None:
                    t.wait_ge(a_hb, b.at(1, 1))
                for c in range(C):
                    for h in range(EH):
                        x = t.matmul(SM[:, c * 3 * N:(c + 1) * 3 * N], U[n.par][:, h, c * P:(c + 1) * P], w_bcd[:, h], start=(h == 0), stop=(h == EH - 1))
                x.then_inc(p_bcd, 1)
                for k in range(2):
                    ps = slot(("ua", "ub")[k], n)
                    for c in range(4):
                        for h in range(EH):
                            o = (c * EH + h) * P
                            x = t.transpose(ps[:, o:o + P], U[n.par][:, h, (4 * k + c) * P:(4 * k + c + 1) * P], ident[:])
                    x.then_inc(p_ut, 1)

            def p3(n):
                t.wait_ge(v_g, n.at(1, 1))
                g2 = GG[:].rearrange("p c n -> p (c n)")
                ps = slot("lv", n)
                for k in range(2):
                    x = t.matmul(ps[:, k * 512:(k + 1) * 512], g2, tlv[:, k * 512:(k + 1) * 512], start=True, stop=True)
                x.then_inc(p_lv, 1)
                t.matmul(SM[:, 0:P], tend[:], g2, start=True, stop=True)
                t.matmul(SM[:, P:2 * P], onesm[:], g2, start=True, stop=True)
                t.transpose(SM[:, 2 * P:3 * P], DB[:].rearrange("p c n -> p (c n)"), ident[:])
                t.transpose(SM[:, 3 * P:4 * P], CT[:].rearrange("p c n -> p (c n)"), ident[:]).then_inc(p_dec, 1)

            def states(b):
                t.wait_ge(v_w, b.at(1, 1))
                t.wait_ge(v_x, b.at(1, 1))
                t.wait_ge(a_ut, b.at(2, 2))
                for c in range(C - 1):
                    x = t.matmul(SM[:, 0:E], W[:, c * P:(c + 1) * P], UT[b.par][:, c], start=(c == 0), stop=(c == C - 2))
                x.then_inc(p_hb, 1)

            def levels(b, k):
                if k == 0:
                    t.wait_ge(d_r, b.at(32 * NCMB, 32 * NCMB))
                    wait(t, v_pos, b.at(1, -1))
                wait(t, v_m, b.at(2, k))

                def pair(out_, c, l, s0, sn, t0, tn):
                    return t.matmul(out_, XK[:, c, l * P + s0:l * P + s0 + sn], XQ[:, c, l * HALF + t0:l * HALF + t0 + tn], start=True, stop=True)
                for cc in range(CG):
                    c = k * CG + cc
                    for l in (6, 5, 4):
                        w = 1 << l
                        for blk in range(P // (2 * w)):
                            s = blk * 2 * w
                            x = pair(PA[s:s + w, cc, s + w:s + 2 * w], c, l, s, w, blk * w, w)
                x.then_inc(p_a, 1)
                for q in range(2):
                    for l in (3 - 2 * q, 2 - 2 * q):
                        for cc in range(CG):
                            x = pair(PM[q][:, (3 - l) % 2, cc], k * CG + cc, l, 0, P, 0, HALF)
                    x.then_inc(p_m, 1)

            def ys(b, k):
                ps = slot(f"y{k}", b)
                t.wait_ge(v_m, b.at(2, k + 1))
                t.wait_ge(a_hb, b.at(1, 1))
                t.wait_ge(g_qm, b.at(1, 1))
                for cc in range(CG):
                    c = k * CG + cc
                    for h in range(EH):
                        o = ps[:, h * 512 + cc * P:h * 512 + (cc + 1) * P]
                        t.matmul(o, UT[b.par][:, c, h * P:(h + 1) * P], MT[k][:, cc], start=True, stop=False)
                        x = t.matmul(o, HB[:, h * P:(h + 1) * P], QM[b.par][:, c], start=False, stop=True)
                x.then_inc(p_y, 1)

            def x2t(m):
                XW = XWB[m.par]
                t.wait_ge(v_xw, m.at(1, 1))
                ps = slot("x2t", m)
                for c in range(C):
                    x = t.transpose(ps[:, c * P:(c + 1) * P], XW[:, 0, c, 0:P], ident[:])
                x.then_inc(p_x2t, 1)

            def logits(m):
                t.wait_ge(a_x2t, m.at(1, 1))
                ps = slot("lg", m)
                for c in range(C):
                    x = t.matmul(ps[:, c * NE:(c + 1) * NE], X2T[:, c * P:(c + 1) * P], gw[:], start=True, stop=True)
                x.then_inc(p_lg, 1)

            def ranks(m):
                t.wait_ge(v_mk, m.at(1, 1))
                if not (isinstance(m.i, int) and m.c == NB - 1):
                    t.wait_ge(v_m, m.at(2, 4))
                ps = PM[0][:].rearrange("p a c t -> p (a c t)")
                mk = MKS[:].rearrange("p c e -> p (c e)")
                t.matmul(ps[:, 0:P], tri[:], mk, start=True, stop=True)
                t.matmul(ps[:, P:2 * P], onesm[:], mk, start=True, stop=True).then_inc(p_rk, 1)

            def outp(b):
                ps = slot("out", b)
                t.wait_ge(v_gated, b.at(2, 2))
                for c in range(C):
                    for h in range(EH):
                        x = t.matmul(ps[:, c * P:(c + 1) * P], U[b.par][:, h, c * P:(c + 1) * P], w_out[:, h], start=(h == 0), stop=(h == EH - 1))
                x.then_inc(p_out, 1)

            def s_up(q):
                t.wait_ge(d_q[q.c % QD], q.uses(QD, 16))
                for f in range(FS // P):
                    wait(t, a_s, q.at(4, f + 1 - 4))
                    t.matmul(s_slot(f), SW1[:, f * P:(f + 1) * P], XQB[q.c % QD][:], start=True, stop=True).then_inc(p_s1, 1)

            def s_down(q):
                t.wait_ge(a_s, q.at(4, 4))
                wait(t, a_ysh, q.at(1, 0))
                for c in range(QB // P):
                    for f in range(FS // P):
                        x = t.matmul(PA[:, c], HS[q.c % 2][:, f, c * P:(c + 1) * P], SW2[:, f], start=(f == 0), stop=(f == FS // P - 1))
                x.then_inc(p_s2, 1)

            def block(q, left):
                if left != 1:
                    s_up(q.next())
                s_down(q)

            def step(b):
                front, back, route = has(b)
                n, m = b.next(), b.next(-1)
                if not isinstance(b.i, int) or b.c == NB - 2:
                    last_use.update({0: ("lg", m.next(-1)), 1: ("y1", m)})
                if front:
                    p1(n)
                    inner(n, (0,))
                if route:
                    outp(m)
                if not back:
                    t.wait_ge(d_sw, 16 * 3)
                    t.wait_ge(v_x1, NB)
                    s_up(Tile(0, 0, QD))
                    s_down(Tile(0, 0, QD))
                if front:
                    inner(n, (1,))
                if route and (not isinstance(b.i, int) or 1 < b.c < NB):
                    ranks(m.next(-1))
                if back:
                    states(b)
                if front:
                    inner(n, (2, 3))
                    p2(n, b)
                if back:
                    levels(b, 0)
                if route:
                    x2t(m)
                if front:
                    p3(n)
                if back:
                    ys(b, 0)
                if route:
                    logits(m)
                if back:
                    levels(b, 1)
                if isinstance(b.i, int) and b.c >= NB - 1:
                    ranks(m)
                if back:
                    ys(b, 1)

            def prologue(b):
                p1(b); inner(b, (0, 1, 2, 3)); p2(b, None); p3(b)

            steps(t, prologue, step)

            t.wait_ge(p_rk, NB)
            t.sem_inc(p_first, 1)
            s_up(Tile(0, 1, QD))
            for c in range(1, NQE):
                block(Tile(0, c, QD), NQE - c)
            t.wait_ge(v_tab, 2)
            t.wait_ge(a_s, 4 * NQE)
            t.wait_ge(a_ysh, NQE)

            def turn(j):
                t.wait_ge(d_xs[j.c % UN], j.uses(UN, 16))
                wait(t, a_tt, j.at(1, -1))
                t.transpose(t_slot(j), XS[j.c % UN][:, 0:P], ident[:]).then_inc(p_t, 1)

            def up(j):
                t.wait_ge(a_tt, j.at(1, 1))
                t.wait_ge(v_ws, j.at(1, 1))
                wait(t, a_g, j.at(1, -3))
                for h in range(FH):
                    x = t.matmul(h_slot(j, h), WS[j.c % UN][:, h * P:(h + 1) * P], XTT[j.c % 4][:], start=True, stop=True)
                x.then_inc(p_1, 1)

            def down(j):
                t.wait_ge(a_g, j.at(1, 1))
                wait(t, v_y, j.at(1, -1))
                for h in range(FH):
                    x = t.matmul(o_slot(j), HT[j.c % 4][:, h], WS[j.c % UN][:, F + FH + P + h * P:F + FH + P + (h + 1) * P], start=(h == 0), stop=(h == FH - 1))
                x.then_inc(p_2, 1)

            def tile(j, left):
                if not left or left > 3:
                    turn(j.next(3))
                if not left or left > 2:
                    up(j.next(2))
                down(j)

            def first_tiles():
                for c in range(3):
                    turn(Tile(0, c, UN))
                for c in range(2):
                    up(Tile(0, c, UN))

            t.wait_ge(v_pos, NB)
            every(t, first_tiles, tile, NT, UN)

            t.wait_ge(v_y, NT)
            s_up(Tile(0, NQE, QD))
            for c in range(NQE, NQ):
                block(Tile(0, c, QD), NQ - c)


def kernel(**inputs):
    import numpy as np
    import concourse.bacc as _bacc
    from concourse import mybir as _mybir
    from concourse.bass_utils import run_bass_kernel_spmd as _run

    def two(a):
        return np.ascontiguousarray(a.reshape(2, 128, -1).transpose(1, 0, 2))

    g = {k.replace("L0_attn_", "").replace("L0_ffn_", "f_"): np.asarray(v) for k, v in inputs.items()}
    idx = np.arange(128)
    f32 = np.float32
    tl = np.zeros((128, 8, 128), f32)
    mk = np.zeros((128, 4, 4, 64), f32)
    for l in range(7):
        mid = (idx >> (l + 1) << (l + 1)) + (1 << l)
        right = (idx >> l) & 1 == 1
        i, t = idx[:, None], idx[None, :]
        tl[:, l] = np.where(right[None, :], (i >= mid[None, :]) & (i <= t), (i > t) & (i < mid[None, :]))
        if l < 4:
            tr = idx[right]
            mk[:, 3 - l] = ((~right)[:, None] & ((idx >> (l + 1))[:, None] == (tr >> (l + 1))[None, :])).astype(f32)[:, None, :]
    tl[:, 7] = idx[:, None] <= idx[None, :]
    w_bcd = np.concatenate([g["W_dt"], g["W_x"]], 0).T
    arr = {
        "x": g["x"], "ident": np.eye(128, dtype=f32), "onesm": np.ones((128, 128), f32), "tlv": tl.reshape(128, 1024),
        "tend": (idx[:, None] > idx[None, :]).astype(f32), "msk": mk,
        "rowmask": (idx[:, None] // 16 == np.arange(8)[None, :]).astype(f32),
        "w_in": g["W_in"].T, "conv_w": two(g["conv_w"].reshape(256, 4)), "conv_b": two(g["conv_b"])[:, :, 0],
        "w_bcd": two(w_bcd), "bdt": np.broadcast_to(g["b_dt"], (128, 16)), "alog": np.broadcast_to(g["A_log"], (128, 16)),
        "gw": np.concatenate([g["f_gW"], np.zeros((128, 1), f32)], 1),
        "gb": np.broadcast_to(np.concatenate([g["f_gb"], np.full(1, -1e30, f32)]), (128, NE)),
        "sb2": np.broadcast_to(g["f_sb2"], (128, 128)), "iota": np.broadcast_to(np.arange(NE, dtype=f32), (128, NE)),
        "idc": (np.arange(TOPK)[None, :, None] * TOK + np.arange(C)[None, None, :] * P + idx[:, None, None]).astype(f32),
        "ereg": np.broadcast_to(np.arange(NE, dtype=f32) * REG, (128, NE)), "tri": (idx[:, None] < idx[None, :]).astype(f32),
        "tilei": np.arange(NT, dtype=f32)[None],
        "we": np.concatenate([g["f_rW1"].transpose(1, 0, 2), g["f_rb1"].reshape(NX, FH, P).transpose(2, 0, 1),
                              np.broadcast_to(g["f_rb2"], (128, NX, P)),
                              g["f_rW2"].reshape(NX, FH, P, P).transpose(2, 0, 1, 3).reshape(P, NX, FH * P)], 2),
        "sw1": g["f_sW1"][0], "sb1": g["f_sb1"].reshape(FS // P, P).T, "sw2": g["f_sW2"].reshape(FS // P, P, P).transpose(1, 0, 2),
        "dcol": two(g["D"])[:, :, 0], "w_out": two(g["W_out"].T),
    }
    nc = _bacc.Bacc("TRN2", target_bir_lowering=False, num_devices=1)
    arrays, d = {}, {}
    for k, a in arr.items():
        a = np.ascontiguousarray(a)
        arrays[f"in_{k}_dram"] = a
        d[k] = nc.dram_tensor(f"in_{k}_dram", a.shape, _mybir.dt.from_np(a.dtype), kind="ExternalInput").ap()
    out = nc.dram_tensor("out_0_dram", (8, 1024, 128), _mybir.dt.float32, kind="ExternalOutput").ap()
    build(nc, d, out)
    r = _run(nc, [arrays], core_ids=[0])
    return r.results[0]["out_0_dram"]
```
